# Optimizing a Trainium2 kernel written in Bass

```python
import numpy as np
import jax
import jax.numpy as jnp

def _softmax(x, axis=-1):
    return jax.nn.softmax(x, axis=axis)

def _gelu(x):
    return jax.nn.gelu(x, approximate=True)

def _silu(x):
    return jax.nn.silu(x)

def _sigmoid(x):
    return jax.nn.sigmoid(x)

def _layernorm(x, axis=-1, eps=1e-05):
    m = jnp.mean(x, axis=axis, keepdims=True)
    v = jnp.var(x, axis=axis, keepdims=True)
    return (x - m) / jnp.sqrt(v + eps)

def _scatter_add(tgt, idx, src, axis=0):
    return tgt.at[idx].add(src)

def _segment_sum(src, seg, n):
    return jax.ops.segment_sum(src, seg, n)
kernel_name = 'mk_gnn_resnorm_d4_gnn_r64_409666'

def setup_inputs(seed: int=0):
    np.random.seed(seed)
    _w = jnp.asarray

    def _rec_inputs():
        import jax
        import jax.numpy as jnp
        _gk = jax.random.key(seed)
        x = -0.0003713 + 1 * jax.random.normal(jax.random.fold_in(_gk, 1), (50000, 128), jnp.float32)
        src = jax.random.randint(jax.random.fold_in(_gk, 2), (12500,), 0, 50000, jnp.int32)
        dst = jnp.minimum((50000 * jax.random.uniform(jax.random.fold_in(_gk, 3), (12500,)) ** 2.0).astype(jnp.int32), 49999)
        _o = jnp.argsort(dst, stable=True)
        src = src[_o]
        dst = dst[_o]
        edge_attr_128 = -8.16379e-05 + 0.999858 * jax.random.normal(jax.random.fold_in(_gk, 11), (12500, 128), jnp.float32)
        edge_weight = jax.random.uniform(jax.random.fold_in(_gk, 13), (12500,), jnp.float32, 0.0, 0.999998)
        return (x, src, dst, edge_attr_128, edge_weight)
    x, src, dst, edge_attr_128, edge_weight = _rec_inputs()

    def _L0_gnn_setup():
        import jax, jax.numpy as jnp
        import numpy as np
        EPS = 0.0
        key = jax.random.key(seed)
        kx, ke, kw, k1, k2 = jax.random.split(key, 5)
        N, E, D, H = (100000, 9375, 128, 128)
        x = jax.random.normal(kx, (N, D), dtype=jnp.float32)
        edge_index = jax.random.randint(ke, (2, E), 0, N, dtype=jnp.int64)
        edge_weight = jax.random.uniform(kw, (E,), dtype=jnp.float32)
        W1 = jax.random.normal(k1, (D, H), dtype=jnp.float32) * (1.0 / np.sqrt(D))
        b1 = jnp.zeros((H,), dtype=jnp.float32)
        W2 = jax.random.normal(k2, (H, D), dtype=jnp.float32) * (1.0 / np.sqrt(H))
        b2 = jnp.zeros((D,), dtype=jnp.float32)
        return {'x': x, 'edge_index': edge_index, 'edge_weight': edge_weight, 'W1': W1, 'b1': b1, 'W2': W2, 'b2': b2}
    _L0_gnn_all = _L0_gnn_setup()
    _L0_gnn_in = {k: v for k, v in _L0_gnn_all.items() if k in ('W1', 'b1', 'W2', 'b2')}
    del _L0_gnn_all

    def _L1_gnn_setup():
        import jax, jax.numpy as jnp
        import numpy as np
        LOG2 = 0.6931471824645996

        def ssp(x):
            return jax.nn.softplus(x) - LOG2
        N, M, F = (50000, 12500, 128)
        key = jax.random.key(seed)
        ks = jax.random.split(key, 12)

        def glorot(k, shape):
            lim = np.sqrt(6.0 / (shape[0] + shape[1])).astype(np.float32)
            return jax.random.uniform(k, shape, jnp.float32, -lim, lim)
        return {'node': jax.random.normal(ks[0], (N, F), jnp.float32), 'edge': jax.random.normal(ks[1], (M, F), jnp.float32), 'edge_index': jax.random.randint(ks[2], (2, M), 0, N, jnp.int32), 'Wn': glorot(ks[3], (F, 128)), 'We1': glorot(ks[4], (F, 128)), 'be1': jnp.zeros((128,), jnp.float32), 'We2': glorot(ks[5], (128, 128)), 'be2': jnp.zeros((128,), jnp.float32), 'W2': glorot(ks[6], (128, 128)), 'b2': jnp.zeros((128,), jnp.float32), 'W3': glorot(ks[7], (128, 128)), 'b3': jnp.zeros((128,), jnp.float32)}
    _L1_gnn_all = _L1_gnn_setup()
    _L1_gnn_in = {k: v for k, v in _L1_gnn_all.items() if k in ('Wn', 'We1', 'be1', 'We2', 'be2', 'W2', 'b2', 'W3', 'b3')}
    del _L1_gnn_all

    def _L2_gnn_setup():
        import jax, jax.numpy as jnp
        import numpy as np
        N_NODES = 10000
        N_EDGES = 10000
        IN_CH = 128
        OUT_CH = 128
        key = jax.random.key(seed)
        k1, k2, k3, k4 = jax.random.split(key, 4)
        x = jax.random.normal(k1, (N_NODES, IN_CH), dtype=jnp.float32)
        edge_index = jax.random.randint(k2, (2, N_EDGES), 0, N_NODES, dtype=jnp.int64)
        bound = 1.0 / np.sqrt(2 * IN_CH)
        W = jax.random.uniform(k3, (OUT_CH, 2 * IN_CH), dtype=jnp.float32, minval=-bound, maxval=bound)
        b = jax.random.uniform(k4, (OUT_CH,), dtype=jnp.float32, minval=-bound, maxval=bound)
        return {'x': x, 'W': W, 'b': b, 'edge_index': edge_index}
    _L2_gnn_all = _L2_gnn_setup()
    _L2_gnn_in = {k: v for k, v in _L2_gnn_all.items() if k in ('W', 'b')}
    del _L2_gnn_all

    def _L3_gnn_setup():
        import jax, jax.numpy as jnp
        import numpy as np
        BN_EPS = 1e-05

        def _bn(x, g, b):
            mu = jnp.mean(x, axis=0)
            var = jnp.mean(jnp.square(x - mu), axis=0)
            return g * (x - mu) * jax.lax.rsqrt(var + BN_EPS) + b
        key = jax.random.key(seed)
        ks = jax.random.split(key, 18)
        N, E, Cin, H, L, Cout = (50000, 9375, 128, 128, 3, 128)
        s_in = 1.0 / np.sqrt(Cin)
        s_h = 1.0 / np.sqrt(H)
        s_2h = 1.0 / np.sqrt(2 * H)
        return {'x': jax.random.normal(ks[0], (N, Cin), jnp.float32), 'edge_index': jax.random.randint(ks[1], (2, E), 0, N, jnp.int32), 'edge_attr': jax.random.normal(ks[2], (E, Cin), jnp.float32), 'W_atom': jax.random.normal(ks[3], (Cin, H), jnp.float32) * s_in, 'b_atom': jnp.zeros((H,), jnp.float32), 'W_bond': jax.random.normal(ks[4], (Cin, H), jnp.float32) * s_in, 'b_bond': jnp.zeros((H,), jnp.float32), 'eps': jnp.zeros((L,), jnp.float32), 'W1': jax.random.normal(ks[5], (L, H, 2 * H), jnp.float32) * s_h, 'b1': jnp.zeros((L, 2 * H), jnp.float32), 'g1': jnp.ones((L, 2 * H), jnp.float32), 'be1': jnp.zeros((L, 2 * H), jnp.float32), 'W2': jax.random.normal(ks[6], (L, 2 * H, H), jnp.float32) * s_2h, 'b2': jnp.zeros((L, H), jnp.float32), 'gn': jnp.ones((L, H), jnp.float32), 'bet': jnp.zeros((L, H), jnp.float32), 'W_out': jax.random.normal(ks[7], (H, Cout), jnp.float32) * s_h, 'b_out': jnp.zeros((Cout,), jnp.float32)}
    _L3_gnn_all = _L3_gnn_setup()
    _L3_gnn_in = {k: v for k, v in _L3_gnn_all.items() if k in ('W_atom', 'b_atom', 'W_bond', 'b_bond', 'eps', 'W1', 'b1', 'g1', 'be1', 'W2', 'b2', 'gn', 'bet', 'W_out', 'b_out')}
    del _L3_gnn_all
    return {'x': x, 'src': src, 'dst': dst, 'edge_attr_128': edge_attr_128, 'edge_weight': edge_weight, 'L0_gnn_W1': _L0_gnn_in['W1'], 'L0_gnn_b1': _L0_gnn_in['b1'], 'L0_gnn_W2': _L0_gnn_in['W2'], 'L0_gnn_b2': _L0_gnn_in['b2'], 'L1_gnn_Wn': _L1_gnn_in['Wn'], 'L1_gnn_We1': _L1_gnn_in['We1'], 'L1_gnn_be1': _L1_gnn_in['be1'], 'L1_gnn_We2': _L1_gnn_in['We2'], 'L1_gnn_be2': _L1_gnn_in['be2'], 'L1_gnn_W2': _L1_gnn_in['W2'], 'L1_gnn_b2': _L1_gnn_in['b2'], 'L1_gnn_W3': _L1_gnn_in['W3'], 'L1_gnn_b3': _L1_gnn_in['b3'], 'L2_gnn_W': _L2_gnn_in['W'], 'L2_gnn_b': _L2_gnn_in['b'], 'L3_gnn_W_atom': _L3_gnn_in['W_atom'], 'L3_gnn_b_atom': _L3_gnn_in['b_atom'], 'L3_gnn_W_bond': _L3_gnn_in['W_bond'], 'L3_gnn_b_bond': _L3_gnn_in['b_bond'], 'L3_gnn_eps': _L3_gnn_in['eps'], 'L3_gnn_W1': _L3_gnn_in['W1'], 'L3_gnn_b1': _L3_gnn_in['b1'], 'L3_gnn_g1': _L3_gnn_in['g1'], 'L3_gnn_be1': _L3_gnn_in['be1'], 'L3_gnn_W2': _L3_gnn_in['W2'], 'L3_gnn_b2': _L3_gnn_in['b2'], 'L3_gnn_gn': _L3_gnn_in['gn'], 'L3_gnn_bet': _L3_gnn_in['bet'], 'L3_gnn_W_out': _L3_gnn_in['W_out'], 'L3_gnn_b_out': _L3_gnn_in['b_out']}

def reference(x, src, dst, edge_attr_128, edge_weight, L0_gnn_W1, L0_gnn_b1, L0_gnn_W2, L0_gnn_b2, L1_gnn_Wn, L1_gnn_We1, L1_gnn_be1, L1_gnn_We2, L1_gnn_be2, L1_gnn_W2, L1_gnn_b2, L1_gnn_W3, L1_gnn_b3, L2_gnn_W, L2_gnn_b, L3_gnn_W_atom, L3_gnn_b_atom, L3_gnn_W_bond, L3_gnn_b_bond, L3_gnn_eps, L3_gnn_W1, L3_gnn_b1, L3_gnn_g1, L3_gnn_be1, L3_gnn_W2, L3_gnn_b2, L3_gnn_gn, L3_gnn_bet, L3_gnn_W_out, L3_gnn_b_out):
    import jax
    import jax.numpy as jnp

    def _L0_gnn_ref(x, edge_index, edge_weight, W1, b1, W2, b2):
        import jax, jax.numpy as jnp
        import numpy as np
        EPS = 0.0
        N = x.shape[0]
        src, dst = (edge_index[0], edge_index[1])
        msg = edge_weight[:, None] * x[src]
        agg = jax.ops.segment_sum(msg, dst, num_segments=N)
        out = (1.0 + EPS) * x + agg
        h = jax.nn.relu(out @ W1 + b1)
        return h @ W2 + b2

    def _L1_gnn_ref(node, edge, edge_index, Wn, We1, be1, We2, be2, W2, b2, W3, b3):
        import jax, jax.numpy as jnp
        import numpy as np
        LOG2 = 0.6931471824645996

        def ssp(x):
            return jax.nn.softplus(x) - LOG2
        N = node.shape[0]
        xn = node @ Wn
        f = ssp(edge @ We1 + be1)
        f = f @ We2 + be2
        msg = xn[edge_index[1]] * f
        agg = jax.ops.segment_sum(msg, edge_index[0], num_segments=N)
        h = ssp(agg @ W2 + b2)
        h = h @ W3 + b3
        return node + h

    def _L2_gnn_ref(x, W, b, edge_index):
        import jax, jax.numpy as jnp
        import numpy as np
        N_NODES = 10000
        N_EDGES = 10000
        IN_CH = 128
        OUT_CH = 128
        src, dst = (edge_index[0], edge_index[1])
        x_i = x[dst]
        x_j = x[src]
        feat = jnp.concatenate([x_i, x_j - x_i], axis=-1)
        msg = feat @ W.T + b
        out = jax.ops.segment_max(msg, dst, num_segments=x.shape[0])
        return jnp.where(jnp.isfinite(out), out, 0.0)

    def _L3_gnn_ref(x, edge_index, edge_attr, W_atom, b_atom, W_bond, b_bond, eps, W1, b1, g1, be1, W2, b2, gn, bet, W_out, b_out):
        import jax, jax.numpy as jnp
        import numpy as np
        BN_EPS = 1e-05

        def _bn(x, g, b):
            mu = jnp.mean(x, axis=0)
            var = jnp.mean(jnp.square(x - mu), axis=0)
            return g * (x - mu) * jax.lax.rsqrt(var + BN_EPS) + b
        N = x.shape[0]
        L = eps.shape[0]
        src, dst = (edge_index[0], edge_index[1])
        h = x @ W_atom + b_atom
        ea = edge_attr @ W_bond + b_bond
        for i in range(L):
            msg = jax.nn.relu(h[src] + ea)
            agg = jax.ops.segment_sum(msg, dst, num_segments=N)
            z = (1.0 + eps[i]) * h + agg
            z = z @ W1[i] + b1[i]
            z = jax.nn.relu(_bn(z, g1[i], be1[i]))
            z = z @ W2[i] + b2[i]
            h = jax.nn.relu(_bn(z, gn[i], bet[i]))
        return h @ W_out + b_out
    edge_index = jnp.stack([src, dst])
    x = _layernorm(x + _L0_gnn_ref(x, edge_index, edge_weight, L0_gnn_W1, L0_gnn_b1, L0_gnn_W2, L0_gnn_b2), axis=-1)
    x = _layernorm(x + _L1_gnn_ref(x, edge_attr_128, edge_index, L1_gnn_Wn, L1_gnn_We1, L1_gnn_be1, L1_gnn_We2, L1_gnn_be2, L1_gnn_W2, L1_gnn_b2, L1_gnn_W3, L1_gnn_b3), axis=-1)
    x = _layernorm(x + _L2_gnn_ref(x, L2_gnn_W, L2_gnn_b, edge_index), axis=-1)
    x = _layernorm(x + _L3_gnn_ref(x, edge_index, edge_attr_128, L3_gnn_W_atom, L3_gnn_b_atom, L3_gnn_W_bond, L3_gnn_b_bond, L3_gnn_eps, L3_gnn_W1, L3_gnn_b1, L3_gnn_g1, L3_gnn_be1, L3_gnn_W2, L3_gnn_b2, L3_gnn_gn, L3_gnn_bet, L3_gnn_W_out, L3_gnn_b_out), axis=-1)
    return x

_drawn_inputs = setup_inputs


def setup_inputs(seed=0):
    import zlib

    import numpy as np

    out = dict(_drawn_inputs(seed))
    spreads = {'L0_gnn_b1': (0.0, 0.1),
     'L0_gnn_b2': (0.0, 0.1),
     'L1_gnn_be1': (0.0, 0.8),
     'L1_gnn_be2': (0.0, 0.404),
     'L1_gnn_b2': (0.0, 0.294),
     'L1_gnn_b3': (0.0, 0.1),
     'L3_gnn_b_atom': (0.0, 0.358),
     'L3_gnn_b_bond': (0.0, 0.1),
     'L3_gnn_eps': (0.0, 0.407),
     'L3_gnn_b1': (0.0, 0.8),
     'L3_gnn_g1': (1.0, 0.2),
     'L3_gnn_be1': (0.0, 0.1),
     'L3_gnn_b2': (0.0, 0.8),
     'L3_gnn_gn': (1.0, 0.2),
     'L3_gnn_bet': (0.0, 0.1),
     'L3_gnn_b_out': (0.0, 0.1)}
    factors = {'L2_gnn_b': 4.683}
    for name, (base, spread) in spreads.items():
        noise = np.random.default_rng([zlib.crc32(name.encode()), seed]).standard_normal(out[name].shape)
        drawn = base * np.exp(spread * noise) if base else spread * noise
        out[name] = jnp.asarray(drawn.astype(out[name].dtype))
    for name, factor in factors.items():
        out[name] = (out[name] * factor).astype(out[name].dtype)
    return out
```

```python
import concourse.bass as bass
from concourse import mybir
from contextlib import ExitStack, contextmanager

fp32 = mybir.dt.float32
bf16 = mybir.dt.bfloat16
i32 = mybir.dt.int32
ALU = mybir.AluOpType
ACT = mybir.ActivationFunctionType

P = 128
F = 128
G = 4
W = G * P
N = 50000
E = 12500
PAIRS = -(-E // (2 * W))
CH = 2 * PAIRS
T = CH * G
EP = CH * W
FULL = E // P
REST = E - FULL * P
NS = 4
HI = -(-N // W)
DC = HI
DPAIRS = (DC - 1) // 2
TP = (N - (DC - 1) * W) // G
SLOT0 = DC * W
ZW = SLOT0 + 2 * EP
FAR = 1 << 20
LOG2 = 0.6931471824645996
LN_EPS = 1e-05
BN_EPS = 1e-05
LAYERS = 3
NEG = -3.0e38
MAXF = 3.4028234663852886e38


@contextmanager
def phase(nc, tag, names):
    sems, every = [], []
    for n in names.split():
        got = [nc.alloc_semaphore(f"{tag}_{n.rstrip('*')}{k}") for k in range(NS if n[-1] == "*" else 1)]
        every += got
        sems.append(got if n[-1] == "*" else got[0])
    yield sems
    nc.clear_and_free_semaphores(every)
    nc.all_engine_barrier()


class Steps:

    def __init__(self, eng, sem):
        self.eng, self.sem, self.base, self.n = eng, sem, 0, 0

    def loop(self, count, body):
        first = self.base + self.n
        body(0)
        per = self.base + self.n - first
        with self.eng.Fori(1, count) as j:
            self.base, self.n = first + j * per, 0
            body(j)
        self.base, self.n = first + count * per, 0


def one(st):
    st.n += 1
    return 1


def steps(st):
    return st.base + st.n


def pipeline(st, chunks, slots, *stages):
    most = max(lag for lag, _ in stages)

    def group(k):
        for h in range(slots):
            for lag, fn in stages:
                turn, slot = k + (h - lag) // slots, (h - lag) % slots
                chunk = slots * turn + slot
                if isinstance(k, int) and not 0 <= chunk < chunks:
                    continue
                fn(chunk, turn, slot)
    even, last = -(-most // slots), (chunks - 1) // slots
    for k in range(even):
        group(k)
    begun = st.base + st.n
    group(even)
    per = st.base + st.n - begun
    with st.eng.Fori(even + 1, last) as k:
        st.base, st.n = begun + (k - even) * per, 0
        group(k)
    st.base, st.n = begun + (last - even) * per, 0
    for k in range(last, (chunks - 1 + most) // slots + 1):
        group(k)


def first(j):
    return isinstance(j, int) and j == 0


class Env:
    pass


def constants(nc, env, A):
    ctx = env.ctx

    def sb(name, shape, dt=fp32):
        return ctx.enter_context(nc.sbuf_tensor(name, shape, dt))

    mats = ["L0_gnn_W1", "L0_gnn_W2", "L1_gnn_Wn", "L1_gnn_We1", "L1_gnn_We2", "L1_gnn_W2", "L1_gnn_W3",
            "L3_gnn_W_atom", "L3_gnn_W_bond", "L3_gnn_W_out"]
    wts = sb("wts", [P, len(mats), F])
    env.w = {m: wts[:, k, :] for k, m in enumerate(mats)}
    w1 = sb("l3_w1", [P, LAYERS, 2 * F])
    w1e = sb("l3_w1e", [P, LAYERS, 2 * F])
    w2 = sb("l3_w2", [P, LAYERS, 2, F])
    env.w1, env.w1e, env.w2 = w1, w1e, w2
    l2w = sb("l2_w", [P, 2, F])
    l2t = sb("l2_t", [P, 2, F])
    env.wi, env.wj = l2t[:, 0, :], l2t[:, 1, :]
    vecs = [("L0_gnn_b1", 1), ("L1_gnn_be1", 1), ("L1_gnn_b2", 1), ("L2_gnn_b", 1), ("L3_gnn_b_atom", 1),
            ("L3_gnn_b_bond", 1), ("L3_gnn_b1", 6), ("L3_gnn_g1", 6), ("L3_gnn_be1", 6), ("L3_gnn_b2", 3),
            ("L3_gnn_gn", 3), ("L3_gnn_bet", 3)]
    rows = sum(n for _, n in vecs)
    vrow = sb("vrow", [rows, F])
    vcol = sb("vcol", [P, rows])
    env.col, at = {}, 0
    for name, n in vecs:
        env.col[name] = vcol[:, at:at + n]
        at += n
    bcs = ["L0_gnn_b2", "L1_gnn_be2", "L1_gnn_b3", "L3_gnn_b_out"]
    bc = sb("bias_rows", [P, len(bcs) + 1, F])
    env.bc = {b: bc[:, k, :] for k, b in enumerate(bcs)}
    env.h0 = bc[:, len(bcs), :]
    epsb = sb("epsb", [P, LAYERS])
    env.onep = sb("onep", [P, LAYERS])
    env.ident = sb("ident", [P, P])
    env.earlier = sb("earlier", [P, P])
    env.below = sb("below", [P, P])
    env.iota = sb("iota_free", [P, W])
    env.iotap = sb("iota_part", [P, 1])
    env.ones = sb("ones", [P, W])
    sp2 = sb("sp2", [P, 4])
    spb = sb("spb", [P, F])
    with phase(nc, "const", "loaded made transposed turned h_in h_mm own_v own_p own_a soft") as (
            loaded, made, transposed, turned, h_in, h_mm, own_v, own_p, own_a, soft):
        with nc.psum_tensor("tp", [P, 512], fp32) as tp, nc.Block() as block:
            loads = []
            for m in mats:
                loads.append((env.w[m], A[m]))
            loads.append((w1[:, :, :], A["L3_gnn_W1"].rearrange("l k n -> k l n")))
            for i in range(LAYERS):
                loads.append((w2[:, i, :, :], A["L3_gnn_W2"][i].rearrange("(h k) n -> k h n", h=2)))
            loads.append((l2w[:, :, :], A["L2_gnn_W"].rearrange("f (h k) -> f h k", h=2)))
            at = 0
            for name, n in vecs:
                src = A[name]
                if n == 1:
                    src = src.rearrange("(a f) -> a f", a=1)
                elif n == 6:
                    src = src.rearrange("l (h f) -> (l h) f", h=2)
                loads.append((vrow[at:at + n, :], src))
                at += n
            for b in bcs:
                loads.append((env.bc[b], A[b].rearrange("(a f) -> a f", a=1).broadcast_to([P, F])))
            loads.append((epsb[:, :], A["L3_gnn_eps"].rearrange("(a f) -> a f", a=1).broadcast_to([P, LAYERS])))

            @block.sync
            def _(sp):
                for dst, src in loads:
                    sp.dma_start(dst, src).then_inc(loaded, 16)

            @block.gpsimd
            def _(pool):
                st = Steps(pool, own_p)
                pool.memset(env.ident[:, :], 0.0).then_inc(own_p, one(st))
                pool.memset(env.earlier[:, :], 1.0).then_inc(own_p, one(st))
                pool.memset(env.below[:, :], 1.0).then_inc(own_p, one(st))
                pool.memset(env.ones[:, :], 1.0).then_inc(own_p, one(st))
                pool.wait_ge(own_p, steps(st))
                pool.affine_select(out=env.ident[:, :], in_=env.ident[:, :], compare_op=ALU.not_equal,
                                          fill=1.0, base=0, pattern=[[-1, P]], channel_multiplier=1).then_inc(own_p, one(st))
                pool.affine_select(out=env.earlier[:, :], in_=env.earlier[:, :], compare_op=ALU.is_gt,
                                          fill=0.0, base=0, pattern=[[-1, P]], channel_multiplier=1).then_inc(own_p, one(st))
                pool.affine_select(out=env.below[:, :], in_=env.below[:, :], compare_op=ALU.is_gt,
                                          fill=0.0, base=0, pattern=[[1, P]], channel_multiplier=-1).then_inc(own_p, one(st))
                pool.iota(env.iota[:, :], pattern=[[1, W]], base=0, channel_multiplier=0,
                                 allow_small_or_imprecise_dtypes=True).then_inc(own_p, one(st))
                pool.iota(env.iotap[:, :], pattern=[[0, 1]], base=0, channel_multiplier=1,
                                 allow_small_or_imprecise_dtypes=True).then_inc(own_p, one(st))
                pool.wait_ge(own_p, steps(st))
                pool.sem_inc(made, 1)

            @block.tensor
            def _(pe):
                pe.wait_ge(loaded, 16 * len(loads))
                pe.wait_ge(made, 1)
                pe.transpose(tp[:, 0:rows], vrow[:, :], env.ident[0:rows, 0:rows])
                pe.transpose(tp[:, 128:256], l2w[:, 0, :], env.ident[:, :])
                pe.transpose(tp[:, 256:384], l2w[:, 1, :], env.ident[:, :]).then_inc(transposed, 1)
                pe.wait_ge(h_in, 1)
                pe.matmul(tp[:, 384:512], spb[:, :], env.w["L1_gnn_W3"], start=True, stop=True).then_inc(h_mm, 1)

            @block.scalar
            def _(act):
                st = Steps(act, own_a)
                act.wait_ge(turned, 1)
                act.activation(sp2[:, 0:1], env.col["L1_gnn_b2"], ACT.Abs).then_inc(own_a, one(st))
                act.wait_ge(own_a, steps(st))
                act.activation(sp2[:, 0:1], sp2[:, 0:1], ACT.Exp, scale=-1.0).then_inc(own_a, one(st))
                act.wait_ge(own_a, steps(st))
                act.activation(sp2[:, 1:2], sp2[:, 0:1], ACT.Ln, bias=1.0).then_inc(soft, 1)

            @block.vector
            def _(v):
                st = Steps(v, own_v)
                v.wait_ge(transposed, 1)
                v.tensor_copy(vcol[:, :], tp[:, 0:rows]).then_inc(own_v, one(st))
                v.tensor_copy(l2t[:, :, :], tp[:, 128:384].rearrange("p (h k) -> p h k", h=2)).then_inc(own_v, one(st))
                v.tensor_scalar(env.onep[:, :], epsb[:, :], 1.0, None, ALU.add).then_inc(own_v, one(st))
                v.wait_ge(own_v, steps(st))
                for i in range(LAYERS):
                    v.tensor_scalar(w1e[:, i, :], w1[:, i, :], env.onep[:, i:i + 1], None, ALU.mult).then_inc(own_v, one(st))
                v.wait_ge(own_v, steps(st))
                v.sem_inc(turned, 1)
                v.tensor_scalar(sp2[:, 2:3], env.col["L1_gnn_b2"], 0.0, -LOG2, ALU.max, ALU.add).then_inc(own_v, one(st))
                v.wait_ge(soft, 1)
                v.wait_ge(own_v, steps(st))
                v.tensor_tensor(sp2[:, 3:4], sp2[:, 1:2], sp2[:, 2:3], ALU.add).then_inc(own_v, one(st))
                v.wait_ge(own_v, steps(st))
                v.tensor_scalar(spb[:, :], env.ones[:, 0:F], sp2[:, 3:4], None, ALU.mult).then_inc(h_in, 1)
                v.wait_ge(h_mm, 1)
                v.tensor_tensor(env.h0, tp[:, 384:512], env.bc["L1_gnn_b3"], ALU.add)



def key_meta(nc, env, tag, load, rows, meta, cols, permuted=False):
    with ExitStack() as ctx:
        def sb(name, shape, dt=fp32):
            return ctx.enter_context(nc.sbuf_tensor(f"{tag}_{name}", shape, dt))
        extra_i = sb("extra_i", [T, 2, P], i32)
        extra = sb("extra", [T, 4, P])
        ec = sb("ec", [T, P, 4])
        part = sb("part", [T, 2, P], i32)
        kf = sb("kf", [T, 3, P])
        mt = sb("mt", [P, T, 4])
        ct = sb("ct", [P, T, 4])
        ps = [ctx.enter_context(nc.psum_tensor(f"{tag}_mp{k}", [P, 512], fp32)) for k in range(2)]
        loaded, cleared, split, turned, copied, stored, own = ctx.enter_context(
            phase(nc, tag + "_meta", "loaded cleared split turned copied stored own"))
        with nc.Block() as block:
            @block.sync
            def _(sp):
                sp.wait_ge(cleared, 1)
                n = load(sp, extra_i, extra, ec, loaded)
                sp.wait_ge(copied, 1)
                sp.dma_start(rows[0].rearrange("(t p) -> t p", p=P), kf[:, 0, :]).then_inc(stored, 16)
                sp.dma_start(rows[1].rearrange("(t p) -> t p", p=P), kf[:, 1, :]).then_inc(stored, 16)
                sp.dma_start(meta, mt[:, :, :].rearrange("p t k -> p (t k)")).then_inc(stored, 16)
                k = 3
                if cols is not None:
                    sp.dma_start(cols, ct[:, :, :].rearrange("p t k -> p (t k)")).then_inc(stored, 16)
                    k += 1
                sp.wait_ge(stored, 16 * k)
                env.key_loads = n

            @block.vector
            def _(v):
                st = Steps(v, own)
                v.memset(extra_i[:, :, :], N).then_inc(own, one(st))
                v.memset(mt[:, :, :], 0.0).then_inc(own, one(st))
                v.memset(ec[:, :, :], 0.0).then_inc(own, one(st))
                v.memset(ct[:, :, :], 0.0).then_inc(own, one(st))
                v.wait_ge(own, steps(st))
                v.memset(extra[:, :, :], 0.0).then_inc(cleared, 1)
                v.wait_ge(loaded, 16 * env.key_loads)
                if permuted:
                    v.tensor_copy(extra_i[:, 0, :], ec[:, :, 1]).then_inc(own, one(st))
                    v.tensor_copy(extra[:, 2, :], ec[:, :, 2]).then_inc(own, one(st))
                    v.tensor_copy(extra_i[:, 1, :], ec[:, :, 0]).then_inc(own, one(st))
                    v.wait_ge(own, steps(st))
                v.tensor_copy(extra[:, 0:2, :], extra_i[:, :, :]).then_inc(own, one(st))
                v.tensor_scalar(part[:, 0, :], extra_i[:, 0, :], 9, None, ALU.logical_shift_right).then_inc(own, one(st))
                v.tensor_scalar(part[:, 1, :], extra_i[:, 0, :], W - 1, None, ALU.bitwise_and).then_inc(own, one(st))
                v.wait_ge(own, steps(st))
                v.tensor_copy(kf[:, 0, :], extra[:, 0, :]).then_inc(own, one(st))
                v.tensor_copy(kf[:, 1:3, :], part[:, :, :]).then_inc(own, one(st))
                v.wait_ge(own, steps(st))
                v.sem_inc(split, 1)
                v.wait_ge(turned, 1)
                for k in range(3):
                    v.tensor_copy(mt[:, :, k], ps[0][:, k * P:k * P + T]).then_inc(own, one(st))
                    v.tensor_copy(ct[:, :, k], ps[1][:, k * P:k * P + T]).then_inc(own, one(st))
                v.wait_ge(own, steps(st))
                v.sem_inc(copied, 1)

            @block.tensor
            def _(pe):
                pe.wait_ge(split, 1)
                for k in range(3):
                    pe.transpose(ps[0][:, k * P:k * P + T], kf[:, k, :], env.ident[0:T, 0:T])
                for k in range(3):
                    last = pe.transpose(ps[1][:, k * P:k * P + T], extra[:, k, :], env.ident[0:T, 0:T])
                last.then_inc(turned, 1)


def rank_edges(nc, env, tag, rows, meta, ranks, vtab, btab, count):
    with ExitStack() as ctx:
        def sb(name, shape, dt=fp32):
            return ctx.enter_context(nc.sbuf_tensor(f"{tag}_r_{name}", shape, dt))

        def pb(name):
            return ctx.enter_context(nc.psum_tensor(f"{tag}_r_{name}", [P, W], fp32))
        mt = sb("mt", [P, 2, G * 4])
        rk = sb("rk", [P, 2, W])
        rh = sb("rh", [P, 2, W])
        ohi = sb("ohi", [P, 2, P], bf16)
        olo = sb("olo", [P, 2, W], bf16)
        oht = sb("oht", [P, 2, P])
        tab = sb("tab", [P, 2, W])
        run = sb("run", [P, W])
        off = sb("off", [P, 1])
        scr = sb("scr", [P, W])
        acc = sb("acc", [P, 2, G, 2])
        res = sb("res", [P, 2, G], i32)
        hist, offp, run_ps = pb("hist"), pb("offp"), pb("run_ps")
        look = [pb(f"look{k}") for k in range(2)]
        sems = ctx.enter_context(phase(
            nc, tag + "_rank", "meta0 meta1 onehot counted total offs tabs own m0 m1 hot hot_used copied looked inc rank0 rank1 st0 st1"))
        (meta0, meta1, onehot, counted, total, offs, tabs, own, m0, m1, hot, hot_used, copied, looked,
         inc, rank0, rank1, st0, st1) = sems
        meta_in, meta2_in, ranked, stored = [meta0, meta1], [m0, m1], [rank0, rank1], [st0, st1]
        mv = meta.rearrange("p (c k) -> p c k", c=CH)
        rvk = rows[0].rearrange("(c w) -> c w", w=W)
        rvh = rows[1].rearrange("(c w) -> c w", w=W)
        rkv = ranks.rearrange("p (c k) -> p c k", c=CH)

        with nc.Block() as block:
            @block.sync
            def _(sp):
                def histo(j):
                    for s in range(2):
                        if not first(j):
                            sp.wait_ge(onehot, (2 * j + s - 1) * G)
                        sp.dma_start(mt[:, s, :], mv[:, 2 * j + s, :]).then_inc(meta_in[s], 16)

                def ranking(j):
                    for s in range(2):
                        if first(j):
                            sp.wait_ge(onehot, CH * G)
                        else:
                            sp.wait_ge(ranked[s], j)
                        c = 2 * j + s
                        sp.dma_start(mt[:, s, :], mv[:, c, :]).then_inc(meta2_in[s], 16)
                        sp.dma_start(rk[:, s, :], rvk[bass.ds(c, 1), :].broadcast_to([P, W])).then_inc(meta2_in[s], 16)
                        sp.dma_start(rh[:, s, :], rvh[bass.ds(c, 1), :].broadcast_to([P, W])).then_inc(meta2_in[s], 16)
                Steps(sp, own).loop(PAIRS, histo)
                Steps(sp, own).loop(PAIRS, ranking)

            def onehots(v, s, g, b):
                v.tensor_scalar(ohi[:, b, :], env.iota[:, 0:P], mt[:, s, g * 4 + 1:g * 4 + 2], None, ALU.is_equal)
                return v.tensor_scalar(olo[:, b, :], env.iota[:, :], mt[:, s, g * 4 + 2:g * 4 + 3], None,
                                       ALU.is_equal)

            @block.vector
            def _(v):
                st = Steps(v, own)

                def histo(j):
                    for s in range(2):
                        v.wait_ge(meta_in[s], 16 * (j + 1))
                        for g in range(G):
                            t = (2 * j + s) * G + g
                            if not (first(j) and s == 0 and g < 2):
                                v.wait_ge(counted, t - 1)
                            onehots(v, s, g, g % 2).then_inc(onehot, 1)
                st.loop(PAIRS, histo)
                v.wait_ge(counted, T)
                v.tensor_copy(count, hist[:, :]).then_inc(own, one(st))
                v.wait_ge(own, steps(st))
                v.tensor_tensor_scan(out=run[:, :], data0=env.ones[:, :], data1=count, initial=0.0,
                                            op0=ALU.mult, op1=ALU.add).then_inc(own, one(st))
                v.wait_ge(own, steps(st))
                v.tensor_copy(off[:, :], run[:, W - 1:W]).then_inc(own, one(st))
                v.wait_ge(own, steps(st))
                v.sem_inc(total, 1)
                v.wait_ge(offs, 1)
                v.tensor_copy(off[:, :], offp[:, 0:1]).then_inc(own, one(st))
                v.wait_ge(own, steps(st))
                v.tensor_scalar(run[:, :], run[:, :], off[:, :], None, ALU.add).then_inc(own, one(st))
                v.wait_ge(own, steps(st))
                v.tensor_tensor(btab, run[:, :], count, ALU.subtract).then_inc(own, one(st))
                v.tensor_scalar(scr[:, :], count, 0.0, None, ALU.is_gt).then_inc(own, one(st))
                v.tensor_scalar(vtab, run[:, :], -1.0 - FAR, None, ALU.add).then_inc(own, one(st))
                v.wait_ge(own, steps(st))
                v.tensor_tensor(vtab, vtab, scr[:, :], ALU.mult).then_inc(own, one(st))
                v.wait_ge(own, steps(st))
                v.tensor_scalar(vtab, vtab, float(FAR), None, ALU.add).then_inc(own, one(st))
                v.wait_ge(own, steps(st))
                v.wait_ge(own, steps(st))
                v.sem_inc(tabs, 1)

                def ranking(j):
                    for s in range(2):
                        v.wait_ge(meta2_in[s], 48 * (j + 1))
                        for g in range(G):
                            t = (2 * j + s) * G + g
                            b = g % 2
                            if not (first(j) and s == 0 and g < 2):
                                v.wait_ge(inc, t - 1)
                            onehots(v, s, g, b)
                            v.tensor_scalar(oht[:, b, :], rh[:, s, g * P:(g + 1) * P], env.iotap[:, :], None,
                                            ALU.is_equal).then_inc(hot, 1)
                            if g == 0 and not first(j):
                                v.wait_ge(ranked[s], j)
                            v.scalar_tensor_tensor(
                                out=scr[:, 0:P], in0=rk[:, s, g * P:(g + 1) * P], scalar=mt[:, s, g * 4:g * 4 + 1],
                                in1=env.earlier[:, :], op0=ALU.is_equal, op1=ALU.mult,
                                accum_out=acc[:, s, g, 0:1]).then_inc(own, one(st))
                            v.wait_ge(own, steps(st))
                            v.wait_ge(looked, t + 1)
                            v.scalar_tensor_tensor(
                                out=scr[:, :], in0=look[b][:, :], scalar=1.0, in1=olo[:, b, :],
                                op0=ALU.mult, op1=ALU.mult, accum_out=acc[:, s, g, 1:2]).then_inc(own, one(st))
                            v.wait_ge(own, steps(st))
                            v.sem_inc(hot_used, 1)
                        if not first(j):
                            v.wait_ge(stored[s], 16 * j)
                        v.tensor_tensor(res[:, s, :], acc[:, s, :, 0], acc[:, s, :, 1], ALU.add)\
                            .then_inc(ranked[s], 1)
                st.loop(PAIRS, ranking)

            @block.tensor
            def _(pe):
                st = Steps(pe, own)

                def count_tile(b, t, start):
                    pe.wait_ge(onehot, t + 1)
                    pe.matmul(hist[:, :], ohi[:, b, :], olo[:, b, :], start=start, stop=False,
                              skip_group_check=True).then_inc(counted, 1)

                def histo(j):
                    for k in range(2 * G):
                        count_tile(k % 2, 2 * G * j + k, first(j) and k == 0)
                st.loop(PAIRS, histo)
                pe.wait_ge(total, 1)
                pe.matmul(offp[:, 0:1], env.below[:, :], off[:, :], start=True, stop=True).then_inc(offs, 1)
                pe.wait_ge(tabs, 1)
                pe.matmul(run_ps[:, :], env.ident[:, :], btab, start=True, stop=False,
                          skip_group_check=True).then_inc(inc, 1)

                def ranking(j):
                    for k in range(2 * G):
                        b = k % 2
                        t = 2 * G * j + k
                        pe.wait_ge(hot, t + 1)
                        pe.wait_ge(copied, t + 1)
                        if not (first(j) and k < 2):
                            pe.wait_ge(hot_used, t - 1)
                        pe.matmul(look[b][:, :], oht[:, b, :], tab[:, b, :], start=True, stop=True)\
                            .then_inc(looked, 1)
                        pe.matmul(run_ps[:, :], ohi[:, b, :], olo[:, b, :], start=False, stop=False,
                                  skip_group_check=True).then_inc(inc, 1)
                st.loop(PAIRS, ranking)

            @block.scalar
            def _(act):
                def ranking(j):
                    for k in range(2 * G):
                        t = 2 * G * j + k
                        act.wait_ge(inc, t + 1)
                        act.activation(tab[:, k % 2, :], run_ps[:, :], ACT.Copy).then_inc(copied, 1)
                Steps(act, own).loop(PAIRS, ranking)

            @block.gpsimd
            def _(pool):
                def store(j):
                    for s in range(2):
                        pool.wait_ge(ranked[s], j + 1)
                        pool.dma_start(rkv[:, 2 * j + s, :], res[:, s, :]).then_inc(stored[s], 16)
                Steps(pool, own).loop(PAIRS, store)
                for s in range(2):
                    pool.wait_ge(stored[s], 16 * PAIRS)


ROW = F + 4
NIX = 8
(IX_SRC, IX_DST, IX_SRC_D, IX_DST_D, IX_SRC_S, IX_DST_S, IX_OUT_D, IX_OUT_S) = range(NIX)
NFL = 4
FL_W, FL_KEEP_S, FL_REAL = range(3)
MROW = 2 * F + 4


def scatter_edges(nc, env, A, D):
    with ExitStack() as ctx:
        row = ctx.enter_context(nc.sbuf_tensor("sc_row", [P, 2, G, ROW], fp32))
        idx = ctx.enter_context(nc.sbuf_tensor("sc_idx", [P, 2, G], i32))
        in0, in1, out0, out1, own = ctx.enter_context(phase(nc, "sc", "in0 in1 out0 out1 own"))
        filled, left = [in0, in1], [out0, out1]
        ev = A["edge_attr_128"]
        cv = D["cols"].rearrange("p (c g k) -> p c g k", c=CH, g=G)
        rv = D["rank_d"].rearrange("p (c g) -> p c g", c=CH)
        whole = PAIRS - 1
        with nc.Block() as block:
            @block.sync
            def _(sp):
                def load(j, last):
                    for s in range(2):
                        c = 2 * j + s
                        if not first(j):
                            sp.wait_ge(left[s], 16 * G * j)
                        sp.dma_start(idx[:, s, :], rv[:, c, :]).then_inc(filled[s], 16)
                        sp.dma_start(row[:, s, :, F:ROW], cv[:, c, :, :]).then_inc(filled[s], 16)
                        if not last:
                            sp.dma_start(row[:, s, :, 0:F],
                                         ev[bass.ds(c * W, W), :].rearrange("(g p) f -> p g f", p=P))\
                                .then_inc(filled[s], 16)
                        elif s == 0:
                            whole_tiles = (E - c * W) // P
                            for g in range(whole_tiles):
                                sp.dma_start(row[:, s, g, 0:F], ev[c * W + g * P:c * W + (g + 1) * P, :])\
                                    .then_inc(filled[s], 16)
                            sp.dma_start(row[0:REST, s, whole_tiles, 0:F], ev[FULL * P:E, :])\
                                .then_inc(filled[s], 16)
                Steps(sp, own).loop(whole, lambda j: load(j, False))
                load(whole, True)

            @block.gpsimd
            def _(pool):
                def scatter(j, extra):
                    for s in range(2):
                        pool.wait_ge(filled[s], 48 * (j + 1) if extra is None else 48 * j + 32 + extra[s])
                        pool.sem_inc(own, 1)
                        for g in range(G):
                            pool.indirect_dma_start(
                                out=D["edges"][:, :], out_offset=bass.IndirectOffsetOnAxis(ap=idx[:, s, g:g + 1], axis=0),
                                in_=row[:, s, g, :], in_offset=None).then_inc(left[s], 16)
                Steps(pool, own).loop(whole, lambda j: scatter(j, None))
                scatter(whole, (16 * ((E - 2 * whole * W) // P + 1), 0))
                for s in range(2):
                    pool.wait_ge(left[s], 16 * G * PAIRS)


def node_tables(nc, env, D, tabs):
    vd, bd, cd, vs, bs, cs = (tabs[:, k, :] for k in range(6))
    with ExitStack() as ctx:
        vv = ctx.enter_context(nc.sbuf_tensor("nt_vv", [P, W, 4], i32))
        free = ctx.enter_context(nc.sbuf_tensor("nt_free", [P, 2, W], fp32))
        made, stored, own = ctx.enter_context(phase(nc, "nt", "made stored own"))
        with nc.Block() as block:
            @block.vector
            def _(v):
                st = Steps(v, own)
                for k, t in enumerate((vd, vs, bd, bs)):
                    v.tensor_copy(vv[:, :, k], t).then_inc(own, one(st))
                v.tensor_scalar(free[:, 0, :], cd, 0.0, None, ALU.is_equal).then_inc(own, one(st))
                v.tensor_scalar(free[:, 1, :], cs, 0.0, None, ALU.is_equal).then_inc(own, one(st))
                v.wait_ge(own, steps(st))
                v.tensor_tensor(free[:, 0, :], free[:, 0, :], free[:, 1, :], ALU.mult).then_inc(own, one(st))
                v.wait_ge(own, steps(st))
                v.sem_inc(made, 1)

            @block.sync
            def _(sp):
                sp.wait_ge(made, 1)
                sp.dma_start(D["bounds"].rearrange("(h l) k -> h (l k)", l=W),
                             vv[0:HI, :, :].rearrange("h l k -> h (l k)")).then_inc(stored, 16)
                sp.dma_start(D["free"].rearrange("(h l) -> h l", l=W), free[0:HI, 0, :]).then_inc(stored, 16)
                sp.wait_ge(stored, 32)


def node_bounds(nc, env, D):
    with ExitStack() as ctx:
        cf = ctx.enter_context(nc.sbuf_tensor("nb_cf", [P, T, 4], fp32))
        ci = ctx.enter_context(nc.sbuf_tensor("nb_ci", [P, 2, T], i32))
        ix = ctx.enter_context(nc.sbuf_tensor("nb_ix", [P, 2, 2, G], i32))
        got = ctx.enter_context(nc.sbuf_tensor("nb_got", [P, 2, 2, G, 4], i32))
        loaded, made, istored, in0, in1, g0, g1, o0, o1, own_v, own = ctx.enter_context(
            phase(nc, "nb", "loaded made istored in0 in1 g0 g1 o0 o1 own_v own"))
        filled, gathered, stored = [in0, in1], [g0, g1], [o0, o1]
        kv = D["keys_i"].rearrange("p (k c g) -> p k c g", k=2, g=G)
        ov = D["edge_bounds"].rearrange("p (c k g b) -> p c k g b", k=2, g=G, b=4)
        with nc.Block() as block:
            @block.vector
            def _(v):
                st = Steps(v, own_v)
                v.wait_ge(loaded, 16)
                v.tensor_copy(ci[:, 0, :], cf[:, :, 0]).then_inc(own_v, one(st))
                v.tensor_copy(ci[:, 1, :], cf[:, :, 1]).then_inc(own_v, one(st))
                v.wait_ge(own_v, steps(st))
                v.sem_inc(made, 1)

            @block.sync
            def _(sp):
                sp.dma_start(cf[:, :, :].rearrange("p t k -> p (t k)"), D["cols_s"]).then_inc(loaded, 16)
                sp.wait_ge(made, 1)
                sp.dma_start(D["keys_i"], ci[:, :, :].rearrange("p k t -> p (k t)")).then_inc(istored, 16)
                sp.wait_ge(istored, 16)

                def load(c, j, s):
                    if not first(j):
                        sp.wait_ge(gathered[s], 128 * j)
                    sp.dma_start(ix[:, s, :, :], kv[:, :, c, :]).then_inc(filled[s], 16)

                def store(c, j, s):
                    sp.wait_ge(gathered[s], 128 * (j + 1))
                    sp.dma_start(ov[:, c, :, :, :].rearrange("p k g b -> p (k g b)"), got[:, s, :, :, :].rearrange("p k g b -> p (k g b)"))\
                        .then_inc(stored[s], 16)
                pipeline(Steps(sp, own), CH, 2, (0, load), (1, store))
                for s in range(2):
                    sp.wait_ge(stored[s], 16 * PAIRS)

            @block.gpsimd
            def _(pool):
                def gather(c, j, s):
                    pool.wait_ge(filled[s], 16 * (j + 1))
                    if not first(j):
                        pool.wait_ge(stored[s], 16 * j)
                    for k in range(2):
                        pool.sem_inc(own, 1)
                        for g in range(G):
                            pool.indirect_dma_start(
                                out=got[:, s, k, g, :], out_offset=None, in_=D["bounds"][:, :],
                                in_offset=bass.IndirectOffsetOnAxis(ap=ix[:, s, k, g:g + 1], axis=0))\
                                .then_inc(gathered[s], 16)
                pipeline(Steps(pool, own), CH, 2, (0, gather))


def slot_indices(nc, env, D):
    with ExitStack() as ctx:
        def sb(name, shape, dt=fp32):
            return ctx.enter_context(nc.sbuf_tensor(f"si_{name}", shape, dt))
        cf, rki, bi = sb("cf", [P, T, 4]), sb("rki", [P, T], i32), sb("bi", [P, CH, 2, G, 4], i32)
        b = sb("b", [P, 2, 4, T])
        rank = sb("rank", [P, T])
        slot, far = sb("slot", [P, T]), sb("far", [P, T])
        real, td, ts, tmp, tmp2, ond, ons = (sb(n, [P, T]) for n in ("real", "td", "ts", "tmp", "tmp2", "ond", "ons"))
        ixf, ixi, ixo = sb("ixf", [P, T]), sb("ixi", [P, T, NIX], i32), sb("ixo", [P, 2, T, NIX], i32)
        fl, rowf, mcol, corner = sb("fl", [P, T, NFL]), sb("rowf", [T, 3, P]), sb("mcol", [P, 2]), sb("corner", [P, 1])
        tp = ctx.enter_context(nc.psum_tensor("si_tp", [P, 512], fp32))
        loaded, iota_done, summed, m_done, made, turned, copied, stored, own, own_p = ctx.enter_context(
            phase(nc, "si", "loaded iota_done summed m_done made turned copied stored own own_p"))
        with nc.Block() as block:
            @block.sync
            def _(sp):
                sp.dma_start(cf[:, :, :].rearrange("p t k -> p (t k)"), D["cols_s"]).then_inc(loaded, 16)
                sp.dma_start(rki[:, :], D["rank_s"]).then_inc(loaded, 16)
                sp.dma_start(bi[:, :, :, :, :].rearrange("p c k g b -> p (c k g b)"), D["edge_bounds"])\
                    .then_inc(loaded, 16)
                sp.wait_ge(copied, 1)
                sp.dma_start(D["keep_d"].rearrange("(t p) -> t p", p=P), rowf[:, 0, :]).then_inc(stored, 16)
                sp.dma_start(D["weights"][0:EP].rearrange("(t p) -> t p", p=P), rowf[:, 1, :]).then_inc(stored, 16)
                sp.dma_start(D["weights"][EP:2 * EP].rearrange("(t p) -> t p", p=P), rowf[:, 2, :])\
                    .then_inc(stored, 16)
                sp.dma_start(D["index"], ixi[:, :, :].rearrange("p t k -> p (t k)")).then_inc(stored, 16)
                sp.dma_start(D["factor"], fl[:, :, :].rearrange("p t k -> p (t k)")).then_inc(stored, 16)
                for k in range(2):
                    sp.dma_start(D["index2"][:, k * T * NIX:(k + 1) * T * NIX],
                                 ixo[:, k, :, :].rearrange("p t k -> p (t k)")).then_inc(stored, 16)
                sp.wait_ge(stored, 112)

            @block.gpsimd
            def _(pool):
                st = Steps(pool, own_p)
                pool.iota(slot[:, :], pattern=[[P, T]], base=0, channel_multiplier=1,
                                 allow_small_or_imprecise_dtypes=True).then_inc(own_p, one(st))
                pool.memset(corner[:, :], 0.0).then_inc(own_p, one(st))
                pool.wait_ge(own_p, steps(st))
                pool.affine_select(out=corner[:, :], in_=corner[:, :], compare_op=ALU.not_equal, fill=1.0,
                                          base=1 - P, pattern=[[0, 1]], channel_multiplier=1).then_inc(own_p, one(st))
                pool.wait_ge(own_p, steps(st))
                pool.sem_inc(iota_done, 1)

            @block.vector
            def _(v):
                st = Steps(v, own)

                def do(ins):
                    ins.then_inc(own, one(st))
                    v.wait_ge(own, steps(st))
                v.wait_ge(loaded, 48)
                v.wait_ge(iota_done, 1)
                for k in range(2):
                    for q in range(4):
                        v.tensor_copy(b[:, k, q, :].rearrange("p (c g) -> p c g", g=G), bi[:, :, k, :, q]).then_inc(own, one(st))
                v.memset(far[:, :], float(FAR)).then_inc(own, one(st))
                v.memset(fl[:, :, :], 0.0).then_inc(own, one(st))
                do(v.tensor_copy(rank[:, :], rki[:, :]))
                src, dst = cf[:, :, 0], cf[:, :, 1]
                s_vd, s_vs, s_bd, s_bs = (b[:, 0, q, :] for q in range(4))
                d_vd, d_vs, d_bd, d_bs = (b[:, 1, q, :] for q in range(4))
                do(v.tensor_scalar(real[:, :], slot[:, :], float(E), None, ALU.is_lt))
                do(v.tensor_scalar(td[:, :], s_vd, float(FAR), None, ALU.is_lt))
                do(v.tensor_tensor(td[:, :], td[:, :], real[:, :], ALU.mult))
                do(v.tensor_scalar(ts[:, :], d_vs, float(FAR), None, ALU.is_lt))

                def put(k, value):
                    do(v.tensor_copy(ixi[:, :, k], value))

                def pick(k, cond, value, other, shift):
                    do(v.tensor_scalar(tmp[:, :], other, float(shift), None, ALU.add))
                    do(v.tensor_tensor(tmp2[:, :], value, cond, ALU.mult))
                    do(v.tensor_scalar(ixf[:, :], cond, -1.0, 1.0, ALU.mult, ALU.add))
                    do(v.tensor_tensor(tmp[:, :], tmp[:, :], ixf[:, :], ALU.mult))
                    do(v.tensor_tensor(tmp[:, :], tmp[:, :], tmp2[:, :], ALU.add))
                    put(k, tmp[:, :])
                do(v.tensor_scalar(tmp[:, :], src, float(N - 1), None, ALU.min))
                put(IX_SRC, tmp[:, :])
                do(v.tensor_scalar(tmp[:, :], dst, float(N - 1), None, ALU.min))
                put(IX_DST, tmp[:, :])
                pick(IX_SRC_D, td[:, :], s_vd, slot[:, :], EP)
                put(IX_DST_D, d_vd)
                put(IX_SRC_S, s_vs)
                pick(IX_DST_S, ts[:, :], d_vs, slot[:, :], EP)
                do(v.tensor_tensor(ond[:, :], slot[:, :], d_vd, ALU.is_equal))
                do(v.tensor_tensor(ond[:, :], ond[:, :], real[:, :], ALU.mult))
                pick(IX_OUT_D, ond[:, :], dst, far[:, :], 0)
                do(v.tensor_tensor(fl[:, :, FL_KEEP_S], rank[:, :], s_bs, ALU.not_equal))
                do(v.tensor_tensor(ons[:, :], rank[:, :], s_bs, ALU.is_equal))
                do(v.tensor_tensor(ons[:, :], ons[:, :], real[:, :], ALU.mult))
                do(v.tensor_tensor(tmp[:, :], ons[:, :], td[:, :], ALU.mult))
                do(v.tensor_tensor(ons[:, :], ons[:, :], tmp[:, :], ALU.subtract))
                pick(IX_OUT_S, ons[:, :], src, far[:, :], 0)
                do(v.tensor_copy(fl[:, :, FL_W], cf[:, :, 2]))
                do(v.tensor_copy(fl[:, :, FL_REAL], real[:, :]))
                do(v.tensor_copy(ixo[:, 0, :, :], ixi[:, :, :]))
                do(v.tensor_copy(ixo[:, 1, :, :], ixi[:, :, :]))
                do(v.tensor_copy(ixo[:, 0, :, 0], ixi[:, :, IX_OUT_D]))
                do(v.tensor_copy(ixo[:, 1, :, 0], ixi[:, :, IX_OUT_S]))
                do(v.reduce_sum(mcol[:, 0:1], ond[:, :], axis=mybir.AxisListType.X))
                do(v.reduce_sum(mcol[:, 1:2], ons[:, :], axis=mybir.AxisListType.X))
                do(v.tensor_tensor(mcol[:, 0:1], mcol[:, 0:1], mcol[:, 1:2], ALU.add))
                v.wait_ge(own, steps(st))
                v.sem_inc(summed, 1)
                v.wait_ge(m_done, 1)
                do(v.tensor_scalar(mcol[:, 1:2], tp[:, 0:1], corner[:, :], -1.0, ALU.mult, ALU.mult))
                do(v.tensor_tensor(ons[:, T - 1:T], ons[:, T - 1:T], mcol[:, 1:2], ALU.add))
                do(v.tensor_tensor(tmp[:, :], slot[:, :], d_bd, ALU.not_equal))
                v.wait_ge(own, steps(st))
                v.sem_inc(made, 1)
                v.wait_ge(turned, 1)
                do(v.tensor_copy(rowf[:, :, :], tp[0:T, 128:512].rearrange("t (k p) -> t k p", k=3)))
                v.wait_ge(own, steps(st))
                v.sem_inc(copied, 1)

            @block.tensor
            def _(pe):
                pe.wait_ge(summed, 1)
                pe.matmul(tp[:, 0:1], env.ones[:, 0:P], mcol[:, 0:1], start=True, stop=True).then_inc(m_done, 1)
                pe.wait_ge(made, 1)
                pe.transpose(tp[0:T, 128:256], tmp[:, :], env.ident[:, :])
                pe.transpose(tp[0:T, 256:384], ond[:, :], env.ident[:, :])
                pe.transpose(tp[0:T, 384:512], ons[:, :], env.ident[:, :]).then_inc(turned, 1)


def rows4(ap, c):
    return ap[bass.ds(c * W, W), :].rearrange("(g p) f -> p g f", p=P)


def spread(row, n=G):
    return row.rearrange("p (a f) -> p a f", a=1).broadcast_to([row.shape[0], n, F])


def norm_stats(v, st, x, stats, mv, scale=1.0, eps=LN_EPS):
    n = x.shape[1]
    for g in range(n):
        v.bn_stats(stats[:, g, :], x[:, g, :]).then_inc(st.sem, one(st))
    v.wait_ge(st.sem, steps(st))
    v.sem_inc(st.sem, one(st))
    for g in range(n):
        v.bn_aggr(mv[:, g, :], stats[:, g, :]).then_inc(st.sem, one(st))
    v.wait_ge(st.sem, steps(st))
    v.tensor_scalar(mv[:, :, 1], mv[:, :, 1], scale, eps, ALU.mult, ALU.add).then_inc(st.sem, one(st))


def norm_apply(v, st, x, mv, sd, out, mask=None):
    v.reciprocal(sd, sd).then_inc(st.sem, one(st))
    v.wait_ge(st.sem, steps(st))
    if mask is not None:
        v.tensor_tensor(sd, sd, mask, ALU.mult).then_inc(st.sem, one(st))
        v.wait_ge(st.sem, steps(st))
    for g in range(x.shape[1]):
        v.tensor_scalar(out[:, g, :], x[:, g, :], mv[:, g, 0:1], sd[:, g:g + 1], ALU.subtract, ALU.mult).then_inc(st.sem, one(st))


def views(D):
    return (D["index"].rearrange("p (c k) -> p c k", c=CH), D["factor"].rearrange("p (c k) -> p c k", c=CH),
            D["keep_d"].rearrange("(c w) -> c w", w=W))


def gather4(pool, out, table, ix, k, sem):
    for g in range(G):
        pool.indirect_dma_start(out=out[:, g, :], out_offset=None, in_=table,
                                in_offset=bass.IndirectOffsetOnAxis(ap=ix[:, g * NIX + k:g * NIX + k + 1], axis=0))\
            .then_inc(sem, 16)


def transpose4(pe, env, out, rows, parts=P):
    for g in range(G):
        last = pe.transpose(out[:, g * parts:(g + 1) * parts], rows[:, g, :], env.ident[0:parts, 0:parts])
    return last


def to_rows4(pe, out, cols, w, parts=P):
    for g in range(G):
        last = pe.matmul(out[0:parts, g * F:(g + 1) * F], cols[:, g * parts:(g + 1) * parts], w,
                         start=True, stop=True)
    return last


def uses(s, n=CH):
    return (n - s + NS - 1) // NS


class Mem:

    def __init__(self, nc, ctx, tag):
        self.nc, self.ctx, self.tag = nc, ctx, tag

    def sb(self, name, *shape, dt=fp32):
        return self.ctx.enter_context(self.nc.sbuf_tensor(f"{self.tag}_{name}", [P, *shape], dt))

    def ps(self, name):
        return self.ctx.enter_context(self.nc.psum_tensor(f"{self.tag}_{name}", [P, W], fp32))

    def sems(self, names):
        return self.ctx.enter_context(phase(self.nc, self.tag, names))


def edge_layer0(nc, env, A, D):
    with ExitStack() as ctx:
        m = Mem(nc, ctx, "e0")
        ix, fl, keep = m.sb("ix", NS, G * NIX, dt=i32), m.sb("fl", NS, G * NFL), m.sb("keep", NS, W)
        xs, xd, ms = m.sb("xs", NS, G, F), m.sb("xd", NS, G, F), m.sb("ms", NS, G, F)
        agg, zs, zd = m.sb("agg", NS, W), m.sb("zs", NS, W), m.sb("zd", NS, W)
        hs, hd = m.sb("hs", NS, W), m.sb("hd", NS, W)
        vv, stats, mv, sd = m.sb("vv", 2 * G, F), m.sb("stats", 2 * G, 6), m.sb("mv", 2 * G, 2), m.sb("sd", 2 * G)
        xo = m.sb("xo", NS, 2, G, F)
        tm, ts, td, ps_s, ps_d, o_s, o_d = (m.ps(n) for n in ("tm", "ts", "td", "ps_s", "ps_d", "o_s", "o_d"))
        (filled, got, stored, weighted, turned, summed, copied, hidden, relued, projected, added, measured, rooted,
         normed, own_v, own_a, own) = m.sems("filled* got* stored* weighted turned summed copied hidden relued projected "
                                             "added measured rooted normed own_v own_a own")
        iv, fv, kv = views(D)
        with nc.Block() as block:
            @block.sync
            def _(sp):
                def load(c, j, s):
                    if not first(j):
                        sp.wait_ge(normed, c + 1 - NS)
                    sp.sem_inc(own, 1)
                    sp.dma_start(ix[:, s, :], iv[:, c, :]).then_inc(filled[s], 16)
                    sp.dma_start(fl[:, s, :], fv[:, c, :]).then_inc(filled[s], 16)
                    sp.dma_start(keep[:, s, :], kv[bass.ds(c, 1), :].broadcast_to([P, W])).then_inc(filled[s], 16)

                def store(c, j, s):
                    sp.wait_ge(normed, c + 1)
                    sp.sem_inc(own, 1)
                    sp.dma_start(rows4(D["x1"], c), xo[:, s, 1, :, :]).then_inc(stored[s], 16)
                    sp.dma_start(rows4(D["x1"], c + CH), xo[:, s, 0, :, :]).then_inc(stored[s], 16)
                pipeline(Steps(sp, own), CH, NS, (NS, store), (0, load))
                for s in range(NS):
                    sp.wait_ge(stored[s], 32 * uses(s))

            @block.gpsimd
            def _(pool):
                def gather(c, j, s):
                    pool.wait_ge(filled[s], 48 * (j + 1))
                    pool.sem_inc(own, 1)
                    gather4(pool, xs[:, s, :, :], A["x"], ix[:, s, :], IX_SRC, got[s])
                    gather4(pool, xd[:, s, :, :], A["x"], ix[:, s, :], IX_DST, got[s])
                pipeline(Steps(pool, own), CH, NS, (0, gather))

            @block.vector
            def _(v):
                st = Steps(v, own_v)

                def weigh(c, j, s):
                    v.wait_ge(got[s], 128 * (j + 1))
                    if not first(j):
                        v.wait_ge(turned, c + 1 - NS)
                    for g in range(G):
                        k = g * NFL + FL_W
                        v.tensor_scalar(ms[:, s, g, :], xs[:, s, g, :], fl[:, s, k:k + 1], None, ALU.mult).then_inc(own_v, one(st))
                    v.wait_ge(own_v, steps(st))
                    v.sem_inc(weighted, 1)

                def scan(c, j, s):
                    v.wait_ge(turned, c + 1)
                    start = 0.0 if first(j) and s == 0 else agg[:, (s - 1) % NS, W - 1:W]
                    v.tensor_tensor_scan(out=agg[:, s, :], data0=keep[:, s, :], data1=tm[:, :], initial=start,
                                                op0=ALU.mult, op1=ALU.add).then_inc(own_v, one(st))
                    v.wait_ge(own_v, steps(st))
                    v.tensor_tensor(zd[:, s, :], td[:, :], agg[:, s, :], ALU.add).then_inc(own_v, one(st))
                    v.wait_ge(own_v, steps(st))
                    v.sem_inc(summed, 1)

                def norm(c, j, s):
                    v.wait_ge(projected, c + 1)
                    v.tensor_tensor(vv[:, 0:G, :], o_s[:, :].rearrange("p (g f) -> p g f", g=G),
                                           xs[:, s, :, :], ALU.add).then_inc(own_v, one(st))
                    v.tensor_tensor(vv[:, G:2 * G, :], o_d[:, :].rearrange("p (g f) -> p g f", g=G),
                                           xd[:, s, :, :], ALU.add).then_inc(own_v, one(st))
                    v.wait_ge(own_v, steps(st))
                    v.sem_inc(added, 1)
                    v.tensor_tensor(vv[:, :, :], vv[:, :, :], spread(env.bc["L0_gnn_b2"], 2 * G), ALU.add).then_inc(own_v, one(st))
                    v.wait_ge(own_v, steps(st))
                    norm_stats(v, st, vv, stats, mv)
                    v.wait_ge(own_v, steps(st))
                    v.sem_inc(measured, 1)
                    v.wait_ge(rooted, c + 1)
                    if not first(j):
                        v.wait_ge(stored[s], 32 * j)
                    norm_apply(v, st, vv, mv, sd[:, :], xo[:, s, :, :, :].rearrange("p k g f -> p (k g) f"))
                    v.wait_ge(own_v, steps(st))
                    v.sem_inc(normed, 1)
                pipeline(st, CH, NS, (2, norm), (1, scan), (0, weigh))

            @block.scalar
            def _(act):
                st = Steps(act, own_a)

                def copy(c, j, s):
                    act.wait_ge(turned, c + 1)
                    act.activation(zs[:, s, :], ts[:, :], ACT.Copy).then_inc(copied, 1)

                def relu(c, j, s):
                    act.wait_ge(hidden, c + 1)
                    if not first(j):
                        act.wait_ge(projected, c + 1 - NS)
                    act.activation(hs[:, s, :], ps_s[:, :], ACT.Relu, bias=env.col["L0_gnn_b1"]).then_inc(own_a, one(st))
                    act.activation(hd[:, s, :], ps_d[:, :], ACT.Relu, bias=env.col["L0_gnn_b1"]).then_inc(own_a, one(st))
                    act.wait_ge(own_a, steps(st))
                    act.sem_inc(relued, 1)

                def root(c, j, s):
                    act.wait_ge(measured, c + 1)
                    act.activation(sd[:, :], mv[:, :, 1], ACT.Sqrt).then_inc(rooted, 1)
                pipeline(st, CH, NS, (2, root), (1, copy), (1, relu))

            @block.tensor
            def _(pe):
                def turn(c, j, s):
                    pe.wait_ge(weighted, c + 1)
                    if not (first(j) and s == 0):
                        pe.wait_ge(summed, c)
                        pe.wait_ge(copied, c)
                    transpose4(pe, env, tm, ms[:, s, :, :])
                    transpose4(pe, env, ts, xs[:, s, :, :])
                    transpose4(pe, env, td, xd[:, s, :, :]).then_inc(turned, 1)

                def hide(c, j, s):
                    pe.wait_ge(summed, c + 1)
                    pe.wait_ge(copied, c + 1)
                    if not (first(j) and s == 0):
                        pe.wait_ge(relued, c)
                    pe.matmul(ps_s[:, :], env.w["L0_gnn_W1"], zs[:, s, :], start=True, stop=True)
                    pe.matmul(ps_d[:, :], env.w["L0_gnn_W1"], zd[:, s, :], start=True, stop=True)\
                        .then_inc(hidden, 1)

                def project(c, j, s):
                    pe.wait_ge(relued, c + 1)
                    if not (first(j) and s == 0):
                        pe.wait_ge(added, c)
                    to_rows4(pe, o_s, hs[:, s, :], env.w["L0_gnn_W2"])
                    to_rows4(pe, o_d, hd[:, s, :], env.w["L0_gnn_W2"]).then_inc(projected, 1)
                pipeline(Steps(pe, own), CH, NS, (2, project), (1, hide), (0, turn))


def soft_plus_scalar(act, st, src, bias, t, r):
    act.activation(r, src, ACT.Relu, bias=bias).then_inc(st.sem, one(st))
    act.activation(t, src, ACT.Abs, bias=bias).then_inc(st.sem, one(st))
    act.wait_ge(st.sem, steps(st))
    act.activation(t, t, ACT.Exp, scale=-1.0).then_inc(st.sem, one(st))
    act.wait_ge(st.sem, steps(st))
    act.activation(t, t, ACT.Ln, bias=1.0).then_inc(st.sem, one(st))


def edge_layer1(nc, env, D):
    with ExitStack() as ctx:
        m = Mem(nc, ctx, "e1")
        ix, fl, rk = m.sb("ix", NS, G * NIX, dt=i32), m.sb("fl", NS, G * NFL), m.sb("rk", NS, G, dt=i32)
        ea, xd, mr = m.sb("ea", NS, G, F), m.sb("xd", NS, G, F), m.sb("mr", NS, G, MROW)
        xt, et, sp_t, sp_r, fs = m.sb("xt", NS, W), m.sb("et", NS, W), m.sb("sp_t", W), m.sb("sp_r", W), m.sb("fs", NS, W)
        fr = m.sb("fr", G, F)
        vv, stats, mv, sd, xo = m.sb("vv", G, F), m.sb("stats", G, 6), m.sb("mv", G, 2), m.sb("sd", G), m.sb("xo", NS, G, F)
        td, te, pe1, pf, px = (m.ps(n) for n in ("td", "te", "pe1", "pf", "px"))
        (filled, got, stored, sent, turned, copied_x, copied_e, hidden, softened, filtered, projected, multiplied,
         measured, rooted, normed, own_v, own_a, own) = m.sems(
            "filled* got* stored* sent* turned copied_x copied_e hidden softened filtered projected multiplied "
            "measured rooted normed own_v own_a own")
        iv, fv, kv = views(D)
        rv = D["rank_s"].rearrange("p (c g) -> p c g", c=CH)
        with nc.Block() as block:
            @block.sync
            def _(sp):
                def load(c, j, s):
                    if not first(j):
                        sp.wait_ge(normed, c + 1 - NS)
                        sp.sem_inc(own, 1)
                        sp.wait_ge(sent[s], 16 * G * j)
                    sp.sem_inc(own, 1)
                    sp.dma_start(ix[:, s, :], iv[:, c, :]).then_inc(filled[s], 16)
                    sp.dma_start(fl[:, s, :], fv[:, c, :]).then_inc(filled[s], 16)
                    sp.dma_start(rk[:, s, :], rv[:, c, :]).then_inc(filled[s], 16)
                    sp.dma_start(ea[:, s, :, :], rows4(D["edges"], c)[:, :, 0:F]).then_inc(filled[s], 16)

                def store(c, j, s):
                    sp.wait_ge(normed, c + 1)
                    sp.sem_inc(own, 1)
                    sp.dma_start(rows4(D["x2"], c + CH), xo[:, s, :, :]).then_inc(stored[s], 16)
                pipeline(Steps(sp, own), CH, NS, (NS, store), (0, load))
                for s in range(NS):
                    sp.wait_ge(stored[s], 16 * uses(s))

            @block.gpsimd
            def _(pool):
                def gather(c, j, s):
                    pool.wait_ge(filled[s], 64 * (j + 1))
                    pool.sem_inc(own, 1)
                    gather4(pool, xd[:, s, :, :], D["x1"], ix[:, s, :], IX_DST_D, got[s])
                    gather4(pool, mr[:, s, :, F:2 * F], D["x1"], ix[:, s, :], IX_SRC_D, got[s])

                def send(c, j, s):
                    pool.wait_ge(multiplied, c + 1)
                    pool.wait_ge(got[s], 128 * (j + 1))
                    pool.sem_inc(own, 1)
                    for g in range(G):
                        pool.indirect_dma_start(
                            out=D["message"], out_offset=bass.IndirectOffsetOnAxis(ap=rk[:, s, g:g + 1], axis=0),
                            in_=mr[:, s, g, :], in_offset=None).then_inc(sent[s], 16)
                pipeline(Steps(pool, own), CH, NS, (0, gather), (3, send))
                for s in range(NS):
                    pool.wait_ge(sent[s], 16 * G * uses(s))

            @block.vector
            def _(v):
                st = Steps(v, own_v)

                def copy(c, j, s):
                    v.wait_ge(turned, c + 1)
                    v.tensor_copy(et[:, s, :], te[:, :]).then_inc(copied_e, 1)

                def filt(c, j, s):
                    v.wait_ge(softened, c + 1)
                    if not first(j):
                        v.wait_ge(projected, c + 1 - NS)
                    v.scalar_tensor_tensor(out=fs[:, s, :], in0=sp_r[:, :], scalar=-LOG2, in1=sp_t[:, :],
                                                  op0=ALU.add, op1=ALU.add).then_inc(own_v, one(st))
                    v.wait_ge(own_v, steps(st))
                    v.sem_inc(filtered, 1)

                def product(c, j, s):
                    v.wait_ge(projected, c + 1)
                    v.wait_ge(got[s], 128 * (j + 1))
                    v.tensor_tensor(fr[:, :, :], pf[:, :].rearrange("p (g f) -> p g f", g=G),
                                           spread(env.bc["L1_gnn_be2"]), ALU.add).then_inc(own_v, one(st))
                    v.wait_ge(own_v, steps(st))
                    if first(j):
                        v.memset(mr[:, s, :, 2 * F:MROW], 0.0).then_inc(own_v, one(st))
                        v.wait_ge(own_v, steps(st))
                    else:
                        v.memset(vv[:, 0, 0:1], 0.0).then_inc(own_v, one(st))
                    v.tensor_tensor(mr[:, s, :, 0:F], fr[:, :, :], px[:, :].rearrange("p (g f) -> p g f", g=G),
                                           ALU.mult).then_inc(own_v, one(st))
                    v.tensor_copy(mr[:, s, :, 2 * F], fl[:, s, :].rearrange("p (g k) -> p g k", k=NFL)
                                         [:, :, FL_KEEP_S]).then_inc(own_v, one(st))
                    v.wait_ge(own_v, steps(st))
                    v.sem_inc(multiplied, 1)
                    v.scalar_tensor_tensor(out=vv[:, :, :], in0=xd[:, s, :, :], scalar=2.0,
                                                  in1=spread(env.h0), op0=ALU.mult, op1=ALU.add).then_inc(own_v, one(st))
                    v.wait_ge(own_v, steps(st))
                    norm_stats(v, st, vv, stats, mv)
                    v.wait_ge(own_v, steps(st))
                    v.sem_inc(measured, 1)
                    v.wait_ge(rooted, c + 1)
                    if not first(j):
                        v.wait_ge(stored[s], 16 * j)
                    norm_apply(v, st, vv, mv, sd[:, :], xo[:, s, :, :])
                    v.wait_ge(own_v, steps(st))
                    v.sem_inc(normed, 1)
                pipeline(st, CH, NS, (2, product), (1, filt), (0, copy))

            @block.scalar
            def _(act):
                st = Steps(act, own_a)

                def copy(c, j, s):
                    act.wait_ge(turned, c + 1)
                    act.activation(xt[:, s, :], td[:, :], ACT.Copy).then_inc(copied_x, 1)

                def soft(c, j, s):
                    act.wait_ge(hidden, c + 1)
                    if not (first(j) and s == 0):
                        act.wait_ge(filtered, c)
                    soft_plus_scalar(act, st, pe1[:, :], env.col["L1_gnn_be1"], sp_t[:, :], sp_r[:, :])
                    act.wait_ge(own_a, steps(st))
                    act.sem_inc(softened, 1)

                def root(c, j, s):
                    act.wait_ge(measured, c + 1)
                    act.activation(sd[:, :], mv[:, :, 1], ACT.Sqrt).then_inc(rooted, 1)
                pipeline(st, CH, NS, (2, root), (1, soft), (0, copy))

            @block.tensor
            def _(pe):
                def turn(c, j, s):
                    pe.wait_ge(got[s], 128 * (j + 1))
                    pe.wait_ge(filled[s], 64 * (j + 1))
                    if not (first(j) and s == 0):
                        pe.wait_ge(copied_x, c)
                        pe.wait_ge(copied_e, c)
                    transpose4(pe, env, td, xd[:, s, :, :])
                    transpose4(pe, env, te, ea[:, s, :, :]).then_inc(turned, 1)

                def hide(c, j, s):
                    pe.wait_ge(copied_e, c + 1)
                    if not (first(j) and s == 0):
                        pe.wait_ge(softened, c)
                    pe.matmul(pe1[:, :], env.w["L1_gnn_We1"], et[:, s, :], start=True, stop=True).then_inc(hidden, 1)

                def project(c, j, s):
                    pe.wait_ge(filtered, c + 1)
                    pe.wait_ge(copied_x, c + 1)
                    if not (first(j) and s == 0):
                        pe.wait_ge(multiplied, c)
                    to_rows4(pe, px, xt[:, s, :], env.w["L1_gnn_Wn"])
                    to_rows4(pe, pf, fs[:, s, :], env.w["L1_gnn_We2"]).then_inc(projected, 1)
                pipeline(Steps(pe, own), CH, NS, (2, project), (1, hide), (0, turn))


def keep_rows(nc, env, D):
    with ExitStack() as ctx:
        m = Mem(nc, ctx, "kr")
        buf, row = m.sb("buf", P, 4), m.sb("row", P)
        loaded, copied, stored = m.sems("loaded copied stored")
        with nc.Block() as block:
            @block.sync
            def _(sp):
                sp.dma_start(buf[0:T, :, :], D["message"].rearrange("(t p) f -> t p f", p=P)[:, :, 2 * F:MROW])\
                    .then_inc(loaded, 16)
                sp.wait_ge(copied, 1)
                sp.dma_start(D["keep_s"].rearrange("(t p) -> t p", p=P), row[0:T, :]).then_inc(stored, 16)
                sp.wait_ge(stored, 16)

            @block.vector
            def _(v):
                v.wait_ge(loaded, 16)
                v.tensor_copy(row[0:T, :], buf[0:T, :, 0]).then_inc(copied, 1)


def source_layer1(nc, env, D):
    with ExitStack() as ctx:
        m = Mem(nc, ctx, "s1")
        mr, keep = m.sb("mr", NS, G, MROW), m.sb("keep", NS, W)
        agg, sp_t, sp_r, fs = m.sb("agg", NS, W), m.sb("sp_t", W), m.sb("sp_r", W), m.sb("fs", NS, W)
        vv, stats, mv, sd, xo = m.sb("vv", G, F), m.sb("stats", G, 6), m.sb("mv", G, 2), m.sb("sd", G), m.sb("xo", NS, G, F)
        tm, ph, po = (m.ps(n) for n in ("tm", "ph", "po"))
        (filled, stored, turned, summed, hidden, softened, filtered, projected, added,
         measured, rooted, normed, own_v, own_a, own) = m.sems(
            "filled* stored* turned summed hidden softened filtered projected added measured rooted normed own_v own_a own")
        kv = D["keep_s"].rearrange("(c w) -> c w", w=W)
        with nc.Block() as block:
            @block.sync
            def _(sp):
                def load(c, j, s):
                    if not first(j):
                        sp.wait_ge(normed, c + 1 - NS)
                    sp.sem_inc(own, 1)
                    sp.dma_start(mr[:, s, :, :], rows4(D["message"], c)).then_inc(filled[s], 16)
                    sp.dma_start(keep[:, s, :], kv[bass.ds(c, 1), :].broadcast_to([P, W])).then_inc(filled[s], 16)

                def store(c, j, s):
                    sp.wait_ge(normed, c + 1)
                    sp.sem_inc(own, 1)
                    sp.dma_start(rows4(D["x2"], c), xo[:, s, :, :]).then_inc(stored[s], 16)
                pipeline(Steps(sp, own), CH, NS, (NS, store), (0, load))
                for s in range(NS):
                    sp.wait_ge(stored[s], 16 * uses(s))

            @block.vector
            def _(v):
                st = Steps(v, own_v)

                def scan(c, j, s):
                    v.wait_ge(turned, c + 1)
                    start = 0.0 if first(j) and s == 0 else agg[:, (s - 1) % NS, W - 1:W]
                    if not first(j):
                        v.wait_ge(hidden, c + 1 - NS)
                    v.tensor_tensor_scan(out=agg[:, s, :], data0=keep[:, s, :], data1=tm[:, :], initial=start,
                                                op0=ALU.mult, op1=ALU.add).then_inc(own_v, one(st))
                    v.wait_ge(own_v, steps(st))
                    v.sem_inc(summed, 1)

                def filt(c, j, s):
                    v.wait_ge(softened, c + 1)
                    if not first(j):
                        v.wait_ge(projected, c + 1 - NS)
                    v.scalar_tensor_tensor(out=fs[:, s, :], in0=sp_r[:, :], scalar=-LOG2, in1=sp_t[:, :],
                                                  op0=ALU.add, op1=ALU.add).then_inc(own_v, one(st))
                    v.wait_ge(own_v, steps(st))
                    v.sem_inc(filtered, 1)

                def norm(c, j, s):
                    v.wait_ge(projected, c + 1)
                    v.scalar_tensor_tensor(out=vv[:, :, :], in0=mr[:, s, :, F:2 * F], scalar=2.0,
                                                  in1=po[:, :].rearrange("p (g f) -> p g f", g=G),
                                                  op0=ALU.mult, op1=ALU.add).then_inc(own_v, one(st))
                    v.wait_ge(own_v, steps(st))
                    v.sem_inc(added, 1)
                    v.tensor_tensor(vv[:, :, :], vv[:, :, :], spread(env.bc["L1_gnn_b3"]), ALU.add).then_inc(own_v, one(st))
                    v.wait_ge(own_v, steps(st))
                    norm_stats(v, st, vv, stats, mv)
                    v.wait_ge(own_v, steps(st))
                    v.sem_inc(measured, 1)
                    v.wait_ge(rooted, c + 1)
                    if not first(j):
                        v.wait_ge(stored[s], 16 * j)
                    norm_apply(v, st, vv, mv, sd[:, :], xo[:, s, :, :])
                    v.wait_ge(own_v, steps(st))
                    v.sem_inc(normed, 1)
                pipeline(st, CH, NS, (2, norm), (1, filt), (0, scan))

            @block.scalar
            def _(act):
                st = Steps(act, own_a)

                def soft(c, j, s):
                    act.wait_ge(hidden, c + 1)
                    if not (first(j) and s == 0):
                        act.wait_ge(filtered, c)
                    soft_plus_scalar(act, st, ph[:, :], env.col["L1_gnn_b2"], sp_t[:, :], sp_r[:, :])
                    act.wait_ge(own_a, steps(st))
                    act.sem_inc(softened, 1)

                def root(c, j, s):
                    act.wait_ge(measured, c + 1)
                    act.activation(sd[:, :], mv[:, :, 1], ACT.Sqrt).then_inc(rooted, 1)
                pipeline(st, CH, NS, (2, root), (1, soft))

            @block.tensor
            def _(pe):
                def turn(c, j, s):
                    pe.wait_ge(filled[s], 32 * (j + 1))
                    if not (first(j) and s == 0):
                        pe.wait_ge(summed, c)
                    transpose4(pe, env, tm, mr[:, s, :, 0:F]).then_inc(turned, 1)

                def hide(c, j, s):
                    pe.wait_ge(summed, c + 1)
                    if not (first(j) and s == 0):
                        pe.wait_ge(softened, c)
                    pe.matmul(ph[:, :], env.w["L1_gnn_W2"], agg[:, s, :], start=True, stop=True).then_inc(hidden, 1)

                def project(c, j, s):
                    pe.wait_ge(filtered, c + 1)
                    if not (first(j) and s == 0):
                        pe.wait_ge(added, c)
                    to_rows4(pe, po, fs[:, s, :], env.w["L1_gnn_W3"]).then_inc(projected, 1)
                pipeline(Steps(pe, own), CH, NS, (2, project), (1, hide), (0, turn))


def edge_layer2(nc, env, D):
    with ExitStack() as ctx:
        m = Mem(nc, ctx, "e2")
        ix, fl, keep = m.sb("ix", NS, G * NIX, dt=i32), m.sb("fl", NS, G * NFL), m.sb("keep", NS, W)
        xs, xd, df = m.sb("xs", NS, G, F), m.sb("xd", NS, G, F), m.sb("df", NS, G, F)
        xt, dt_, pen, agg = m.sb("xt", NS, W), m.sb("dt", NS, W), m.sb("pen", NS, W), m.sb("agg", NS, W)
        ab, fin, am = m.sb("ab", W), m.sb("fin", W), m.sb("am", NS, W)
        vv, stats, mv, sd = m.sb("vv", 2 * G, F), m.sb("stats", 2 * G, 6), m.sb("mv", 2 * G, 2), m.sb("sd", 2 * G)
        mask, xo = m.sb("mask", 2 * G), m.sb("xo", NS, 2, G, F)
        ta, tb, pm, tr = (m.ps(n) for n in ("ta", "tb", "pm", "tr"))
        (filled, got, stored, differed, turned, copied_x, copied_d, mixed, scanned, maxed, returned, added,
         measured, rooted, normed, own_v, own_a, own) = m.sems(
            "filled* got* stored* differed turned copied_x copied_d mixed scanned maxed returned added measured rooted "
            "normed own_v own_a own")
        iv, fv, kv = views(D)
        with nc.Block() as block:
            @block.sync
            def _(sp):
                def load(c, j, s):
                    if not first(j):
                        sp.wait_ge(normed, c + 1 - NS)
                    sp.sem_inc(own, 1)
                    sp.dma_start(ix[:, s, :], iv[:, c, :]).then_inc(filled[s], 16)
                    sp.dma_start(fl[:, s, :], fv[:, c, :]).then_inc(filled[s], 16)
                    sp.dma_start(keep[:, s, :], kv[bass.ds(c, 1), :].broadcast_to([P, W])).then_inc(filled[s], 16)

                def store(c, j, s):
                    sp.wait_ge(normed, c + 1)
                    sp.sem_inc(own, 1)
                    sp.dma_start(rows4(D["x3"], c), xo[:, s, 0, :, :]).then_inc(stored[s], 16)
                    sp.dma_start(rows4(D["x3"], c + CH), xo[:, s, 1, :, :]).then_inc(stored[s], 16)
                pipeline(Steps(sp, own), CH, NS, (NS, store), (0, load))
                for s in range(NS):
                    sp.wait_ge(stored[s], 32 * uses(s))

            @block.gpsimd
            def _(pool):
                def gather(c, j, s):
                    pool.wait_ge(filled[s], 48 * (j + 1))
                    pool.sem_inc(own, 1)
                    gather4(pool, xs[:, s, :, :], D["x2"], ix[:, s, :], IX_SRC_S, got[s])
                    gather4(pool, xd[:, s, :, :], D["x2"], ix[:, s, :], IX_DST_S, got[s])
                pipeline(Steps(pool, own), CH, NS, (0, gather))

            @block.vector
            def _(v):
                st = Steps(v, own_v)

                def differ(c, j, s):
                    v.wait_ge(got[s], 128 * (j + 1))
                    v.tensor_tensor(df[:, s, :, :], xs[:, s, :, :], xd[:, s, :, :], ALU.subtract).then_inc(own_v, one(st))
                    v.tensor_scalar(pen[:, s, :], keep[:, s, :], -1.0, -NEG, ALU.add, ALU.mult).then_inc(own_v, one(st))
                    v.wait_ge(own_v, steps(st))
                    v.sem_inc(differed, 1)

                def copy(c, j, s):
                    v.wait_ge(turned, c + 1)
                    v.tensor_copy(dt_[:, s, :], tb[:, :]).then_inc(copied_d, 1)

                def scan(c, j, s):
                    v.wait_ge(mixed, c + 1)
                    start = NEG if first(j) and s == 0 else agg[:, (s - 1) % NS, W - 1:W]
                    v.tensor_tensor_scan(out=agg[:, s, :], data0=pen[:, s, :], data1=pm[:, :], initial=start,
                                                op0=ALU.add, op1=ALU.max).then_inc(own_v, one(st))
                    v.wait_ge(own_v, steps(st))
                    v.sem_inc(scanned, 1)
                    v.tensor_scalar(ab[:, :], agg[:, s, :], env.col["L2_gnn_b"], None, ALU.add).then_inc(own_v, one(st))
                    v.wait_ge(own_v, steps(st))
                    v.tensor_tensor(fin[:, :], ab[:, :], ab[:, :], ALU.subtract).then_inc(own_v, one(st))
                    if not first(j):
                        v.wait_ge(returned, c + 1 - NS)
                    v.memset(am[:, s, :], 0.0).then_inc(own_v, one(st))
                    v.wait_ge(own_v, steps(st))
                    v.tensor_scalar(fin[:, :], fin[:, :], 0.0, None, ALU.is_equal).then_inc(own_v, one(st))
                    v.wait_ge(own_v, steps(st))
                    v.sem_inc(own_v, one(st))
                    v.copy_predicated(am[:, s, :], fin[:, :].bitcast(i32), ab[:, :]).then_inc(own_v, one(st))
                    v.wait_ge(own_v, steps(st))
                    v.sem_inc(maxed, 1)

                def norm(c, j, s):
                    v.wait_ge(returned, c + 1)
                    v.tensor_tensor(vv[:, 0:G, :], tr[:, :].rearrange("p (g f) -> p g f", g=G),
                                           xd[:, s, :, :], ALU.add).then_inc(own_v, one(st))
                    v.wait_ge(own_v, steps(st))
                    v.sem_inc(added, 1)
                    v.tensor_copy(vv[:, G:2 * G, :], xs[:, s, :, :]).then_inc(own_v, one(st))
                    v.memset(mask[:, 0:G], 1.0).then_inc(own_v, one(st))
                    v.tensor_copy(mask[:, G:2 * G], fl[:, s, :].rearrange("p (g k) -> p g k", k=NFL)
                                         [:, :, FL_REAL]).then_inc(own_v, one(st))
                    v.wait_ge(own_v, steps(st))
                    norm_stats(v, st, vv, stats, mv)
                    v.wait_ge(own_v, steps(st))
                    v.sem_inc(measured, 1)
                    v.wait_ge(rooted, c + 1)
                    if not first(j):
                        v.wait_ge(stored[s], 32 * j)
                    norm_apply(v, st, vv, mv, sd[:, :], xo[:, s, :, :, :].rearrange("p k g f -> p (k g) f"),
                               mask[:, :])
                    v.wait_ge(own_v, steps(st))
                    v.sem_inc(normed, 1)
                pipeline(st, CH, NS, (2, norm), (1, scan), (0, differ), (0, copy))

            @block.scalar
            def _(act):
                st = Steps(act, own_a)

                def copy(c, j, s):
                    act.wait_ge(turned, c + 1)
                    act.activation(xt[:, s, :], ta[:, :], ACT.Copy).then_inc(copied_x, 1)

                def root(c, j, s):
                    act.wait_ge(measured, c + 1)
                    act.activation(sd[:, :], mv[:, :, 1], ACT.Sqrt).then_inc(rooted, 1)
                pipeline(st, CH, NS, (2, root), (0, copy))

            @block.tensor
            def _(pe):
                def turn(c, j, s):
                    pe.wait_ge(differed, c + 1)
                    if not (first(j) and s == 0):
                        pe.wait_ge(copied_x, c)
                        pe.wait_ge(copied_d, c)
                    transpose4(pe, env, ta, xd[:, s, :, :])
                    transpose4(pe, env, tb, df[:, s, :, :]).then_inc(turned, 1)

                def mix(c, j, s):
                    pe.wait_ge(copied_x, c + 1)
                    pe.wait_ge(copied_d, c + 1)
                    if not (first(j) and s == 0):
                        pe.wait_ge(scanned, c)
                    pe.matmul(pm[:, :], env.wi, xt[:, s, :], start=True, stop=False)
                    pe.matmul(pm[:, :], env.wj, dt_[:, s, :], start=False, stop=True).then_inc(mixed, 1)

                def back(c, j, s):
                    pe.wait_ge(maxed, c + 1)
                    if not (first(j) and s == 0):
                        pe.wait_ge(added, c)
                    for g in range(G):
                        last = pe.transpose(tr[:, g * F:(g + 1) * F], am[:, s, g * P:(g + 1) * P], env.ident[:, :])
                    last.then_inc(returned, 1)
                pipeline(Steps(pe, own), CH, NS, (2, back), (1, mix), (0, turn))


def parts_of(c):
    return TP if isinstance(c, int) and c == DC - 1 else P


def node_rows(ap, c):
    if isinstance(c, int) and c == DC - 1:
        return ap[c * W:N, :].rearrange("(p g) f -> p (g f)", g=G)
    return ap[bass.ds(c * W, W), :].rearrange("(p g) f -> p (g f)", g=G)


def columns(ap, c, wide=W, base=0):
    return ap[:, bass.ds(c * W + base, wide)]


def dense_front(nc, env, A, D):
    with ExitStack() as ctx:
        m = Mem(nc, ctx, "df")
        x, free = m.sb("x", NS, G, F), m.sb("free", NS, G)
        xt, hid, x1, vv, x3 = m.sb("xt", NS, W), m.sb("hid", NS, W), m.sb("x1", G, F), m.sb("vv", G, F), m.sb("x3", NS, G, F)
        x3t, h = m.sb("x3t", NS, W), m.sb("h", NS, W)
        va, stats, mv, sd = m.sb("va", G, F), m.sb("stats", G, 6), m.sb("mv", G, 2), m.sb("sd", G)
        stats2, mv2, sd2 = m.sb("stats2", G, 6), m.sb("mv2", G, 2), m.sb("sd2", G)
        tx, ph, po, tx3, pa = (m.ps(n) for n in ("tx", "ph", "po", "tx3", "pa"))
        (filled, stored, turned, copied, hidden, relued, projected, added, measured, rooted, first_done, measured2,
         rooted2, normed, turned3, copied3, mapped, biased, own_v, own_a, own) = m.sems(
            "filled* stored* turned copied hidden relued projected added measured rooted first_done measured2 rooted2 "
            "normed turned3 copied3 mapped biased own_v own_a own")
        freev = D["free"].rearrange("(c p g) -> c p g", c=DC, g=G)
        with nc.Block() as block:
            @block.sync
            def _(sp):
                def load(c, j, s):
                    n = parts_of(c)
                    if not first(j):
                        sp.wait_ge(normed, c + 1 - NS)
                        sp.sem_inc(own, 1)
                    sp.dma_start(x[0:n, s, :, :].rearrange("p g f -> p (g f)"), node_rows(A["x"], c))\
                        .then_inc(filled[s], 16)
                    sp.dma_start(free[0:n, s, :], freev[c, 0:n, :]).then_inc(filled[s], 16)

                def store(c, j, s):
                    n = parts_of(c)
                    sp.wait_ge(normed, c + 1)
                    sp.sem_inc(own, 1)
                    sp.dma_start(node_rows(D["x3n"], c), x3[0:n, s, :, :].rearrange("p g f -> p (g f)"))\
                        .then_inc(stored[s], 16)
                    sp.wait_ge(biased, c + 1)
                    sp.sem_inc(own, 1)
                    sp.dma_start(columns(D["za"], c, n * G), h[:, s, 0:n * G]).then_inc(stored[s], 16)
                pipeline(Steps(sp, own), DC, NS, (0, load), (NS, store))
                for s in range(NS):
                    sp.wait_ge(stored[s], 32 * uses(s, DC))

            @block.vector
            def _(v):
                st = Steps(v, own_v)

                def norm1(c, j, s):
                    n = parts_of(c)
                    v.wait_ge(projected, c + 1)
                    v.tensor_tensor(va[0:n, :, :], po[0:n, :].rearrange("p (g f) -> p g f", g=G),
                                           x[0:n, s, :, :], ALU.add).then_inc(own_v, one(st))
                    v.wait_ge(own_v, steps(st))
                    v.sem_inc(added, 1)
                    v.tensor_tensor(va[0:n, :, :], va[0:n, :, :], spread(env.bc["L0_gnn_b2"][0:n, :]), ALU.add).then_inc(own_v, one(st))
                    v.wait_ge(own_v, steps(st))
                    norm_stats(v, st, va[0:n], stats[0:n], mv[0:n])
                    v.wait_ge(own_v, steps(st))
                    v.sem_inc(measured, 1)
                    v.wait_ge(rooted, c + 1)
                    norm_apply(v, st, va[0:n], mv[0:n], sd[0:n, :], x1[0:n])
                    v.wait_ge(own_v, steps(st))
                    v.scalar_tensor_tensor(out=vv[0:n, :, :], in0=x1[0:n, :, :], scalar=2.0,
                                                  in1=spread(env.h0[0:n, :]), op0=ALU.mult, op1=ALU.add).then_inc(own_v, one(st))
                    v.wait_ge(own_v, steps(st))
                    norm_stats(v, st, vv[0:n], stats2[0:n], mv2[0:n], 1.0 + LN_EPS, LN_EPS * LN_EPS)
                    v.wait_ge(own_v, steps(st))
                    v.sem_inc(measured2, 1)
                    v.wait_ge(rooted2, c + 1)
                    if not first(j):
                        v.wait_ge(stored[s], 32 * j)
                    norm_apply(v, st, vv[0:n], mv2[0:n], sd2[0:n, :], x3[0:n, s, :, :], free[0:n, s, :])
                    v.wait_ge(own_v, steps(st))
                    v.sem_inc(normed, 1)

                def copy3(c, j, s):
                    n = parts_of(c) * G
                    v.wait_ge(turned3, c + 1)
                    if not first(j):
                        v.wait_ge(mapped, c + 1 - NS)
                    v.tensor_copy(x3t[:, s, 0:n], tx3[:, 0:n]).then_inc(copied3, 1)
                pipeline(st, DC, NS, (2, norm1), (3, copy3))

            @block.scalar
            def _(act):
                st = Steps(act, own_a)

                def copy(c, j, s):
                    n = parts_of(c) * G
                    act.wait_ge(turned, c + 1)
                    act.activation(xt[:, s, 0:n], tx[:, 0:n], ACT.Copy).then_inc(copied, 1)

                def relu(c, j, s):
                    n = parts_of(c) * G
                    act.wait_ge(hidden, c + 1)
                    act.activation(hid[:, s, 0:n], ph[:, 0:n], ACT.Relu, bias=env.col["L0_gnn_b1"]).then_inc(relued, 1)

                def root(c, j, s):
                    n = parts_of(c)
                    act.wait_ge(measured, c + 1)
                    act.activation(sd[0:n, :], mv[0:n, :, 1], ACT.Sqrt).then_inc(rooted, 1)

                def root2(c, j, s):
                    n = parts_of(c)
                    act.wait_ge(measured2, c + 1)
                    act.activation(sd2[0:n, :], mv2[0:n, :, 1], ACT.Sqrt).then_inc(rooted2, 1)

                def bias(c, j, s):
                    n = parts_of(c) * G
                    act.wait_ge(mapped, c + 1)
                    if not first(j):
                        act.wait_ge(stored[s], 32 * j)
                    act.activation(h[:, s, 0:n], pa[:, 0:n], ACT.Identity, bias=env.col["L3_gnn_b_atom"])\
                        .then_inc(biased, 1)
                pipeline(st, DC, NS, (2, root), (0, copy), (2, root2), (1, relu), (3, bias))

            @block.tensor
            def _(pe):
                def turn(c, j, s):
                    n = parts_of(c)
                    pe.wait_ge(filled[s], 32 * (j + 1))
                    if not (first(j) and s == 0):
                        pe.wait_ge(copied, c)
                    transpose4(pe, env, tx, x[0:n, s, :, :], n).then_inc(turned, 1)

                def hide(c, j, s):
                    n = parts_of(c) * G
                    pe.wait_ge(copied, c + 1)
                    if not (first(j) and s == 0):
                        pe.wait_ge(relued, c)
                    pe.matmul(ph[:, 0:n], env.w["L0_gnn_W1"], xt[:, s, 0:n], start=True, stop=True).then_inc(hidden, 1)

                def project(c, j, s):
                    n = parts_of(c)
                    pe.wait_ge(relued, c + 1)
                    if not (first(j) and s == 0):
                        pe.wait_ge(added, c)
                    to_rows4(pe, po, hid[:, s, :], env.w["L0_gnn_W2"], n).then_inc(projected, 1)

                def turn3(c, j, s):
                    n = parts_of(c)
                    pe.wait_ge(normed, c + 1)
                    if not (first(j) and s == 0):
                        pe.wait_ge(copied3, c)
                    transpose4(pe, env, tx3, x3[0:n, s, :, :], n).then_inc(turned3, 1)

                def atom(c, j, s):
                    n = parts_of(c) * G
                    pe.wait_ge(copied3, c + 1)
                    if not (first(j) and s == 0):
                        pe.wait_ge(biased, c)
                    pe.matmul(pa[:, 0:n], env.w["L3_gnn_W_atom"], x3t[:, s, 0:n], start=True, stop=True)\
                        .then_inc(mapped, 1)
                pipeline(Steps(pe, own), DC, NS, (3, turn3), (0, turn), (2, project), (1, hide), (3, atom))


def slot_states(nc, env, D):
    n3 = 3 * CH
    with ExitStack() as ctx:
        m = Mem(nc, ctx, "ss")
        x, xt, o, ot = m.sb("x", NS, G, F), m.sb("xt", NS, W), m.sb("o", NS, G, F), m.sb("ot", NS, W)
        tx, pr, pt = (m.ps(n) for n in ("tx", "pr", "pt"))
        filled, stored, turned, copied, mapped, rows_out, cols_out, own = m.sems(
            "filled* stored* turned copied mapped rows_out cols_out own")
        bcol = {0: env.col["L3_gnn_b_atom"], 2: env.col["L3_gnn_b_bond"]}
        wts = {0: env.w["L3_gnn_W_atom"], 1: env.w["L3_gnn_W_atom"], 2: env.w["L3_gnn_W_bond"]}

        def run(kind):
            source = D["x3"] if kind == 0 else D["edges"][:, 0:F]
            target = D["hd"] if kind == 0 else D["ea"]
            with nc.Block() as block:
                @block.sync
                def _(sp):
                    def load(c, j, s):
                        if not first(j):
                            sp.wait_ge(turned, base + c + 1 - NS)
                            sp.sem_inc(own, 1)
                        sp.dma_start(x[:, s, :, :], rows4(source, c)).then_inc(filled[s], 16)

                    def store(c, j, s):
                        sp.wait_ge(cols_out, base + c + 1)
                        sp.sem_inc(own, 1)
                        sp.dma_start(columns(target, c), ot[:, s, :]).then_inc(stored[s], 16)
                    pipeline(Steps(sp, own), count, NS, (0, load), (NS, store))
                    for s in range(NS):
                        sp.wait_ge(stored[s], 16 * (uses_before[s] + uses(s, count)))

                @block.scalar
                def _(act):
                    def copy(c, j, s):
                        act.wait_ge(turned, base + c + 1)
                        act.activation(xt[:, s, :], tx[:, :], ACT.Copy).then_inc(copied, 1)
                    pipeline(Steps(act, own), count, NS, (0, copy))

                @block.vector
                def _(v):
                    def bias(c, j, s):
                        v.wait_ge(mapped, base + c + 1)
                        if not first(j):
                            v.wait_ge(stored[s], 16 * (uses_before[s] + j))
                        v.tensor_scalar(ot[:, s, :], pt[:, :], bcol[kind], None, ALU.add).then_inc(cols_out, 1)
                    pipeline(Steps(v, own), count, NS, (1, bias))

                @block.tensor
                def _(pe):
                    def turn(c, j, s):
                        pe.wait_ge(filled[s], 16 * (uses_before[s] + j + 1))
                        if not (first(j) and s == 0):
                            pe.wait_ge(copied, base + c)
                        transpose4(pe, env, tx, x[:, s, :, :]).then_inc(turned, 1)

                    def apply(c, j, s):
                        pe.wait_ge(copied, base + c + 1)
                        if not (first(j) and s == 0):
                            pe.wait_ge(cols_out, base + c)
                        pe.matmul(pt[:, :], wts[kind], xt[:, s, :], start=True, stop=True).then_inc(mapped, 1)
                    pipeline(Steps(pe, own), count, NS, (0, turn), (1, apply))
        base, uses_before = 0, [0] * NS
        count = 2 * CH
        run(0)
        base += count
        uses_before = [uses(s, count) for s in range(NS)]
        count = CH
        run(2)


def rows_of_states(nc, env, D, tag, src, norm):
    with ExitStack() as ctx:
        m = Mem(nc, ctx, tag)
        z, h, r = m.sb("z", NS, W), m.sb("h", NS, W), m.sb("r", NS, G, F)
        tr = [m.ps("tr0"), m.ps("tr1")]
        filled, stored, made, turned, copied, own = m.sems("filled* stored* made turned copied own")
        count = 2 * CH
        hh = z if norm is None else h
        with nc.Block() as block:
            @block.sync
            def _(sp):
                def load(c, j, s):
                    if not first(j):
                        sp.wait_ge(copied, c + 1 - NS)
                        sp.sem_inc(own, 1)
                    sp.dma_start(z[:, s, :], src(c)).then_inc(filled[s], 16)

                def store(c, j, s):
                    sp.wait_ge(copied, c + 1)
                    sp.sem_inc(own, 1)
                    sp.dma_start(rows4(D["hr"], c), r[:, s, :, :]).then_inc(stored[s], 16)
                    if norm is not None:
                        sp.dma_start(columns(D["hd"], c), hh[:, s, :]).then_inc(stored[s], 16)
                pipeline(Steps(sp, own), count, NS, (0, load), (NS, store))
                for s in range(NS):
                    sp.wait_ge(stored[s], (16 if norm is None else 32) * uses(s, count))

            if norm is not None:
                @block.scalar
                def _(act):
                    def make(c, j, s):
                        act.wait_ge(filled[s], 16 * (j + 1))
                        if not first(j):
                            act.wait_ge(stored[s], 32 * j)
                        act.activation(h[:, s, :], z[:, s, :], ACT.Relu, scale=norm[0], bias=norm[1]).then_inc(made, 1)
                    pipeline(Steps(act, own), count, NS, (0, make))

            @block.tensor
            def _(pe):
                def turn(c, j, s):
                    if norm is None:
                        pe.wait_ge(filled[s], 16 * (j + 1))
                    else:
                        pe.wait_ge(made, c + 1)
                    if not (first(j) and s < 2):
                        pe.wait_ge(copied, c - 1)
                    for g in range(G):
                        last = pe.transpose(tr[s % 2][:, g * F:(g + 1) * F], hh[:, s, g * P:(g + 1) * P],
                                            env.ident[:, :])
                    last.then_inc(turned, 1)
                pipeline(Steps(pe, own), count, NS, (0, turn))

            @block.vector
            def _(v):
                def copy(c, j, s):
                    v.wait_ge(turned, c + 1)
                    if not first(j):
                        v.wait_ge(stored[s], (16 if norm is None else 32) * j)
                    v.tensor_copy(r[:, s, :, :], tr[s % 2][:, :].rearrange("p (g f) -> p g f", g=G))\
                        .then_inc(copied, 1)
                pipeline(Steps(v, own), count, NS, (0, copy))


def aggregate_states(nc, env, D, i, z):
    with ExitStack() as ctx:
        m = Mem(nc, ctx, f"ag{i}")
        ix, keep = m.sb("ix", NS, G * NIX, dt=i32), m.sb("keep", NS, W)
        hs, hd, ea = m.sb("hs", NS, G, F), m.sb("hd", NS, W), m.sb("ea", NS, W)
        ms, agg, zd, zs = m.sb("ms", NS, W), m.sb("agg", NS, W), m.sb("zd", NS, W), m.sb("zs", NS, W)
        ts = [m.ps("ts0"), m.ps("ts1")]
        filled, got, stored, turned, scaled, summed, relued, done, own_v, own = m.sems(
            "filled* got* stored* turned scaled summed relued done own_v own")
        iv, fv, kv = views(D)
        with nc.Block() as block:
            @block.sync
            def _(sp):
                def load(c, j, s):
                    if not first(j):
                        sp.wait_ge(done, c + 1 - NS)
                        sp.sem_inc(own, 1)
                    sp.dma_start(ix[:, s, :], iv[:, c, :]).then_inc(filled[s], 16)
                    sp.dma_start(keep[:, s, :], kv[bass.ds(c, 1), :].broadcast_to([P, W])).then_inc(filled[s], 16)
                    sp.dma_start(hd[:, s, :], columns(D["hd"], c)).then_inc(filled[s], 16)
                    sp.dma_start(ea[:, s, :], columns(D["ea"], c)).then_inc(filled[s], 16)

                def store(c, j, s):
                    sp.wait_ge(done, c + 1)
                    sp.sem_inc(own, 1)
                    sp.dma_start(columns(z, c, W, SLOT0), zd[:, s, :]).then_inc(stored[s], 16)
                    sp.dma_start(columns(z, c, W, SLOT0 + EP), zs[:, s, :]).then_inc(stored[s], 16)
                pipeline(Steps(sp, own), CH, NS, (0, load), (NS, store))
                for s in range(NS):
                    sp.wait_ge(stored[s], 32 * uses(s))

            @block.gpsimd
            def _(pool):
                def gather(c, j, s):
                    pool.wait_ge(filled[s], 64 * (j + 1))
                    pool.sem_inc(own, 1)
                    gather4(pool, hs[:, s, :, :], D["hr"], ix[:, s, :], IX_SRC_D, got[s])
                pipeline(Steps(pool, own), CH, NS, (0, gather))

            @block.tensor
            def _(pe):
                def turn(c, j, s):
                    pe.wait_ge(got[s], 64 * (j + 1))
                    if not (first(j) and s < 2):
                        pe.wait_ge(scaled, c - 1)
                    transpose4(pe, env, ts[s % 2], hs[:, s, :, :]).then_inc(turned, 1)
                pipeline(Steps(pe, own), CH, NS, (0, turn))

            @block.scalar
            def _(act):
                def relu(c, j, s):
                    act.wait_ge(summed, c + 1)
                    act.activation(ms[:, s, :], ms[:, s, :], ACT.Relu).then_inc(relued, 1)
                pipeline(Steps(act, own), CH, NS, (0, relu))

            @block.vector
            def _(v):
                st = Steps(v, own_v)

                def add(c, j, s):
                    v.wait_ge(turned, c + 1)
                    if not first(j):
                        v.wait_ge(stored[s], 32 * j)
                    v.tensor_tensor(ms[:, s, :], ts[s % 2][:, :], ea[:, s, :], ALU.add).then_inc(own_v, one(st))
                    v.wait_ge(own_v, steps(st))
                    v.sem_inc(summed, 1)
                    v.tensor_scalar(zs[:, s, :], ts[s % 2][:, :], env.onep[:, i:i + 1], None, ALU.mult).then_inc(own_v, one(st))
                    v.wait_ge(own_v, steps(st))
                    v.sem_inc(scaled, 1)

                def scan(c, j, s):
                    v.wait_ge(relued, c + 1)
                    start = 0.0 if first(j) and s == 0 else agg[:, (s - 1) % NS, W - 1:W]
                    v.tensor_tensor_scan(out=agg[:, s, :], data0=keep[:, s, :], data1=ms[:, s, :],
                                                initial=start, op0=ALU.mult, op1=ALU.add).then_inc(own_v, one(st))
                    v.wait_ge(own_v, steps(st))
                    v.scalar_tensor_tensor(out=zd[:, s, :], in0=hd[:, s, :], scalar=env.onep[:, i:i + 1],
                                                  in1=agg[:, s, :], op0=ALU.mult, op1=ALU.add).then_inc(own_v, one(st))
                    v.wait_ge(own_v, steps(st))
                    v.sem_inc(done, 1)
                pipeline(st, CH, NS, (0, add), (1, scan))


def norm_constants(nc, env, tag, halves, bias, gain, offset, nodes, slots, out):
    with ExitStack() as ctx:
        m = Mem(nc, ctx, tag)
        mv, t, sm = m.sb("mv", halves, 2), m.sb("t", 4, halves), m.sb("sm", halves, 2)
        measured, rooted, own = m.sems("measured rooted own")
        with nc.Block() as block:
            @block.vector
            def _(v):
                st = Steps(v, own)

                def do(ins):
                    ins.then_inc(own, one(st))
                    v.wait_ge(own, steps(st))
                for k in range(halves):
                    v.bn_aggr(mv[:, k, :], nodes[:, k, :, :]).then_inc(own, one(st))
                    v.reduce_sum(sm[:, k, 0:1], slots[:, k, :, 0], axis=mybir.AxisListType.X).then_inc(own, one(st))
                    v.reduce_sum(sm[:, k, 1:2], slots[:, k, :, 1], axis=mybir.AxisListType.X).then_inc(own, one(st))
                v.wait_ge(own, steps(st))
                do(v.tensor_scalar(sm[:, :, :], sm[:, :, :], 1.0 / N, None, ALU.mult))
                do(v.tensor_tensor(t[:, 0, :], mv[:, :, 0], mv[:, :, 0], ALU.mult))
                do(v.tensor_tensor(t[:, 0, :], t[:, 0, :], mv[:, :, 1], ALU.add))
                do(v.tensor_tensor(t[:, 0, :], t[:, 0, :], sm[:, :, 1], ALU.add))
                do(v.tensor_tensor(t[:, 1, :], mv[:, :, 0], sm[:, :, 0], ALU.add))
                do(v.tensor_tensor(t[:, 2, :], t[:, 1, :], t[:, 1, :], ALU.mult))
                do(v.tensor_tensor(t[:, 0, :], t[:, 0, :], t[:, 2, :], ALU.subtract))
                do(v.tensor_scalar(t[:, 0, :], t[:, 0, :], BN_EPS, None, ALU.add))
                v.wait_ge(own, steps(st))
                v.sem_inc(measured, 1)
                v.wait_ge(rooted, 1)
                do(v.reciprocal(t[:, 2, :], t[:, 3, :]))
                do(v.tensor_tensor(out[:, 0, 0:halves], t[:, 2, :], gain, ALU.mult))
                do(v.tensor_tensor(t[:, 1, :], t[:, 1, :], bias, ALU.add))
                do(v.tensor_tensor(t[:, 1, :], bias, t[:, 1, :], ALU.subtract))
                do(v.tensor_tensor(t[:, 1, :], t[:, 1, :], out[:, 0, 0:halves], ALU.mult))
                do(v.tensor_tensor(out[:, 1, 0:halves], t[:, 1, :], offset, ALU.add))

            @block.scalar
            def _(act):
                act.wait_ge(measured, 1)
                act.activation(t[:, 3, :], t[:, 0, :], ACT.Sqrt).then_inc(rooted, 1)


def column_pass(nc, env, D, i, which, slots, source, target, prev, norm1, stats):
    tag = f"p{which}{'s' if slots else 'n'}{i}"
    count = 2 * CH if slots else DC
    base = SLOT0 if slots else 0
    w1 = env.w1 if slots else env.w1e
    halves = 2 if which == "a" else 1
    with ExitStack() as ctx:
        m = Mem(nc, ctx, tag)
        z, wt = m.sb("z", NS, W), m.sb("wt", NS, W)
        h = m.sb("h", NS, W) if prev is not None else z
        y, z2, scr = m.sb("y", NS, 2, W), m.sb("z2", NS, W), m.sb("scr", 2, W)
        p1 = [[m.ps(f"p1{a}{b}") for b in range(2)] for a in range(2)]
        p2 = [m.ps(f"p2{a}") for a in range(2)]
        filled, stored, made, multiplied, relued, projected, done, own_v, own_a, own = m.sems(
            "filled* stored* made multiplied relued projected done own_v own_a own")

        def wide(c):
            return W if slots else parts_of(c) * G
        loads = 32 if slots else 16
        with nc.Block() as block:
            @block.sync
            def _(sp):
                def load(c, j, s):
                    if not first(j):
                        sp.wait_ge(done, c + 1 - NS)
                        sp.sem_inc(own, 1)
                    sp.dma_start(z[:, s, 0:wide(c)], columns(source, c, wide(c), base)).then_inc(filled[s], 16)
                    if slots:
                        sp.dma_start(wt[:, s, :], D["weights"].rearrange("(c w) -> c w", w=W)[bass.ds(c, 1), :]
                                     .broadcast_to([P, W])).then_inc(filled[s], 16)

                def store(c, j, s):
                    sp.wait_ge(done, c + 1)
                    sp.sem_inc(own, 1)
                    sp.dma_start(columns(target, c, wide(c), base), z2[:, s, 0:wide(c)]).then_inc(stored[s], 16)
                if which == "a":
                    pipeline(Steps(sp, own), count, NS, (0, load))
                else:
                    pipeline(Steps(sp, own), count, NS, (0, load), (NS, store))
                    for s in range(NS):
                        sp.wait_ge(stored[s], 16 * uses(s, count))

            @block.scalar
            def _(act):
                st = Steps(act, own_a)

                def make(c, j, s):
                    act.wait_ge(filled[s], loads * (j + 1))
                    if not first(j):
                        act.wait_ge(multiplied, c + 1 - NS)
                    act.activation(h[:, s, 0:wide(c)], z[:, s, 0:wide(c)], ACT.Relu, scale=prev[0], bias=prev[1])\
                        .then_inc(made, 1)

                def relu(c, j, s):
                    n = wide(c)
                    act.wait_ge(multiplied, c + 1)
                    if not first(j):
                        act.wait_ge(projected, c + 1 - NS)
                    for k in range(2):
                        act.activation(y[:, s, k, 0:n], p1[s % 2][k][:, 0:n], ACT.Relu,
                                              scale=norm1[:, 0, k:k + 1], bias=norm1[:, 1, k:k + 1]).then_inc(own_a, one(st))
                    act.wait_ge(own_a, steps(st))
                    act.sem_inc(relued, 1)
                stages = []
                if prev is not None:
                    stages.append((0, make))
                if which == "b":
                    stages.append((1, relu))
                if stages:
                    pipeline(st, count, NS, *stages)

            @block.tensor
            def _(pe):
                def multiply(c, j, s):
                    n = wide(c)
                    if prev is None:
                        pe.wait_ge(filled[s], loads * (j + 1))
                    else:
                        pe.wait_ge(made, c + 1)
                    if not (first(j) and s < 2):
                        pe.wait_ge(done if which == "a" else relued, c - 1)
                    for k in range(2):
                        last = pe.matmul(p1[s % 2][k][:, 0:n], w1[:, i, k * F:(k + 1) * F], h[:, s, 0:n],
                                         start=True, stop=True)
                    last.then_inc(multiplied, 1)

                def project(c, j, s):
                    n = wide(c)
                    pe.wait_ge(relued, c + 1)
                    if not (first(j) and s < 2):
                        pe.wait_ge(done, c - 1)
                    for k in range(2):
                        last = pe.matmul(p2[s % 2][:, 0:n], env.w2[:, i, k, :], y[:, s, k, 0:n],
                                         start=k == 0, stop=k == 1)
                    last.then_inc(projected, 1)
                if which == "a":
                    pipeline(Steps(pe, own), count, NS, (0, multiply))
                else:
                    pipeline(Steps(pe, own), count, NS, (0, multiply), (1, project))

            @block.vector
            def _(v):
                st = Steps(v, own_v)

                def measure(c, j, s):
                    n = wide(c)
                    v.wait_ge(multiplied if which == "a" else projected, c + 1)
                    if which == "b" and not first(j):
                        v.wait_ge(stored[s], 16 * j)
                    for k in range(halves):
                        p = p1[s % 2][k] if which == "a" else p2[s % 2]
                        if slots:
                            v.wait_ge(filled[s], loads * (j + 1))
                            v.scalar_tensor_tensor(out=scr[:, k, :], in0=p[:, :], scalar=1.0, in1=wt[:, s, :],
                                                          op0=ALU.mult, op1=ALU.mult,
                                                          accum_out=stats[:, k, c, 0:1]).then_inc(own_v, one(st))
                            v.wait_ge(own_v, steps(st))
                            v.scalar_tensor_tensor(out=scr[:, k, :], in0=p[:, :], scalar=1.0, in1=scr[:, k, :],
                                                          op0=ALU.mult, op1=ALU.mult,
                                                          accum_out=stats[:, k, c, 1:2]).then_inc(own_v, one(st))
                        else:
                            v.bn_stats(stats[:, k, c, :], p[:, 0:n]).then_inc(own_v, one(st))
                    if which == "b":
                        v.tensor_copy(z2[:, s, 0:n], p2[s % 2][:, 0:n]).then_inc(own_v, one(st))
                    v.wait_ge(own_v, steps(st))
                    v.sem_inc(done, 1)
                pipeline(st, count, NS, (0 if which == "a" else 1, measure))


def results(nc, env, D, out, slots, source, norm):
    tag = "rs" if slots else "rn"
    count = 2 * CH if slots else DC
    base = SLOT0 if slots else 0
    with ExitStack() as ctx:
        m = Mem(nc, ctx, tag)
        z, h, x3, ix = m.sb("z", NS, W), m.sb("h", NS, W), m.sb("x3", NS, G, F), m.sb("ix", NS, G * NIX, dt=i32)
        vv, stats, mv, sd, xo = m.sb("vv", 2, G, F), m.sb("stats", 2, G, 6), m.sb("mv", 2, G, 2), m.sb("sd", 2, G), m.sb("xo", NS, G, F)
        po = [m.ps("po0"), m.ps("po1")]
        filled, stored, made, projected, added, measured, rooted, normed, own_v, own_a, own = m.sems(
            "filled* stored* made projected added measured rooted normed own_v own_a own")
        iv, fv, kv = views(D)
        loads = 48 if slots else 32

        def wide(c):
            return W if slots else parts_of(c) * G
        with nc.Block() as block:
            @block.sync
            def _(sp):
                def load(c, j, s):
                    n = wide(c)
                    if not first(j):
                        sp.wait_ge(added, c + 1 - NS)
                        sp.sem_inc(own, 1)
                        if slots:
                            sp.wait_ge(stored[s], 64 * j)
                            sp.sem_inc(own, 1)
                    sp.dma_start(z[:, s, 0:n], columns(source, c, n, base)).then_inc(filled[s], 16)
                    if slots:
                        sp.dma_start(x3[:, s, :, :], rows4(D["x3"], c)).then_inc(filled[s], 16)
                        sp.dma_start(ix[:, s, :], D["index2"].rearrange("p (c k) -> p c k", c=2 * CH)[:, c, :])\
                            .then_inc(filled[s], 16)
                    else:
                        p_ = parts_of(c)
                        sp.dma_start(x3[0:p_, s, :, :].rearrange("p g f -> p (g f)"), node_rows(D["x3n"], c))\
                            .then_inc(filled[s], 16)

                def store(c, j, s):
                    p_ = parts_of(c)
                    sp.wait_ge(normed, c + 1)
                    sp.sem_inc(own, 1)
                    sp.dma_start(node_rows(out, c), xo[0:p_, s, :, :].rearrange("p g f -> p (g f)"))\
                        .then_inc(stored[s], 16)
                if slots:
                    pipeline(Steps(sp, own), count, NS, (0, load))
                else:
                    pipeline(Steps(sp, own), count, NS, (0, load), (NS, store))
                    for s in range(NS):
                        sp.wait_ge(stored[s], 16 * uses(s, count))

            if slots:
                @block.gpsimd
                def _(pool):
                    def scatter(c, j, s):
                        pool.wait_ge(normed, c + 1)
                        pool.sem_inc(own, 1)
                        for g in range(G):
                            pool.indirect_dma_start(
                                out=out, out_offset=bass.IndirectOffsetOnAxis(ap=ix[:, s, g * NIX:g * NIX + 1], axis=0),
                                in_=xo[:, s, g, :], in_offset=None, bounds_check=N - 1, oob_is_err=False)\
                                .then_inc(stored[s], 16)
                    pipeline(Steps(pool, own), count, NS, (0, scatter))
                    for s in range(NS):
                        pool.wait_ge(stored[s], 64 * uses(s, count))

            @block.scalar
            def _(act):
                def make(c, j, s):
                    n = wide(c)
                    act.wait_ge(filled[s], loads * (j + 1))
                    if not first(j):
                        act.wait_ge(projected, c + 1 - NS)
                    act.activation(h[:, s, 0:n], z[:, s, 0:n], ACT.Relu, scale=norm[0], bias=norm[1]).then_inc(made, 1)

                def root(c, j, s):
                    n = P if slots else parts_of(c)
                    act.wait_ge(measured, c + 1)
                    act.activation(sd[0:n, s % 2, :], mv[0:n, s % 2, :, 1], ACT.Sqrt).then_inc(rooted, 1)
                pipeline(Steps(act, own_a), count, NS, (0, make), (1, root))

            @block.tensor
            def _(pe):
                def project(c, j, s):
                    n = P if slots else parts_of(c)
                    pe.wait_ge(made, c + 1)
                    if not (first(j) and s < 2):
                        pe.wait_ge(added, c - 1)
                    to_rows4(pe, po[s % 2], h[:, s, :], env.w["L3_gnn_W_out"], n).then_inc(projected, 1)
                pipeline(Steps(pe, own), count, NS, (0, project))

            @block.vector
            def _(v):
                st = Steps(v, own_v)

                def measure(c, j, s):
                    n = P if slots else parts_of(c)
                    b = s % 2
                    v.wait_ge(projected, c + 1)
                    v.tensor_tensor(vv[0:n, b, :, :], po[b][0:n, :].rearrange("p (g f) -> p g f", g=G),
                                           x3[0:n, s, :, :], ALU.add).then_inc(own_v, one(st))
                    v.wait_ge(own_v, steps(st))
                    v.sem_inc(added, 1)
                    v.tensor_tensor(vv[0:n, b, :, :], vv[0:n, b, :, :], spread(env.bc["L3_gnn_b_out"][0:n, :]),
                                           ALU.add).then_inc(own_v, one(st))
                    v.wait_ge(own_v, steps(st))
                    norm_stats(v, st, vv[0:n, b], stats[0:n, b], mv[0:n, b])
                    v.wait_ge(own_v, steps(st))
                    v.sem_inc(measured, 1)

                def apply(c, j, s):
                    n = P if slots else parts_of(c)
                    b = s % 2
                    v.wait_ge(rooted, c + 1)
                    if not first(j):
                        v.wait_ge(stored[s], (64 if slots else 16) * j)
                    norm_apply(v, st, vv[0:n, b], mv[0:n, b], sd[0:n, b, :], xo[0:n, s, :, :])
                    v.wait_ge(own_v, steps(st))
                    v.sem_inc(normed, 1)
                pipeline(st, count, NS, (0, measure), (1, apply))


def program(nc, A, out, D):
    env = Env()
    with ExitStack() as ctx:
        env.ctx = ctx
        constants(nc, env, A)
        with nc.sbuf_tensor("tabs", [P, 6, W], fp32) as tabs:
            def load_edges(sp, keys, extra, ec, loaded):
                for dst, src in ((keys[:, 0, :], A["dst"]), (keys[:, 1, :], A["src"]),
                                 (extra[:, 2, :], A["edge_weight"])):
                    sp.dma_start(dst[0:FULL, :], src[0:FULL * P].rearrange("(t p) -> t p", p=P))\
                        .then_inc(loaded, 16)
                    sp.dma_start(dst[FULL:FULL + 1, 0:REST],
                                 src[FULL * P:E].rearrange("(t p) -> t p", t=1)).then_inc(loaded, 16)
                return 6

            def load_permuted(sp, keys, extra, ec, loaded):
                sp.dma_start(ec[:, :, :], D["edges"].rearrange("(t p) f -> t p f", p=P)[:, :, F:ROW])\
                    .then_inc(loaded, 16)
                return 1
            rows = (D["row_key"], D["row_high"])
            env.key_loads = 6
            key_meta(nc, env, "d", load_edges, rows, D["meta"], D["cols"])
            rank_edges(nc, env, "d", rows, D["meta"], D["rank_d"], tabs[:, 0, :], tabs[:, 1, :], tabs[:, 2, :])
            scatter_edges(nc, env, A, D)
            env.key_loads = 1
            key_meta(nc, env, "s", load_permuted, rows, D["meta"], D["cols_s"], permuted=True)
            rank_edges(nc, env, "s", rows, D["meta"], D["rank_s"], tabs[:, 3, :], tabs[:, 4, :], tabs[:, 5, :])
            node_tables(nc, env, D, tabs)
        node_bounds(nc, env, D)
        slot_indices(nc, env, D)
        edge_layer0(nc, env, A, D)
        edge_layer1(nc, env, D)
        keep_rows(nc, env, D)
        source_layer1(nc, env, D)
        edge_layer2(nc, env, D)
        dense_front(nc, env, A, D)
        slot_states(nc, env, D)
        rows_of_states(nc, env, D, "r0", lambda c: columns(D["hd"], c), None)

        def stat(name, *shape):
            return ctx.enter_context(nc.sbuf_tensor(name, [P, *shape], fp32))
        node_stats, slot_sums = stat("node_stats", 2, DC, 6), stat("slot_sums", 2, 2 * CH, 2)
        norm1, norm2 = stat("norm1", 2, 2), stat("norm2", 2, 1)
        source, prev = D["za"], None
        for i in range(LAYERS):
            aggregate_states(nc, env, D, i, source)
            target = D["zb"] if source is D["za"] else D["za"]
            column_pass(nc, env, D, i, "a", False, source, None, prev, None, node_stats)
            column_pass(nc, env, D, i, "a", True, source, None, None, None, slot_sums)
            b2i = slice(2 * i, 2 * i + 2)
            norm_constants(nc, env, f"c1{i}", 2, env.col["L3_gnn_b1"][:, b2i], env.col["L3_gnn_g1"][:, b2i],
                           env.col["L3_gnn_be1"][:, b2i], node_stats, slot_sums, norm1)
            column_pass(nc, env, D, i, "b", False, source, target, prev, norm1, node_stats)
            column_pass(nc, env, D, i, "b", True, source, target, None, norm1, slot_sums)
            norm_constants(nc, env, f"c2{i}", 1, env.col["L3_gnn_b2"][:, i:i + 1], env.col["L3_gnn_gn"][:, i:i + 1],
                           env.col["L3_gnn_bet"][:, i:i + 1], node_stats, slot_sums, norm2)
            source, prev = target, (norm2[:, 0, :], norm2[:, 1, :])
            if i < LAYERS - 1:
                rows_of_states(nc, env, D, f"r{i + 1}", lambda c: columns(source, c, W, SLOT0), prev)
        results(nc, env, D, out, False, source, prev)
        results(nc, env, D, out, True, source, prev)


_INS = ["x", "src", "dst", "edge_attr_128", "edge_weight", "L0_gnn_W1", "L0_gnn_b1", "L0_gnn_W2", "L0_gnn_b2",
        "L1_gnn_Wn", "L1_gnn_We1", "L1_gnn_be1", "L1_gnn_We2", "L1_gnn_be2", "L1_gnn_W2", "L1_gnn_b2", "L1_gnn_W3",
        "L1_gnn_b3", "L2_gnn_W", "L2_gnn_b", "L3_gnn_W_atom", "L3_gnn_b_atom", "L3_gnn_W_bond", "L3_gnn_b_bond",
        "L3_gnn_eps", "L3_gnn_W1", "L3_gnn_b1", "L3_gnn_g1", "L3_gnn_be1", "L3_gnn_W2", "L3_gnn_b2", "L3_gnn_gn",
        "L3_gnn_bet", "L3_gnn_W_out", "L3_gnn_b_out"]
_SCRATCH = {
    "row_key": ((EP,), fp32), "row_high": ((EP,), fp32), "meta": ((P, T * 4), fp32), "cols": ((P, T * 4), fp32),
    "rank_d": ((P, T), i32), "rank_s": ((P, T), i32), "cols_s": ((P, T * 4), fp32), "edges": ((EP, ROW), fp32),
    "bounds": ((HI * W, 4), i32), "free": ((HI * W,), fp32), "keys_i": ((P, 2 * T), i32),
    "edge_bounds": ((P, T * 2 * 4), i32), "keep_d": ((EP,), fp32), "weights": ((2 * EP,), fp32),
    "x3n": ((N, F), fp32), "za": ((F, ZW), fp32), "zb": ((F, ZW), fp32), "hd": ((F, 2 * EP), fp32),
    "ea": ((F, EP), fp32), "hr": ((2 * EP, F), fp32), "index2": ((P, 2 * T * NIX), i32),
    "x1": ((2 * EP, F), fp32), "x2": ((2 * EP, F), fp32), "x3": ((2 * EP, F), fp32),
    "message": ((EP, MROW), fp32), "keep_s": ((EP,), fp32),
    "index": ((P, T * NIX), i32), "factor": ((P, T * NFL), fp32),
}


def kernel(**inputs):
    import numpy as _np
    import concourse.bacc as _bacc
    from concourse import mybir as _mybir
    from concourse.bass_utils import run_bass_kernel_spmd as _run

    nc = _bacc.Bacc("TRN2", target_bir_lowering=False, num_devices=1)
    arrays, args = {}, {}
    for name in _INS:
        a = _np.ascontiguousarray(inputs[name])
        arrays[f"in_{name}"] = a
        args[name] = nc.dram_tensor(f"in_{name}", a.shape, _mybir.dt.from_np(a.dtype), kind="ExternalInput").ap()
    out = nc.dram_tensor("out", (N, F), fp32, kind="ExternalOutput").ap()
    scratch = {n: nc.dram_tensor(f"scratch_{n}", s, dt, kind=SCRATCH_KIND).ap() for n, (s, dt) in _SCRATCH.items()}
    program(nc, args, out, scratch)
    r = _run(nc, [arrays], core_ids=[0])
    return r.results[0]["out"]


SCRATCH_KIND = "Internal"
```

```python
import concourse.bass as bass
from concourse import mybir
from contextlib import ExitStack, contextmanager

fp32 = mybir.dt.float32
bf16 = mybir.dt.bfloat16
i32 = mybir.dt.int32
ALU = mybir.AluOpType
ACT = mybir.ActivationFunctionType

P = 128
F = 128
G = 4
W = G * P
N = 50000
E = 12500
PAIRS = -(-E // (2 * W))
CH = 2 * PAIRS
T = CH * G
EP = CH * W
FULL = E // P
REST = E - FULL * P
NS = 4
HI = -(-N // W)
DC = HI
DPAIRS = (DC - 1) // 2
TP = (N - (DC - 1) * W) // G
SLOT0 = DC * W
ZW = SLOT0 + 2 * EP
FAR = 1 << 20
LOG2 = 0.6931471824645996
LN_EPS = 1e-05
BN_EPS = 1e-05
LAYERS = 3
NEG = -3.0e38
MAXF = 3.4028234663852886e38


@contextmanager
def phase(nc, tag, names):
    sems, every = [], []
    for n in names.split():
        got = [nc.alloc_semaphore(f"{tag}_{n.rstrip('*')}{k}") for k in range(NS if n[-1] == "*" else 1)]
        every += got
        sems.append(got if n[-1] == "*" else got[0])
    yield sems
    nc.clear_and_free_semaphores(every)
    nc.all_engine_barrier()


class Steps:

    def __init__(self, eng, sem):
        self.eng, self.sem, self.base, self.n = eng, sem, 0, 0

    def loop(self, count, body):
        first = self.base + self.n
        body(0)
        per = self.base + self.n - first
        with self.eng.Fori(1, count) as j:
            self.base, self.n = first + j * per, 0
            body(j)
        self.base, self.n = first + count * per, 0


def one(st):
    st.n += 1
    return 1


def steps(st):
    return st.base + st.n


def pipeline(st, chunks, slots, *stages):
    most = max(lag for lag, _ in stages)

    def group(k):
        for h in range(slots):
            for lag, fn in stages:
                turn, slot = k + (h - lag) // slots, (h - lag) % slots
                chunk = slots * turn + slot
                if isinstance(k, int) and not 0 <= chunk < chunks:
                    continue
                fn(chunk, turn, slot)
    even, last = -(-most // slots), (chunks - 1) // slots
    for k in range(even):
        group(k)
    begun = st.base + st.n
    group(even)
    per = st.base + st.n - begun
    with st.eng.Fori(even + 1, last) as k:
        st.base, st.n = begun + (k - even) * per, 0
        group(k)
    st.base, st.n = begun + (last - even) * per, 0
    for k in range(last, (chunks - 1 + most) // slots + 1):
        group(k)


def first(j):
    return isinstance(j, int) and j == 0


class Env:
    pass


def constants(nc, env, A):
    ctx = env.ctx

    def sb(name, shape, dt=fp32):
        return ctx.enter_context(nc.sbuf_tensor(name, shape, dt))

    mats = ["L0_gnn_W1", "L0_gnn_W2", "L1_gnn_Wn", "L1_gnn_We1", "L1_gnn_We2", "L1_gnn_W2", "L1_gnn_W3",
            "L3_gnn_W_atom", "L3_gnn_W_bond", "L3_gnn_W_out"]
    wts = sb("wts", [P, len(mats), F])
    env.w = {m: wts[:, k, :] for k, m in enumerate(mats)}
    w1 = sb("l3_w1", [P, LAYERS, 2 * F])
    w1e = sb("l3_w1e", [P, LAYERS, 2 * F])
    w2 = sb("l3_w2", [P, LAYERS, 2, F])
    env.w1, env.w1e, env.w2 = w1, w1e, w2
    l2w = sb("l2_w", [P, 2, F])
    l2t = sb("l2_t", [P, 2, F])
    env.wi, env.wj = l2t[:, 0, :], l2t[:, 1, :]
    vecs = [("L0_gnn_b1", 1), ("L1_gnn_be1", 1), ("L1_gnn_b2", 1), ("L2_gnn_b", 1), ("L3_gnn_b_atom", 1),
            ("L3_gnn_b_bond", 1), ("L3_gnn_b1", 6), ("L3_gnn_g1", 6), ("L3_gnn_be1", 6), ("L3_gnn_b2", 3),
            ("L3_gnn_gn", 3), ("L3_gnn_bet", 3)]
    rows = sum(n for _, n in vecs)
    vrow = sb("vrow", [rows, F])
    vcol = sb("vcol", [P, rows])
    env.col, at = {}, 0
    for name, n in vecs:
        env.col[name] = vcol[:, at:at + n]
        at += n
    bcs = ["L0_gnn_b2", "L1_gnn_be2", "L1_gnn_b3", "L3_gnn_b_out"]
    bc = sb("bias_rows", [P, len(bcs) + 1, F])
    env.bc = {b: bc[:, k, :] for k, b in enumerate(bcs)}
    env.h0 = bc[:, len(bcs), :]
    epsb = sb("epsb", [P, LAYERS])
    env.onep = sb("onep", [P, LAYERS])
    env.ident = sb("ident", [P, P])
    env.earlier = sb("earlier", [P, P])
    env.below = sb("below", [P, P])
    env.iota = sb("iota_free", [P, W])
    env.iotap = sb("iota_part", [P, 1])
    env.ones = sb("ones", [P, W])
    env.eps = sb("eps", [P, 3])
    sp2 = sb("sp2", [P, 4])
    spb = sb("spb", [P, F])
    with phase(nc, "const", "loaded made transposed turned h_in h_mm own_v own_p own_a soft") as (
            loaded, made, transposed, turned, h_in, h_mm, own_v, own_p, own_a, soft):
        with nc.psum_tensor("tp", [P, 512], fp32) as tp, nc.Block() as block:
            loads = []
            for m in mats:
                loads.append((env.w[m], A[m]))
            loads.append((w1[:, :, :], A["L3_gnn_W1"].rearrange("l k n -> k l n")))
            for i in range(LAYERS):
                loads.append((w2[:, i, :, :], A["L3_gnn_W2"][i].rearrange("(h k) n -> k h n", h=2)))
            loads.append((l2w[:, :, :], A["L2_gnn_W"].rearrange("f (h k) -> f h k", h=2)))
            at = 0
            for name, n in vecs:
                src = A[name]
                if n == 1:
                    src = src.rearrange("(a f) -> a f", a=1)
                elif n == 6:
                    src = src.rearrange("l (h f) -> (l h) f", h=2)
                loads.append((vrow[at:at + n, :], src))
                at += n
            for b in bcs:
                loads.append((env.bc[b], A[b].rearrange("(a f) -> a f", a=1).broadcast_to([P, F])))
            loads.append((epsb[:, :], A["L3_gnn_eps"].rearrange("(a f) -> a f", a=1).broadcast_to([P, LAYERS])))

            @block.sync
            def _(sp):
                for dst, src in loads:
                    sp.dma_start(dst, src).then_inc(loaded, 16)

            @block.gpsimd
            def _(pool):
                st = Steps(pool, own_p)
                pool.memset(env.ident[:, :], 0.0).then_inc(own_p, one(st))
                pool.memset(env.earlier[:, :], 1.0).then_inc(own_p, one(st))
                pool.memset(env.below[:, :], 1.0).then_inc(own_p, one(st))
                pool.memset(env.ones[:, :], 1.0).then_inc(own_p, one(st))
                pool.wait_ge(own_p, steps(st))
                pool.affine_select(out=env.ident[:, :], in_=env.ident[:, :], compare_op=ALU.not_equal,
                                          fill=1.0, base=0, pattern=[[-1, P]], channel_multiplier=1).then_inc(own_p, one(st))
                pool.affine_select(out=env.earlier[:, :], in_=env.earlier[:, :], compare_op=ALU.is_gt,
                                          fill=0.0, base=0, pattern=[[-1, P]], channel_multiplier=1).then_inc(own_p, one(st))
                pool.affine_select(out=env.below[:, :], in_=env.below[:, :], compare_op=ALU.is_gt,
                                          fill=0.0, base=0, pattern=[[1, P]], channel_multiplier=-1).then_inc(own_p, one(st))
                pool.iota(env.iota[:, :], pattern=[[1, W]], base=0, channel_multiplier=0,
                                 allow_small_or_imprecise_dtypes=True).then_inc(own_p, one(st))
                pool.iota(env.iotap[:, :], pattern=[[0, 1]], base=0, channel_multiplier=1,
                                 allow_small_or_imprecise_dtypes=True).then_inc(own_p, one(st))
                pool.wait_ge(own_p, steps(st))
                pool.sem_inc(made, 1)

            @block.tensor
            def _(pe):
                pe.wait_ge(loaded, 16 * len(loads))
                pe.wait_ge(made, 1)
                pe.transpose(tp[:, 0:rows], vrow[:, :], env.ident[0:rows, 0:rows])
                pe.transpose(tp[:, 128:256], l2w[:, 0, :], env.ident[:, :])
                pe.transpose(tp[:, 256:384], l2w[:, 1, :], env.ident[:, :]).then_inc(transposed, 1)
                pe.wait_ge(h_in, 1)
                pe.matmul(tp[:, 384:512], spb[:, :], env.w["L1_gnn_W3"], start=True, stop=True).then_inc(h_mm, 1)

            @block.scalar
            def _(act):
                st = Steps(act, own_a)
                act.wait_ge(turned, 1)
                act.activation(sp2[:, 0:1], env.col["L1_gnn_b2"], ACT.Abs).then_inc(own_a, one(st))
                act.wait_ge(own_a, steps(st))
                act.activation(sp2[:, 0:1], sp2[:, 0:1], ACT.Exp, scale=-1.0).then_inc(own_a, one(st))
                act.wait_ge(own_a, steps(st))
                act.activation(sp2[:, 1:2], sp2[:, 0:1], ACT.Ln, bias=1.0).then_inc(soft, 1)

            @block.vector
            def _(v):
                st = Steps(v, own_v)
                v.memset(env.eps[:, 0:1], 0.25 * LN_EPS).then_inc(own_v, one(st))
                v.memset(env.eps[:, 2:3], LN_EPS).then_inc(own_v, one(st))
                v.memset(env.eps[:, 1:2], LN_EPS * LN_EPS).then_inc(own_v, one(st))
                v.wait_ge(transposed, 1)
                v.tensor_copy(vcol[:, :], tp[:, 0:rows]).then_inc(own_v, one(st))
                v.tensor_copy(l2t[:, :, :], tp[:, 128:384].rearrange("p (h k) -> p h k", h=2)).then_inc(own_v, one(st))
                v.tensor_scalar(env.onep[:, :], epsb[:, :], 1.0, None, ALU.add).then_inc(own_v, one(st))
                v.wait_ge(own_v, steps(st))
                for i in range(LAYERS):
                    v.tensor_scalar(w1e[:, i, :], w1[:, i, :], env.onep[:, i:i + 1], None, ALU.mult).then_inc(own_v, one(st))
                v.wait_ge(own_v, steps(st))
                v.sem_inc(turned, 1)
                v.tensor_scalar(sp2[:, 2:3], env.col["L1_gnn_b2"], 0.0, -LOG2, ALU.max, ALU.add).then_inc(own_v, one(st))
                v.wait_ge(soft, 1)
                v.wait_ge(own_v, steps(st))
                v.tensor_tensor(sp2[:, 3:4], sp2[:, 1:2], sp2[:, 2:3], ALU.add).then_inc(own_v, one(st))
                v.wait_ge(own_v, steps(st))
                v.tensor_scalar(spb[:, :], env.ones[:, 0:F], sp2[:, 3:4], None, ALU.mult).then_inc(h_in, 1)
                v.wait_ge(h_mm, 1)
                v.tensor_tensor(env.h0, tp[:, 384:512], env.bc["L1_gnn_b3"], ALU.add)



def key_meta(nc, env, tag, load, rows, meta, cols, permuted=False):
    with ExitStack() as ctx:
        def sb(name, shape, dt=fp32):
            return ctx.enter_context(nc.sbuf_tensor(f"{tag}_{name}", shape, dt))
        extra_i = sb("extra_i", [T, 2, P], i32)
        extra = sb("extra", [T, 4, P])
        ec = sb("ec", [T, P, 4])
        part = sb("part", [T, 2, P], i32)
        kf = sb("kf", [T, 3, P])
        mt = sb("mt", [P, T, 4])
        ct = sb("ct", [P, T, 4])
        ps = [ctx.enter_context(nc.psum_tensor(f"{tag}_mp{k}", [P, 512], fp32)) for k in range(2)]
        loaded, cleared, split, turned, copied, stored, own = ctx.enter_context(
            phase(nc, tag + "_meta", "loaded cleared split turned copied stored own"))
        with nc.Block() as block:
            @block.sync
            def _(sp):
                sp.wait_ge(cleared, 1)
                n = load(sp, extra_i, extra, ec, loaded)
                sp.wait_ge(copied, 1)
                sp.dma_start(rows[0].rearrange("(t p) -> t p", p=P), kf[:, 0, :]).then_inc(stored, 16)
                sp.dma_start(rows[1].rearrange("(t p) -> t p", p=P), kf[:, 1, :]).then_inc(stored, 16)
                sp.dma_start(meta, mt[:, :, :].rearrange("p t k -> p (t k)")).then_inc(stored, 16)
                k = 3
                if cols is not None:
                    sp.dma_start(cols, ct[:, :, :].rearrange("p t k -> p (t k)")).then_inc(stored, 16)
                    k += 1
                sp.wait_ge(stored, 16 * k)
                env.key_loads = n

            @block.vector
            def _(v):
                st = Steps(v, own)
                v.memset(extra_i[:, :, :], N).then_inc(own, one(st))
                v.memset(mt[:, :, :], 0.0).then_inc(own, one(st))
                v.memset(ec[:, :, :], 0.0).then_inc(own, one(st))
                v.memset(ct[:, :, :], 0.0).then_inc(own, one(st))
                v.wait_ge(own, steps(st))
                v.memset(extra[:, :, :], 0.0).then_inc(cleared, 1)
                v.wait_ge(loaded, 16 * env.key_loads)
                if permuted:
                    v.tensor_copy(extra_i[:, 0, :], ec[:, :, 1]).then_inc(own, one(st))
                    v.tensor_copy(extra[:, 2, :], ec[:, :, 2]).then_inc(own, one(st))
                    v.tensor_copy(extra_i[:, 1, :], ec[:, :, 0]).then_inc(own, one(st))
                    v.wait_ge(own, steps(st))
                v.tensor_copy(extra[:, 0:2, :], extra_i[:, :, :]).then_inc(own, one(st))
                v.tensor_scalar(part[:, 0, :], extra_i[:, 0, :], 9, None, ALU.logical_shift_right).then_inc(own, one(st))
                v.tensor_scalar(part[:, 1, :], extra_i[:, 0, :], W - 1, None, ALU.bitwise_and).then_inc(own, one(st))
                v.wait_ge(own, steps(st))
                v.tensor_copy(kf[:, 0, :], extra[:, 0, :]).then_inc(own, one(st))
                v.tensor_copy(kf[:, 1:3, :], part[:, :, :]).then_inc(own, one(st))
                v.wait_ge(own, steps(st))
                v.sem_inc(split, 1)
                v.wait_ge(turned, 1)
                for k in range(3):
                    v.tensor_copy(mt[:, :, k], ps[0][:, k * P:k * P + T]).then_inc(own, one(st))
                    v.tensor_copy(ct[:, :, k], ps[1][:, k * P:k * P + T]).then_inc(own, one(st))
                v.wait_ge(own, steps(st))
                v.sem_inc(copied, 1)

            @block.tensor
            def _(pe):
                pe.wait_ge(split, 1)
                for k in range(3):
                    pe.transpose(ps[0][:, k * P:k * P + T], kf[:, k, :], env.ident[0:T, 0:T])
                for k in range(3):
                    last = pe.transpose(ps[1][:, k * P:k * P + T], extra[:, k, :], env.ident[0:T, 0:T])
                last.then_inc(turned, 1)


def rank_edges(nc, env, tag, rows, meta, ranks, vtab, btab, count):
    with ExitStack() as ctx:
        def sb(name, shape, dt=fp32):
            return ctx.enter_context(nc.sbuf_tensor(f"{tag}_r_{name}", shape, dt))

        def pb(name):
            return ctx.enter_context(nc.psum_tensor(f"{tag}_r_{name}", [P, W], fp32))
        mt = sb("mt", [P, 2, G * 4])
        rk = sb("rk", [P, 2, W])
        rh = sb("rh", [P, 2, W])
        ohi = sb("ohi", [P, G, P], bf16)
        olo = sb("olo", [P, G, W], bf16)
        oht = sb("oht", [P, G, P])
        tab = sb("tab", [P, 2, W])
        run = sb("run", [P, W])
        off = sb("off", [P, 1])
        scr = sb("scr", [P, W])
        tie = sb("tie", [P, G, P])
        acc = sb("acc", [P, 2, G, 2])
        res = sb("res", [P, 2, G], i32)
        hist, offp, run_ps = pb("hist"), pb("offp"), pb("run_ps")
        look = [pb(f"look{k}") for k in range(2)]
        sems = ctx.enter_context(phase(
            nc, tag + "_rank", "meta0 meta1 onehot counted total offs tabs own m0 m1 hot hot_used copied looked inc rank0 rank1 st0 st1"))
        (meta0, meta1, onehot, counted, total, offs, tabs, own, m0, m1, hot, hot_used, copied, looked,
         inc, rank0, rank1, st0, st1) = sems
        meta_in, meta2_in, ranked, stored = [meta0, meta1], [m0, m1], [rank0, rank1], [st0, st1]
        mv = meta.rearrange("p (c k) -> p c k", c=CH)
        rvk = rows[0].rearrange("(c w) -> c w", w=W)
        rvh = rows[1].rearrange("(c w) -> c w", w=W)
        rkv = ranks.rearrange("p (c k) -> p c k", c=CH)

        with nc.Block() as block:
            @block.sync
            def _(sp):
                def histo(j):
                    for s in range(2):
                        if not first(j):
                            sp.wait_ge(onehot, (2 * j + s - 1) * G)
                        sp.dma_start(mt[:, s, :], mv[:, 2 * j + s, :]).then_inc(meta_in[s], 16)

                def ranking(j):
                    for s in range(2):
                        if first(j):
                            sp.wait_ge(onehot, CH * G)
                        else:
                            sp.wait_ge(ranked[s], j)
                        c = 2 * j + s
                        sp.dma_start(mt[:, s, :], mv[:, c, :]).then_inc(meta2_in[s], 16)
                        sp.dma_start(rk[:, s, :], rvk[bass.ds(c, 1), :].broadcast_to([P, W])).then_inc(meta2_in[s], 16)
                        sp.dma_start(rh[:, s, :], rvh[bass.ds(c, 1), :].broadcast_to([P, W])).then_inc(meta2_in[s], 16)
                Steps(sp, own).loop(PAIRS, histo)
                Steps(sp, own).loop(PAIRS, ranking)

            def onehots(v, s, g, b):
                v.tensor_scalar(ohi[:, b, :], env.iota[:, 0:P], mt[:, s, g * 4 + 1:g * 4 + 2], None, ALU.is_equal)
                return v.tensor_scalar(olo[:, b, :], env.iota[:, :], mt[:, s, g * 4 + 2:g * 4 + 3], None,
                                       ALU.is_equal)

            @block.vector
            def _(v):
                st = Steps(v, own)

                def histo(j):
                    for s in range(2):
                        v.wait_ge(meta_in[s], 16 * (j + 1))
                        for g in range(G):
                            t = (2 * j + s) * G + g
                            if not (first(j) and s == 0):
                                v.wait_ge(counted, t - 3)
                            onehots(v, s, g, g).then_inc(onehot, 1)
                st.loop(PAIRS, histo)
                v.wait_ge(counted, T)
                v.tensor_copy(count, hist[:, :]).then_inc(own, one(st))
                v.wait_ge(own, steps(st))
                v.tensor_tensor_scan(out=run[:, :], data0=env.ones[:, :], data1=count, initial=0.0,
                                            op0=ALU.mult, op1=ALU.add).then_inc(own, one(st))
                v.wait_ge(own, steps(st))
                v.tensor_copy(off[:, :], run[:, W - 1:W]).then_inc(own, one(st))
                v.wait_ge(own, steps(st))
                v.sem_inc(total, 1)
                v.wait_ge(offs, 1)
                v.tensor_copy(off[:, :], offp[:, 0:1]).then_inc(own, one(st))
                v.wait_ge(own, steps(st))
                v.tensor_scalar(run[:, :], run[:, :], off[:, :], None, ALU.add).then_inc(own, one(st))
                v.wait_ge(own, steps(st))
                v.tensor_tensor(btab, run[:, :], count, ALU.subtract).then_inc(own, one(st))
                v.tensor_scalar(scr[:, :], count, 0.0, None, ALU.is_gt).then_inc(own, one(st))
                v.tensor_scalar(vtab, run[:, :], -1.0 - FAR, None, ALU.add).then_inc(own, one(st))
                v.wait_ge(own, steps(st))
                v.tensor_tensor(vtab, vtab, scr[:, :], ALU.mult).then_inc(own, one(st))
                v.wait_ge(own, steps(st))
                v.tensor_scalar(vtab, vtab, float(FAR), None, ALU.add).then_inc(own, one(st))
                v.wait_ge(own, steps(st))
                v.wait_ge(own, steps(st))
                v.sem_inc(tabs, 1)

                before = steps(st)

                def prepare(j, s, g):
                    t = (2 * j + s) * G + g
                    if g == 0:
                        v.wait_ge(meta2_in[s], 48 * (j + 1))
                        if not first(j):
                            v.wait_ge(ranked[s], j)
                    if not (first(j) and s == 0):
                        v.wait_ge(inc, t - 2)
                        v.wait_ge(hot_used, t - 3)
                    onehots(v, s, g, g)
                    v.tensor_scalar(oht[:, g, :], rh[:, s, g * P:(g + 1) * P], env.iotap[:, :], None,
                                    ALU.is_equal).then_inc(hot, 1)
                    v.wait_ge(own, before + t)
                    v.scalar_tensor_tensor(
                        out=tie[:, g, :], in0=rk[:, s, g * P:(g + 1) * P], scalar=mt[:, s, g * 4:g * 4 + 1],
                        in1=env.earlier[:, :], op0=ALU.is_equal, op1=ALU.mult,
                        accum_out=acc[:, s, g, 0:1]).then_inc(own, 1)

                def look_up(j, s, g):
                    t = (2 * j + s) * G + g
                    b = g % 2
                    v.wait_ge(looked, t + 1)
                    v.wait_ge(own, before + t + 1)
                    if not (first(j) and s == 0 and g == 0):
                        v.wait_ge(hot_used, t)
                    v.scalar_tensor_tensor(
                        out=scr[:, :], in0=look[b][:, :], scalar=1.0, in1=olo[:, g, :],
                        op0=ALU.mult, op1=ALU.mult, accum_out=acc[:, s, g, 1:2]).then_inc(hot_used, 1)

                def ranking(j, more=True):
                    for s in range(2):
                        for g in range(G):
                            if g < G - 1:
                                prepare(j, s, g + 1)
                            elif s == 0:
                                prepare(j, 1, 0)
                            elif more:
                                prepare(j + 1, 0, 0)
                            look_up(j, s, g)
                        v.wait_ge(hot_used, (2 * j + s + 1) * G)
                        if not first(j):
                            v.wait_ge(stored[s], 16 * j)
                        v.tensor_tensor(res[:, s, :], acc[:, s, :, 0], acc[:, s, :, 1], ALU.add)\
                            .then_inc(ranked[s], 1)
                prepare(0, 0, 0)
                st.loop(PAIRS - 1, ranking)
                ranking(PAIRS - 1, more=False)

            @block.tensor
            def _(pe):
                st = Steps(pe, own)

                def count_tile(b, t, start):
                    pe.wait_ge(onehot, t + 1)
                    pe.matmul(hist[:, :], ohi[:, b, :], olo[:, b, :], start=start, stop=False,
                              skip_group_check=True).then_inc(counted, 1)

                def histo(j):
                    for k in range(2 * G):
                        count_tile(k % G, 2 * G * j + k, first(j) and k == 0)
                st.loop(PAIRS, histo)
                pe.wait_ge(total, 1)
                pe.matmul(offp[:, 0:1], env.below[:, :], off[:, :], start=True, stop=True).then_inc(offs, 1)
                pe.wait_ge(tabs, 1)
                pe.matmul(run_ps[:, :], env.ident[:, :], btab, start=True, stop=False,
                          skip_group_check=True).then_inc(inc, 1)

                def ranking(j):
                    for k in range(2 * G):
                        b = k % 2
                        t = 2 * G * j + k
                        pe.wait_ge(hot, t + 1)
                        pe.wait_ge(copied, t + 1)
                        pe.matmul(run_ps[:, :], ohi[:, k % G, :], olo[:, k % G, :], start=False, stop=False,
                                  skip_group_check=True).then_inc(inc, 1)
                        if not (first(j) and k < 2):
                            pe.wait_ge(hot_used, t - 1)
                        pe.matmul(look[b][:, :], oht[:, k % G, :], tab[:, b, :], start=True, stop=True)\
                            .then_inc(looked, 1)
                st.loop(PAIRS, ranking)

            @block.scalar
            def _(act):
                def ranking(j):
                    for k in range(2 * G):
                        t = 2 * G * j + k
                        act.wait_ge(inc, t + 1)
                        act.activation(tab[:, k % 2, :], run_ps[:, :], ACT.Copy).then_inc(copied, 1)
                Steps(act, own).loop(PAIRS, ranking)

            @block.gpsimd
            def _(pool):
                def store(j):
                    for s in range(2):
                        pool.wait_ge(ranked[s], j + 1)
                        pool.dma_start(rkv[:, 2 * j + s, :], res[:, s, :]).then_inc(stored[s], 16)
                Steps(pool, own).loop(PAIRS, store)
                for s in range(2):
                    pool.wait_ge(stored[s], 16 * PAIRS)


ROW = F + 4
NIX = 8
(IX_SRC, IX_DST, IX_SRC_D, IX_DST_D, IX_SRC_S, IX_DST_S, IX_OUT_D, IX_OUT_S) = range(NIX)
NFL = 4
FL_W, FL_KEEP_S, FL_REAL = range(3)
MROW = 2 * F + 4


def scatter_edges(nc, env, A, D):
    with ExitStack() as ctx:
        row = ctx.enter_context(nc.sbuf_tensor("sc_row", [P, 2, G, ROW], fp32))
        idx = ctx.enter_context(nc.sbuf_tensor("sc_idx", [P, 2, G], i32))
        in0, in1, out0, out1, own = ctx.enter_context(phase(nc, "sc", "in0 in1 out0 out1 own"))
        filled, left = [in0, in1], [out0, out1]
        ev = A["edge_attr_128"]
        cv = D["cols"].rearrange("p (c g k) -> p c g k", c=CH, g=G)
        rv = D["rank_d"].rearrange("p (c g) -> p c g", c=CH)
        whole = PAIRS - 1
        with nc.Block() as block:
            @block.sync
            def _(sp):
                def load(j, last):
                    for s in range(2):
                        c = 2 * j + s
                        if not first(j):
                            sp.wait_ge(left[s], 16 * G * j)
                        sp.dma_start(idx[:, s, :], rv[:, c, :]).then_inc(filled[s], 16)
                        sp.dma_start(row[:, s, :, F:ROW], cv[:, c, :, :]).then_inc(filled[s], 16)
                        if not last:
                            sp.dma_start(row[:, s, :, 0:F],
                                         ev[bass.ds(c * W, W), :].rearrange("(g p) f -> p g f", p=P))\
                                .then_inc(filled[s], 16)
                        elif s == 0:
                            whole_tiles = (E - c * W) // P
                            for g in range(whole_tiles):
                                sp.dma_start(row[:, s, g, 0:F], ev[c * W + g * P:c * W + (g + 1) * P, :])\
                                    .then_inc(filled[s], 16)
                            sp.dma_start(row[0:REST, s, whole_tiles, 0:F], ev[FULL * P:E, :])\
                                .then_inc(filled[s], 16)
                Steps(sp, own).loop(whole, lambda j: load(j, False))
                load(whole, True)

            @block.gpsimd
            def _(pool):
                def scatter(j, extra):
                    for s in range(2):
                        pool.wait_ge(filled[s], 48 * (j + 1) if extra is None else 48 * j + 32 + extra[s])
                        pool.sem_inc(own, 1)
                        for g in range(G):
                            pool.indirect_dma_start(
                                out=D["edges"][:, :], out_offset=bass.IndirectOffsetOnAxis(ap=idx[:, s, g:g + 1], axis=0),
                                in_=row[:, s, g, :], in_offset=None).then_inc(left[s], 16)
                Steps(pool, own).loop(whole, lambda j: scatter(j, None))
                scatter(whole, (16 * ((E - 2 * whole * W) // P + 1), 0))
                for s in range(2):
                    pool.wait_ge(left[s], 16 * G * PAIRS)


def node_tables(nc, env, D, tabs):
    vd, bd, cd, vs, bs, cs = (tabs[:, k, :] for k in range(6))
    with ExitStack() as ctx:
        vv = ctx.enter_context(nc.sbuf_tensor("nt_vv", [P, W, 4], i32))
        free = ctx.enter_context(nc.sbuf_tensor("nt_free", [P, 2, W], fp32))
        made, stored, own = ctx.enter_context(phase(nc, "nt", "made stored own"))
        with nc.Block() as block:
            @block.vector
            def _(v):
                st = Steps(v, own)
                for k, t in enumerate((vd, vs, bd, bs)):
                    v.tensor_copy(vv[:, :, k], t).then_inc(own, one(st))
                v.tensor_scalar(free[:, 0, :], cd, 0.0, None, ALU.is_equal).then_inc(own, one(st))
                v.tensor_scalar(free[:, 1, :], cs, 0.0, None, ALU.is_equal).then_inc(own, one(st))
                v.wait_ge(own, steps(st))
                v.tensor_tensor(free[:, 0, :], free[:, 0, :], free[:, 1, :], ALU.mult).then_inc(own, one(st))
                v.wait_ge(own, steps(st))
                v.sem_inc(made, 1)

            @block.sync
            def _(sp):
                sp.wait_ge(made, 1)
                sp.dma_start(D["bounds"].rearrange("(h l) k -> h (l k)", l=W),
                             vv[0:HI, :, :].rearrange("h l k -> h (l k)")).then_inc(stored, 16)
                sp.dma_start(D["free"].rearrange("(h l) -> h l", l=W), free[0:HI, 0, :]).then_inc(stored, 16)
                sp.wait_ge(stored, 32)


def slot_indices(nc, env, D):
    with ExitStack() as ctx:
        def sb(name, shape, dt=fp32):
            return ctx.enter_context(nc.sbuf_tensor(f"si_{name}", shape, dt))
        cf, rki, bi = sb("cf", [P, T, 4]), sb("rki", [P, T], i32), sb("bi", [P, T, 2, 4], i32)
        b = sb("b", [P, 2, 4, T])
        rank = sb("rank", [P, T])
        slot, far = sb("slot", [P, T]), sb("far", [P, T])
        real, td, ts, tmp, tmp2, ond, ons = (sb(n, [P, T]) for n in ("real", "td", "ts", "tmp", "tmp2", "ond", "ons"))
        ixf, ixi, ixo = sb("ixf", [P, T]), sb("ixi", [P, T, NIX], i32), sb("ixo", [P, 2, T, NIX], i32)
        fl, rowf, mcol, corner = sb("fl", [P, T, NFL]), sb("rowf", [T, 3, P]), sb("mcol", [P, 2]), sb("corner", [P, 1])
        tp = ctx.enter_context(nc.psum_tensor("si_tp", [P, 512], fp32))
        loaded, iota_done, summed, m_done, made, turned, copied, stored, own, own_p = ctx.enter_context(
            phase(nc, "si", "loaded iota_done summed m_done made turned copied stored own own_p"))
        with nc.Block() as block:
            @block.sync
            def _(sp):
                sp.dma_start(cf[:, :, :].rearrange("p t k -> p (t k)"), D["cols_s"]).then_inc(loaded, 16)
                sp.dma_start(rki[:, :], D["rank_s"]).then_inc(loaded, 16)
                sp.dma_start(bi[:, :, :, :].rearrange("p t k b -> p (t k b)"), D["edge_bounds"])\
                    .then_inc(loaded, 16)
                sp.wait_ge(copied, 1)
                sp.dma_start(D["keep_d"].rearrange("(t p) -> t p", p=P), rowf[:, 0, :]).then_inc(stored, 16)
                sp.dma_start(D["weights"][0:EP].rearrange("(t p) -> t p", p=P), rowf[:, 1, :]).then_inc(stored, 16)
                sp.dma_start(D["weights"][EP:2 * EP].rearrange("(t p) -> t p", p=P), rowf[:, 2, :])\
                    .then_inc(stored, 16)
                sp.dma_start(D["index"], ixi[:, :, :].rearrange("p t k -> p (t k)")).then_inc(stored, 16)
                sp.dma_start(D["factor"], fl[:, :, :].rearrange("p t k -> p (t k)")).then_inc(stored, 16)
                for k in range(2):
                    sp.dma_start(D["index2"][:, k * T * NIX:(k + 1) * T * NIX],
                                 ixo[:, k, :, :].rearrange("p t k -> p (t k)")).then_inc(stored, 16)
                sp.wait_ge(stored, 112)

            @block.gpsimd
            def _(pool):
                st = Steps(pool, own_p)
                pool.iota(slot[:, :], pattern=[[P, T]], base=0, channel_multiplier=1,
                                 allow_small_or_imprecise_dtypes=True).then_inc(own_p, one(st))
                pool.memset(corner[:, :], 0.0).then_inc(own_p, one(st))
                pool.wait_ge(own_p, steps(st))
                pool.affine_select(out=corner[:, :], in_=corner[:, :], compare_op=ALU.not_equal, fill=1.0,
                                          base=1 - P, pattern=[[0, 1]], channel_multiplier=1).then_inc(own_p, one(st))
                pool.wait_ge(own_p, steps(st))
                pool.sem_inc(iota_done, 1)

            @block.vector
            def _(v):
                st = Steps(v, own)

                def do(ins):
                    ins.then_inc(own, one(st))
                    v.wait_ge(own, steps(st))
                v.wait_ge(loaded, 48)
                v.wait_ge(iota_done, 1)
                for k in range(2):
                    for q in range(4):
                        v.tensor_copy(b[:, k, q, :], bi[:, :, k, q]).then_inc(own, one(st))
                v.memset(far[:, :], float(FAR)).then_inc(own, one(st))
                v.memset(fl[:, :, :], 0.0).then_inc(own, one(st))
                do(v.tensor_copy(rank[:, :], rki[:, :]))
                src, dst = cf[:, :, 0], cf[:, :, 1]
                s_vd, s_vs, s_bd, s_bs = (b[:, 0, q, :] for q in range(4))
                d_vd, d_vs, d_bd, d_bs = (b[:, 1, q, :] for q in range(4))
                do(v.tensor_scalar(real[:, :], slot[:, :], float(E), None, ALU.is_lt))
                do(v.tensor_scalar(td[:, :], s_vd, float(FAR), None, ALU.is_lt))
                do(v.tensor_tensor(td[:, :], td[:, :], real[:, :], ALU.mult))
                do(v.tensor_scalar(ts[:, :], d_vs, float(FAR), None, ALU.is_lt))

                def put(k, value):
                    do(v.tensor_copy(ixi[:, :, k], value))

                def pick(k, cond, value, other, shift):
                    do(v.tensor_scalar(tmp[:, :], other, float(shift), None, ALU.add))
                    do(v.tensor_tensor(tmp2[:, :], value, cond, ALU.mult))
                    do(v.tensor_scalar(ixf[:, :], cond, -1.0, 1.0, ALU.mult, ALU.add))
                    do(v.tensor_tensor(tmp[:, :], tmp[:, :], ixf[:, :], ALU.mult))
                    do(v.tensor_tensor(tmp[:, :], tmp[:, :], tmp2[:, :], ALU.add))
                    put(k, tmp[:, :])
                do(v.tensor_scalar(tmp[:, :], src, float(N - 1), None, ALU.min))
                put(IX_SRC, tmp[:, :])
                do(v.tensor_scalar(tmp[:, :], dst, float(N - 1), None, ALU.min))
                put(IX_DST, tmp[:, :])
                pick(IX_SRC_D, td[:, :], s_vd, slot[:, :], EP)
                put(IX_DST_D, d_vd)
                put(IX_SRC_S, s_vs)
                pick(IX_DST_S, ts[:, :], d_vs, slot[:, :], EP)
                do(v.tensor_tensor(ond[:, :], slot[:, :], d_vd, ALU.is_equal))
                do(v.tensor_tensor(ond[:, :], ond[:, :], real[:, :], ALU.mult))
                pick(IX_OUT_D, ond[:, :], dst, far[:, :], 0)
                do(v.tensor_tensor(fl[:, :, FL_KEEP_S], rank[:, :], s_bs, ALU.not_equal))
                do(v.tensor_tensor(ons[:, :], rank[:, :], s_bs, ALU.is_equal))
                do(v.tensor_tensor(ons[:, :], ons[:, :], real[:, :], ALU.mult))
                do(v.tensor_tensor(tmp[:, :], ons[:, :], td[:, :], ALU.mult))
                do(v.tensor_tensor(ons[:, :], ons[:, :], tmp[:, :], ALU.subtract))
                pick(IX_OUT_S, ons[:, :], src, far[:, :], 0)
                do(v.tensor_copy(fl[:, :, FL_W], cf[:, :, 2]))
                do(v.tensor_copy(fl[:, :, FL_REAL], real[:, :]))
                do(v.tensor_copy(ixo[:, 0, :, :], ixi[:, :, :]))
                do(v.tensor_copy(ixo[:, 1, :, :], ixi[:, :, :]))
                do(v.tensor_copy(ixo[:, 0, :, 0], ixi[:, :, IX_OUT_D]))
                do(v.tensor_copy(ixo[:, 1, :, 0], ixi[:, :, IX_OUT_S]))
                do(v.reduce_sum(mcol[:, 0:1], ond[:, :], axis=mybir.AxisListType.X))
                do(v.reduce_sum(mcol[:, 1:2], ons[:, :], axis=mybir.AxisListType.X))
                do(v.tensor_tensor(mcol[:, 0:1], mcol[:, 0:1], mcol[:, 1:2], ALU.add))
                v.wait_ge(own, steps(st))
                v.sem_inc(summed, 1)
                v.wait_ge(m_done, 1)
                do(v.tensor_scalar(mcol[:, 1:2], tp[:, 0:1], corner[:, :], -1.0, ALU.mult, ALU.mult))
                do(v.tensor_tensor(ons[:, T - 1:T], ons[:, T - 1:T], mcol[:, 1:2], ALU.add))
                do(v.tensor_tensor(tmp[:, :], slot[:, :], d_bd, ALU.not_equal))
                v.wait_ge(own, steps(st))
                v.sem_inc(made, 1)
                v.wait_ge(turned, 1)
                do(v.tensor_copy(rowf[:, :, :], tp[0:T, 128:512].rearrange("t (k p) -> t k p", k=3)))
                v.wait_ge(own, steps(st))
                v.sem_inc(copied, 1)

            @block.tensor
            def _(pe):
                pe.wait_ge(summed, 1)
                pe.matmul(tp[:, 0:1], env.ones[:, 0:P], mcol[:, 0:1], start=True, stop=True).then_inc(m_done, 1)
                pe.wait_ge(made, 1)
                pe.transpose(tp[0:T, 128:256], tmp[:, :], env.ident[:, :])
                pe.transpose(tp[0:T, 256:384], ond[:, :], env.ident[:, :])
                pe.transpose(tp[0:T, 384:512], ons[:, :], env.ident[:, :]).then_inc(turned, 1)


def rows4(ap, c):
    return ap[bass.ds(c * W, W), :].rearrange("(g p) f -> p g f", p=P)


def spread(row, n=G):
    return row.rearrange("p (a f) -> p a f", a=1).broadcast_to([row.shape[0], n, F])


def moments(v, st, x, stats, mv):
    n = x.shape[1]
    for g in range(n):
        v.bn_stats(stats[:, g, :], x[:, g, :]).then_inc(st.sem, one(st))
    v.wait_ge(st.sem, steps(st))
    v.sem_inc(st.sem, one(st))
    for g in range(n):
        v.bn_aggr(mv[:, g, :], stats[:, g, :]).then_inc(st.sem, one(st))


def norm_stats(v, st, x, stats, mv, scale=1.0, eps=LN_EPS):
    moments(v, st, x, stats, mv)
    v.wait_ge(st.sem, steps(st))
    v.tensor_scalar(mv[:, :, 1], mv[:, :, 1], scale, eps, ALU.mult, ALU.add).then_inc(st.sem, one(st))


def norm_apply(v, st, x, mv, sd, out, mask=None):
    v.reciprocal(sd, sd).then_inc(st.sem, one(st))
    v.wait_ge(st.sem, steps(st))
    if mask is not None:
        v.tensor_tensor(sd, sd, mask, ALU.mult).then_inc(st.sem, one(st))
        v.wait_ge(st.sem, steps(st))
    for g in range(x.shape[1]):
        v.tensor_scalar(out[:, g, :], x[:, g, :], mv[:, g, 0:1], sd[:, g:g + 1], ALU.subtract, ALU.mult).then_inc(st.sem, one(st))


def views(D):
    return (D["index"].rearrange("p (c k) -> p c k", c=CH), D["factor"].rearrange("p (c k) -> p c k", c=CH),
            D["keep_d"].rearrange("(c w) -> c w", w=W))


def gather4(pool, out, table, ix, k, sem):
    for g in range(G):
        pool.indirect_dma_start(out=out[:, g, :], out_offset=None, in_=table,
                                in_offset=bass.IndirectOffsetOnAxis(ap=ix[:, g * NIX + k:g * NIX + k + 1], axis=0))\
            .then_inc(sem, 16)


def transpose4(pe, env, out, rows, parts=P):
    for g in range(G):
        last = pe.transpose(out[:, g * parts:(g + 1) * parts], rows[:, g, :], env.ident[0:parts, 0:parts])
    return last


def to_rows4(pe, out, cols, w, parts=P):
    for g in range(G):
        last = pe.matmul(out[0:parts, g * F:(g + 1) * F], cols[:, g * parts:(g + 1) * parts], w,
                         start=True, stop=True)
    return last


def uses(s, n=CH):
    return (n - s + NS - 1) // NS


class Mem:

    def __init__(self, nc, ctx, tag):
        self.nc, self.ctx, self.tag = nc, ctx, tag

    def sb(self, name, *shape, dt=fp32):
        return self.ctx.enter_context(self.nc.sbuf_tensor(f"{self.tag}_{name}", [P, *shape], dt))

    def ps(self, name):
        return self.ctx.enter_context(self.nc.psum_tensor(f"{self.tag}_{name}", [P, W], fp32))

    def sems(self, names):
        return self.ctx.enter_context(phase(self.nc, self.tag, names))


def edge_layer0(nc, env, A, D):
    with ExitStack() as ctx:
        m = Mem(nc, ctx, "e0")
        ix, fl, keep = m.sb("ix", NS, G * NIX, dt=i32), m.sb("fl", NS, G * NFL), m.sb("keep", NS, W)
        xs, xd, ms = m.sb("xs", NS, G, F), m.sb("xd", NS, G, F), m.sb("ms", NS, G, F)
        agg, zs, zd = m.sb("agg", NS, W), m.sb("zs", NS, W), m.sb("zd", NS, W)
        hs, hd = m.sb("hs", NS, W), m.sb("hd", NS, W)
        vv, stats, mv, sd = m.sb("vv", 2 * G, F), m.sb("stats", 2 * G, 6), m.sb("mv", 2 * G, 2), m.sb("sd", 2 * G)
        xo = m.sb("xo", NS, 2, G, F)
        tm, ts, td, ps_s, ps_d, o_s, o_d = (m.ps(n) for n in ("tm", "ts", "td", "ps_s", "ps_d", "o_s", "o_d"))
        (filled, got, stored, weighted, turned, summed, copied, hidden, relued, projected, added, measured, rooted,
         normed, own_v, own_a, own) = m.sems("filled* got* stored* weighted turned summed copied hidden relued projected "
                                             "added measured rooted normed own_v own_a own")
        iv, fv, kv = views(D)
        with nc.Block() as block:
            @block.sync
            def _(sp):
                def load(c, j, s):
                    if not first(j):
                        sp.wait_ge(summed, c + 1 - NS)
                        sp.sem_inc(own, 1)
                        sp.wait_ge(got[s], 128 * j)
                    sp.sem_inc(own, 1)
                    sp.dma_start(ix[:, s, :], iv[:, c, :]).then_inc(filled[s], 16)
                    sp.dma_start(fl[:, s, :], fv[:, c, :]).then_inc(filled[s], 16)
                    sp.dma_start(keep[:, s, :], kv[bass.ds(c, 1), :].broadcast_to([P, W])).then_inc(filled[s], 16)

                def store(c, j, s):
                    sp.wait_ge(normed, c + 1)
                    sp.sem_inc(own, 1)
                    sp.dma_start(rows4(D["x1"], c), xo[:, s, 1, :, :]).then_inc(stored[s], 16)
                    sp.dma_start(rows4(D["x1"], c + CH), xo[:, s, 0, :, :]).then_inc(stored[s], 16)
                pipeline(Steps(sp, own), CH, NS, (6, store), (0, load))
                for s in range(NS):
                    sp.wait_ge(stored[s], 32 * uses(s))

            @block.gpsimd
            def _(pool):
                def gather(c, j, s):
                    if not first(j):
                        pool.wait_ge(added, c + 1 - NS)
                    pool.wait_ge(filled[s], 48 * (j + 1))
                    pool.sem_inc(own, 1)
                    gather4(pool, xs[:, s, :, :], A["x"], ix[:, s, :], IX_SRC, got[s])
                    gather4(pool, xd[:, s, :, :], A["x"], ix[:, s, :], IX_DST, got[s])
                pipeline(Steps(pool, own), CH, NS, (0, gather))

            @block.vector
            def _(v):
                st = Steps(v, own_v)

                def weigh(c, j, s):
                    v.wait_ge(got[s], 128 * (j + 1))
                    if not first(j):
                        v.wait_ge(turned, c + 1 - NS)
                    for g in range(G):
                        k = g * NFL + FL_W
                        v.tensor_scalar(ms[:, s, g, :], xs[:, s, g, :], fl[:, s, k:k + 1], None, ALU.mult).then_inc(own_v, one(st))
                    v.wait_ge(own_v, steps(st))
                    v.sem_inc(weighted, 1)

                def scan(c, j, s):
                    v.wait_ge(turned, c + 1)
                    start = 0.0 if first(j) and s == 0 else agg[:, (s - 1) % NS, W - 1:W]
                    v.tensor_tensor_scan(out=agg[:, s, :], data0=keep[:, s, :], data1=tm[:, :], initial=start,
                                                op0=ALU.mult, op1=ALU.add).then_inc(own_v, one(st))
                    v.wait_ge(own_v, steps(st))
                    v.tensor_tensor(zd[:, s, :], td[:, :], agg[:, s, :], ALU.add).then_inc(own_v, one(st))
                    v.wait_ge(own_v, steps(st))
                    v.sem_inc(summed, 1)

                def measure(c, j, s):
                    v.wait_ge(projected, c + 1)
                    v.tensor_tensor(vv[:, 0:G, :], o_s[:, :].rearrange("p (g f) -> p g f", g=G),
                                           xs[:, s, :, :], ALU.add).then_inc(own_v, one(st))
                    v.tensor_tensor(vv[:, G:2 * G, :], o_d[:, :].rearrange("p (g f) -> p g f", g=G),
                                           xd[:, s, :, :], ALU.add).then_inc(own_v, one(st))
                    v.wait_ge(own_v, steps(st))
                    v.sem_inc(added, 1)
                    v.tensor_tensor(vv[:, :, :], vv[:, :, :], spread(env.bc["L0_gnn_b2"], 2 * G), ALU.add).then_inc(own_v, one(st))
                    v.wait_ge(own_v, steps(st))
                    moments(v, st, vv, stats, mv)
                    v.wait_ge(own_v, steps(st))
                    v.sem_inc(measured, 1)

                def finish(c, j, s):
                    v.wait_ge(rooted, c + 1)
                    if not first(j):
                        v.wait_ge(stored[s], 32 * j)
                    norm_apply(v, st, vv, mv, sd[:, :], xo[:, s, :, :, :].rearrange("p k g f -> p (k g) f"))
                    v.wait_ge(own_v, steps(st))
                    v.sem_inc(normed, 1)
                pipeline(st, CH, NS, (1, scan), (3, finish), (0, weigh), (2, measure))

            @block.scalar
            def _(act):
                st = Steps(act, own_a)

                def copy(c, j, s):
                    act.wait_ge(turned, c + 1)
                    act.activation(zs[:, s, :], ts[:, :], ACT.Copy).then_inc(copied, 1)

                def relu(c, j, s):
                    act.wait_ge(hidden, c + 1)
                    if not first(j):
                        act.wait_ge(projected, c + 1 - NS)
                    act.activation(hs[:, s, :], ps_s[:, :], ACT.Relu, bias=env.col["L0_gnn_b1"]).then_inc(own_a, one(st))
                    act.activation(hd[:, s, :], ps_d[:, :], ACT.Relu, bias=env.col["L0_gnn_b1"]).then_inc(own_a, one(st))
                    act.wait_ge(own_a, steps(st))
                    act.sem_inc(relued, 1)

                def root(c, j, s):
                    act.wait_ge(measured, c + 1)
                    act.activation(sd[:, :], mv[:, :, 1], ACT.Sqrt, bias=env.eps[:, 2:3]).then_inc(rooted, 1)
                pipeline(st, CH, NS, (1, relu), (0, copy), (2, root))

            @block.tensor
            def _(pe):
                def turn(c, j, s):
                    pe.wait_ge(weighted, c + 1)
                    if not (first(j) and s == 0):
                        pe.wait_ge(summed, c)
                        pe.wait_ge(copied, c)
                    transpose4(pe, env, tm, ms[:, s, :, :])
                    transpose4(pe, env, ts, xs[:, s, :, :])
                    transpose4(pe, env, td, xd[:, s, :, :]).then_inc(turned, 1)

                def hide(c, j, s):
                    pe.wait_ge(summed, c + 1)
                    pe.wait_ge(copied, c + 1)
                    if not (first(j) and s == 0):
                        pe.wait_ge(relued, c)
                    pe.matmul(ps_s[:, :], env.w["L0_gnn_W1"], zs[:, s, :], start=True, stop=True)
                    pe.matmul(ps_d[:, :], env.w["L0_gnn_W1"], zd[:, s, :], start=True, stop=True)\
                        .then_inc(hidden, 1)

                def project(c, j, s):
                    pe.wait_ge(relued, c + 1)
                    if not (first(j) and s == 0):
                        pe.wait_ge(added, c)
                    to_rows4(pe, o_s, hs[:, s, :], env.w["L0_gnn_W2"])
                    to_rows4(pe, o_d, hd[:, s, :], env.w["L0_gnn_W2"]).then_inc(projected, 1)
                pipeline(Steps(pe, own), CH, NS, (2, project), (1, hide), (0, turn))


def soft_plus_scalar(act, st, src, bias, t, r):
    act.activation(r, src, ACT.Relu, bias=bias).then_inc(st.sem, one(st))
    act.activation(t, src, ACT.Abs, bias=bias).then_inc(st.sem, one(st))
    act.wait_ge(st.sem, steps(st))
    act.activation(t, t, ACT.Exp, scale=-1.0).then_inc(st.sem, one(st))
    act.wait_ge(st.sem, steps(st))
    act.activation(t, t, ACT.Ln, bias=1.0).then_inc(st.sem, one(st))


def edge_layer1(nc, env, D):
    with ExitStack() as ctx:
        m = Mem(nc, ctx, "e1")
        ix, fl, rk = m.sb("ix", NS, G * NIX, dt=i32), m.sb("fl", NS, G * NFL), m.sb("rk", NS, G, dt=i32)
        ea, xd, mr = m.sb("ea", NS, G, F), m.sb("xd", NS, G, F), m.sb("mr", NS, G, MROW)
        xt, et, sp_t, sp_r, fs = m.sb("xt", NS, W), m.sb("et", NS, W), m.sb("sp_t", W), m.sb("sp_r", W), m.sb("fs", NS, W)
        fr = m.sb("fr", G, F)
        vv, stats, mv, sd, xo = m.sb("vv", G, F), m.sb("stats", G, 6), m.sb("mv", G, 2), m.sb("sd", G), m.sb("xo", NS, G, F)
        td, te, pe1, pf, px = (m.ps(n) for n in ("td", "te", "pe1", "pf", "px"))
        (filled, ranks_in, got, stored, sent, turned, copied_x, copied_e, hidden, softened, filtered, projected, multiplied,
         measured, rooted, normed, own_v, own_a, own) = m.sems(
            "filled* ranks_in* got* stored* sent* turned copied_x copied_e hidden softened filtered projected multiplied "
            "measured rooted normed own_v own_a own")
        iv, fv, kv = views(D)
        rv = D["rank_s"].rearrange("p (c g) -> p c g", c=CH)
        with nc.Block() as block:
            @block.sync
            def _(sp):
                def load(c, j, s):
                    if not first(j):
                        sp.wait_ge(measured, c + 1 - NS)
                    sp.sem_inc(own, 1)
                    sp.dma_start(ix[:, s, :], iv[:, c, :]).then_inc(filled[s], 16)
                    sp.dma_start(fl[:, s, :], fv[:, c, :]).then_inc(filled[s], 16)
                    sp.dma_start(ea[:, s, :, :], rows4(D["edges"], c)[:, :, 0:F]).then_inc(filled[s], 16)

                def load_ranks(c, j, s):
                    if not first(j):
                        sp.wait_ge(sent[s], 16 * G * j)
                    sp.sem_inc(own, 1)
                    sp.dma_start(rk[:, s, :], rv[:, c, :]).then_inc(ranks_in[s], 16)

                def store(c, j, s):
                    sp.wait_ge(normed, c + 1)
                    sp.sem_inc(own, 1)
                    sp.dma_start(rows4(D["x2"], c + CH), xo[:, s, :, :]).then_inc(stored[s], 16)
                pipeline(Steps(sp, own), CH, NS, (6, store), (0, load), (1, load_ranks))
                for s in range(NS):
                    sp.wait_ge(stored[s], 16 * uses(s))

            @block.gpsimd
            def _(pool):
                def gather(c, j, s):
                    pool.wait_ge(filled[s], 48 * (j + 1))
                    pool.sem_inc(own, 1)
                    gather4(pool, xd[:, s, :, :], D["x1"], ix[:, s, :], IX_DST_D, got[s])

                def gather_src(c, j, s):
                    if not first(j):
                        pool.wait_ge(sent[s], 16 * G * j)
                    pool.sem_inc(own, 1)
                    gather4(pool, mr[:, s, :, F:2 * F], D["x1"], ix[:, s, :], IX_SRC_D, got[s])

                def send(c, j, s):
                    pool.wait_ge(multiplied, c + 1)
                    pool.wait_ge(got[s], 128 * (j + 1))
                    pool.wait_ge(ranks_in[s], 16 * (j + 1))
                    pool.sem_inc(own, 1)
                    for g in range(G):
                        pool.indirect_dma_start(
                            out=D["message"], out_offset=bass.IndirectOffsetOnAxis(ap=rk[:, s, g:g + 1], axis=0),
                            in_=mr[:, s, g, :], in_offset=None).then_inc(sent[s], 16)
                pipeline(Steps(pool, own), CH, NS, (0, gather), (3, send), (0, gather_src))
                for s in range(NS):
                    pool.wait_ge(sent[s], 16 * G * uses(s))

            @block.vector
            def _(v):
                st = Steps(v, own_v)

                def copy(c, j, s):
                    v.wait_ge(turned, c + 1)
                    v.tensor_copy(et[:, s, :], te[:, :]).then_inc(copied_e, 1)

                def filt(c, j, s):
                    v.wait_ge(softened, c + 1)
                    if not first(j):
                        v.wait_ge(projected, c + 1 - NS)
                    v.scalar_tensor_tensor(out=fs[:, s, :], in0=sp_r[:, :], scalar=-LOG2, in1=sp_t[:, :],
                                                  op0=ALU.add, op1=ALU.add).then_inc(own_v, one(st))
                    v.wait_ge(own_v, steps(st))
                    v.sem_inc(filtered, 1)

                def product(c, j, s):
                    v.wait_ge(projected, c + 1)
                    v.wait_ge(got[s], 128 * (j + 1))
                    v.tensor_tensor(fr[:, :, :], pf[:, :].rearrange("p (g f) -> p g f", g=G),
                                           spread(env.bc["L1_gnn_be2"]), ALU.add).then_inc(own_v, one(st))
                    v.wait_ge(own_v, steps(st))
                    if first(j):
                        v.memset(mr[:, s, :, 2 * F:MROW], 0.0).then_inc(own_v, one(st))
                        v.wait_ge(own_v, steps(st))
                    else:
                        v.memset(vv[:, 0, 0:1], 0.0).then_inc(own_v, one(st))
                    v.tensor_tensor(mr[:, s, :, 0:F], fr[:, :, :], px[:, :].rearrange("p (g f) -> p g f", g=G),
                                           ALU.mult).then_inc(own_v, one(st))
                    v.tensor_copy(mr[:, s, :, 2 * F], fl[:, s, :].rearrange("p (g k) -> p g k", k=NFL)
                                         [:, :, FL_KEEP_S]).then_inc(own_v, one(st))
                    v.wait_ge(own_v, steps(st))
                    v.sem_inc(multiplied, 1)
                    v.scalar_tensor_tensor(out=vv[:, :, :], in0=xd[:, s, :, :], scalar=2.0,
                                                  in1=spread(env.h0), op0=ALU.mult, op1=ALU.add).then_inc(own_v, one(st))
                    v.wait_ge(own_v, steps(st))
                    moments(v, st, vv, stats, mv)
                    v.wait_ge(own_v, steps(st))
                    v.sem_inc(measured, 1)

                def finish(c, j, s):
                    v.wait_ge(rooted, c + 1)
                    if not first(j):
                        v.wait_ge(stored[s], 16 * j)
                    norm_apply(v, st, vv, mv, sd[:, :], xo[:, s, :, :])
                    v.wait_ge(own_v, steps(st))
                    v.sem_inc(normed, 1)
                pipeline(st, CH, NS, (3, finish), (2, product), (1, filt), (0, copy))

            @block.scalar
            def _(act):
                st = Steps(act, own_a)

                def copy(c, j, s):
                    act.wait_ge(turned, c + 1)
                    act.activation(xt[:, s, :], td[:, :], ACT.Copy).then_inc(copied_x, 1)

                def soft(c, j, s):
                    act.wait_ge(hidden, c + 1)
                    if not (first(j) and s == 0):
                        act.wait_ge(filtered, c)
                    soft_plus_scalar(act, st, pe1[:, :], env.col["L1_gnn_be1"], sp_t[:, :], sp_r[:, :])
                    act.wait_ge(own_a, steps(st))
                    act.sem_inc(softened, 1)

                def root(c, j, s):
                    act.wait_ge(measured, c + 1)
                    act.activation(sd[:, :], mv[:, :, 1], ACT.Sqrt, bias=env.eps[:, 2:3]).then_inc(rooted, 1)
                pipeline(st, CH, NS, (3, root), (1, soft), (0, copy))

            @block.tensor
            def _(pe):
                def turn(c, j, s):
                    pe.wait_ge(got[s], 128 * (j + 1))
                    pe.wait_ge(filled[s], 48 * (j + 1))
                    if not (first(j) and s == 0):
                        pe.wait_ge(copied_x, c)
                        pe.wait_ge(copied_e, c)
                    transpose4(pe, env, td, xd[:, s, :, :])
                    transpose4(pe, env, te, ea[:, s, :, :]).then_inc(turned, 1)

                def hide(c, j, s):
                    pe.wait_ge(copied_e, c + 1)
                    if not (first(j) and s == 0):
                        pe.wait_ge(softened, c)
                    pe.matmul(pe1[:, :], env.w["L1_gnn_We1"], et[:, s, :], start=True, stop=True).then_inc(hidden, 1)

                def project(c, j, s):
                    pe.wait_ge(filtered, c + 1)
                    pe.wait_ge(copied_x, c + 1)
                    if not (first(j) and s == 0):
                        pe.wait_ge(multiplied, c)
                    to_rows4(pe, px, xt[:, s, :], env.w["L1_gnn_Wn"])
                    to_rows4(pe, pf, fs[:, s, :], env.w["L1_gnn_We2"]).then_inc(projected, 1)
                pipeline(Steps(pe, own), CH, NS, (2, project), (1, hide), (0, turn))


def keep_rows(nc, env, D):
    with ExitStack() as ctx:
        m = Mem(nc, ctx, "kr")
        buf, row = m.sb("buf", P, 4), m.sb("row", P)
        loaded, copied, stored = m.sems("loaded copied stored")
        with nc.Block() as block:
            @block.sync
            def _(sp):
                sp.dma_start(buf[0:T, :, :], D["message"].rearrange("(t p) f -> t p f", p=P)[:, :, 2 * F:MROW])\
                    .then_inc(loaded, 16)
                sp.wait_ge(copied, 1)
                sp.dma_start(D["keep_s"].rearrange("(t p) -> t p", p=P), row[0:T, :]).then_inc(stored, 16)
                sp.wait_ge(stored, 16)

            @block.vector
            def _(v):
                v.wait_ge(loaded, 16)
                v.tensor_copy(row[0:T, :], buf[0:T, :, 0]).then_inc(copied, 1)


def source_layer1(nc, env, D):
    with ExitStack() as ctx:
        m = Mem(nc, ctx, "s1")
        mr, keep = m.sb("mr", NS, G, MROW), m.sb("keep", NS, W)
        agg, sp_t, sp_r, fs = m.sb("agg", NS, W), m.sb("sp_t", 2, W), m.sb("sp_r", 2, W), m.sb("fs", NS, W)
        vv, stats, mv, sd, xo = m.sb("vv", G, F), m.sb("stats", G, 6), m.sb("mv", G, 2), m.sb("sd", G), m.sb("xo", NS, G, F)
        tm, po, ph = m.ps("tm"), m.ps("po"), [m.ps("ph0"), m.ps("ph1")]
        (filled, stored, turned, summed, hidden, softened, filtered, projected, added,
         measured, rooted, normed, own_v, own_a, own) = m.sems(
            "filled* stored* turned summed hidden softened filtered projected added measured rooted normed own_v own_a own")
        kv = D["keep_s"].rearrange("(c w) -> c w", w=W)
        with nc.Block() as block:
            @block.sync
            def _(sp):
                def load(c, j, s):
                    if not first(j):
                        sp.wait_ge(added, c + 1 - NS)
                    sp.sem_inc(own, 1)
                    sp.dma_start(mr[:, s, :, :], rows4(D["message"], c)).then_inc(filled[s], 16)
                    sp.dma_start(keep[:, s, :], kv[bass.ds(c, 1), :].broadcast_to([P, W])).then_inc(filled[s], 16)

                def store(c, j, s):
                    sp.wait_ge(normed, c + 1)
                    sp.sem_inc(own, 1)
                    sp.dma_start(rows4(D["x2"], c), xo[:, s, :, :]).then_inc(stored[s], 16)
                pipeline(Steps(sp, own), CH, NS, (6, store), (0, load))
                for s in range(NS):
                    sp.wait_ge(stored[s], 16 * uses(s))

            @block.vector
            def _(v):
                st = Steps(v, own_v)

                def scan(c, j, s):
                    v.wait_ge(turned, c + 1)
                    start = 0.0 if first(j) and s == 0 else agg[:, (s - 1) % NS, W - 1:W]
                    if not first(j):
                        v.wait_ge(hidden, c + 1 - NS)
                    v.tensor_tensor_scan(out=agg[:, s, :], data0=keep[:, s, :], data1=tm[:, :], initial=start,
                                                op0=ALU.mult, op1=ALU.add).then_inc(own_v, one(st))
                    v.wait_ge(own_v, steps(st))
                    v.sem_inc(summed, 1)

                def filt(c, j, s):
                    v.wait_ge(softened, c + 1)
                    if not first(j):
                        v.wait_ge(projected, c + 1 - NS)
                    v.scalar_tensor_tensor(out=fs[:, s, :], in0=sp_r[:, s % 2, :], scalar=-LOG2, in1=sp_t[:, s % 2, :],
                                                  op0=ALU.add, op1=ALU.add).then_inc(own_v, one(st))
                    v.wait_ge(own_v, steps(st))
                    v.sem_inc(filtered, 1)

                def measure(c, j, s):
                    v.wait_ge(projected, c + 1)
                    v.scalar_tensor_tensor(out=vv[:, :, :], in0=mr[:, s, :, F:2 * F], scalar=2.0,
                                                  in1=po[:, :].rearrange("p (g f) -> p g f", g=G),
                                                  op0=ALU.mult, op1=ALU.add).then_inc(own_v, one(st))
                    v.wait_ge(own_v, steps(st))
                    v.sem_inc(added, 1)
                    v.tensor_tensor(vv[:, :, :], vv[:, :, :], spread(env.bc["L1_gnn_b3"]), ALU.add).then_inc(own_v, one(st))
                    v.wait_ge(own_v, steps(st))
                    moments(v, st, vv, stats, mv)
                    v.wait_ge(own_v, steps(st))
                    v.sem_inc(measured, 1)

                def finish(c, j, s):
                    v.wait_ge(rooted, c + 1)
                    if not first(j):
                        v.wait_ge(stored[s], 16 * j)
                    norm_apply(v, st, vv, mv, sd[:, :], xo[:, s, :, :])
                    v.wait_ge(own_v, steps(st))
                    v.sem_inc(normed, 1)
                pipeline(st, CH, NS, (2, filt), (0, scan), (3, finish), (2, measure))

            @block.scalar
            def _(act):
                st = Steps(act, own_a)

                def soft(c, j, s):
                    act.wait_ge(hidden, c + 1)
                    if not (first(j) and s < 2):
                        act.wait_ge(filtered, c - 1)
                    soft_plus_scalar(act, st, ph[s % 2][:, :], env.col["L1_gnn_b2"], sp_t[:, s % 2, :],
                                     sp_r[:, s % 2, :])
                    act.wait_ge(own_a, steps(st))
                    act.sem_inc(softened, 1)

                def root(c, j, s):
                    act.wait_ge(measured, c + 1)
                    act.activation(sd[:, :], mv[:, :, 1], ACT.Sqrt, bias=env.eps[:, 2:3]).then_inc(rooted, 1)
                pipeline(st, CH, NS, (3, root), (1, soft))

            @block.tensor
            def _(pe):
                def turn(c, j, s):
                    pe.wait_ge(filled[s], 32 * (j + 1))
                    if not (first(j) and s == 0):
                        pe.wait_ge(summed, c)
                    transpose4(pe, env, tm, mr[:, s, :, 0:F]).then_inc(turned, 1)

                def hide(c, j, s):
                    pe.wait_ge(summed, c + 1)
                    if not (first(j) and s < 2):
                        pe.wait_ge(softened, c - 1)
                    pe.matmul(ph[s % 2][:, :], env.w["L1_gnn_W2"], agg[:, s, :], start=True, stop=True).then_inc(hidden, 1)

                def project(c, j, s):
                    pe.wait_ge(filtered, c + 1)
                    if not (first(j) and s == 0):
                        pe.wait_ge(added, c)
                    to_rows4(pe, po, fs[:, s, :], env.w["L1_gnn_W3"]).then_inc(projected, 1)
                pipeline(Steps(pe, own), CH, NS, (0, turn), (2, project), (0, hide))


def edge_layer2(nc, env, D):
    with ExitStack() as ctx:
        m = Mem(nc, ctx, "e2")
        ix, fl, keep = m.sb("ix", NS, G * NIX, dt=i32), m.sb("fl", NS, G * NFL), m.sb("keep", NS, W)
        xs, xd, df = m.sb("xs", NS, G, F), m.sb("xd", NS, G, F), m.sb("df", NS, G, F)
        xt, dt_, pen, agg = m.sb("xt", NS, W), m.sb("dt", NS, W), m.sb("pen", NS, W), m.sb("agg", NS, W)
        ab, fin, am = m.sb("ab", W), m.sb("fin", W), m.sb("am", NS, W)
        vv, stats, mv, sd = m.sb("vv", NS, 2 * G, F), m.sb("stats", 2 * G, 6), m.sb("mv", 2 * G, 2), m.sb("sd", 2 * G)
        mask, xo = m.sb("mask", NS, 2 * G), m.sb("xo", NS, 2, G, F)
        ta, tb, pm, tr = m.ps("ta"), m.ps("tb"), m.ps("pm"), [m.ps("tr0"), m.ps("tr1")]
        (filled, got, stored, differed, turned, copied_x, copied_d, mixed, scanned, maxed, returned, added,
         measured, rooted, normed, own_v, own_a, own) = m.sems(
            "filled* got* stored* differed turned copied_x copied_d mixed scanned maxed returned added measured rooted "
            "normed own_v own_a own")
        iv, fv, kv = views(D)
        with nc.Block() as block:
            @block.sync
            def _(sp):
                def load(c, j, s):
                    if not first(j):
                        sp.wait_ge(differed, c + 1 - NS)
                        sp.sem_inc(own, 1)
                        sp.wait_ge(got[s], 128 * j)
                    sp.sem_inc(own, 1)
                    sp.dma_start(ix[:, s, :], iv[:, c, :]).then_inc(filled[s], 16)
                    sp.dma_start(fl[:, s, :], fv[:, c, :]).then_inc(filled[s], 16)
                    sp.dma_start(keep[:, s, :], kv[bass.ds(c, 1), :].broadcast_to([P, W])).then_inc(filled[s], 16)

                def store(c, j, s):
                    sp.wait_ge(normed, c + 1)
                    sp.sem_inc(own, 1)
                    sp.dma_start(rows4(D["x3"], c), xo[:, s, 0, :, :]).then_inc(stored[s], 16)
                    sp.dma_start(rows4(D["x3"], c + CH), xo[:, s, 1, :, :]).then_inc(stored[s], 16)
                pipeline(Steps(sp, own), CH, NS, (6, store), (0, load))
                for s in range(NS):
                    sp.wait_ge(stored[s], 32 * uses(s))

            @block.gpsimd
            def _(pool):
                def gather(c, j, s):
                    if not first(j):
                        pool.wait_ge(added, c + 1 - NS)
                        pool.wait_ge(copied_x, c + 1 - NS)
                    pool.wait_ge(filled[s], 48 * (j + 1))
                    pool.sem_inc(own, 1)
                    gather4(pool, xs[:, s, :, :], D["x2"], ix[:, s, :], IX_SRC_S, got[s])
                    gather4(pool, xd[:, s, :, :], D["x2"], ix[:, s, :], IX_DST_S, got[s])
                pipeline(Steps(pool, own), CH, NS, (0, gather))

            @block.vector
            def _(v):
                st = Steps(v, own_v)

                def differ(c, j, s):
                    v.wait_ge(got[s], 128 * (j + 1))
                    if not first(j):
                        v.wait_ge(normed, c + 1 - NS)
                    v.memset(mask[:, s, 0:G], 1.0).then_inc(own_v, one(st))
                    v.tensor_copy(mask[:, s, G:2 * G], fl[:, s, :].rearrange("p (g k) -> p g k", k=NFL)
                                         [:, :, FL_REAL]).then_inc(own_v, one(st))
                    v.tensor_tensor(df[:, s, :, :], xs[:, s, :, :], xd[:, s, :, :], ALU.subtract).then_inc(own_v, one(st))
                    v.tensor_scalar(pen[:, s, :], keep[:, s, :], -1.0, -NEG, ALU.add, ALU.mult).then_inc(own_v, one(st))
                    v.wait_ge(own_v, steps(st))
                    v.sem_inc(differed, 1)

                def copy(c, j, s):
                    v.wait_ge(turned, c + 1)
                    v.tensor_copy(dt_[:, s, :], tb[:, :]).then_inc(copied_d, 1)

                def scan(c, j, s):
                    v.wait_ge(mixed, c + 1)
                    start = NEG if first(j) and s == 0 else agg[:, (s - 1) % NS, W - 1:W]
                    v.tensor_tensor_scan(out=agg[:, s, :], data0=pen[:, s, :], data1=pm[:, :], initial=start,
                                                op0=ALU.add, op1=ALU.max).then_inc(own_v, one(st))
                    v.wait_ge(own_v, steps(st))
                    v.sem_inc(scanned, 1)
                    v.tensor_scalar(ab[:, :], agg[:, s, :], env.col["L2_gnn_b"], None, ALU.add).then_inc(own_v, one(st))
                    v.wait_ge(own_v, steps(st))
                    v.tensor_tensor(fin[:, :], ab[:, :], ab[:, :], ALU.subtract).then_inc(own_v, one(st))
                    if not first(j):
                        v.wait_ge(returned, c + 1 - NS)
                    v.memset(am[:, s, :], 0.0).then_inc(own_v, one(st))
                    v.wait_ge(own_v, steps(st))
                    v.tensor_scalar(fin[:, :], fin[:, :], 0.0, None, ALU.is_equal).then_inc(own_v, one(st))
                    v.wait_ge(own_v, steps(st))
                    v.sem_inc(own_v, one(st))
                    v.copy_predicated(am[:, s, :], fin[:, :].bitcast(i32), ab[:, :]).then_inc(own_v, one(st))
                    v.wait_ge(own_v, steps(st))
                    v.sem_inc(maxed, 1)

                def measure(c, j, s):
                    v.wait_ge(returned, c + 1)
                    v.tensor_tensor(vv[:, s, 0:G, :], tr[s % 2][:, :].rearrange("p (g f) -> p g f", g=G),
                                           xd[:, s, :, :], ALU.add).then_inc(own_v, one(st))
                    v.wait_ge(own_v, steps(st))
                    v.sem_inc(added, 1)
                    v.wait_ge(copied_x, c + 1)
                    moments(v, st, vv[:, s], stats, mv)
                    v.wait_ge(own_v, steps(st))
                    v.sem_inc(measured, 1)

                def finish(c, j, s):
                    v.wait_ge(rooted, c + 1)
                    if not first(j):
                        v.wait_ge(stored[s], 32 * j)
                    norm_apply(v, st, vv[:, s], mv, sd[:, :], xo[:, s, :, :, :].rearrange("p k g f -> p (k g) f"),
                               mask[:, s, :])
                    v.wait_ge(own_v, steps(st))
                    v.sem_inc(normed, 1)
                pipeline(st, CH, NS, (0, differ), (1, scan), (3, finish), (0, copy), (2, measure))

            @block.scalar
            def _(act):
                st = Steps(act, own_a)

                def copy(c, j, s):
                    act.wait_ge(turned, c + 1)
                    act.activation(xt[:, s, :], ta[:, :], ACT.Copy)
                    if not first(j):
                        act.wait_ge(normed, c + 1 - NS)
                    act.activation(vv[:, s, G:2 * G, :], xs[:, s, :, :], ACT.Copy).then_inc(copied_x, 1)

                def root(c, j, s):
                    act.wait_ge(measured, c + 1)
                    act.activation(sd[:, :], mv[:, :, 1], ACT.Sqrt, bias=env.eps[:, 2:3]).then_inc(rooted, 1)
                pipeline(st, CH, NS, (0, copy), (2, root))

            @block.tensor
            def _(pe):
                def turn(c, j, s):
                    pe.wait_ge(differed, c + 1)
                    if not (first(j) and s == 0):
                        pe.wait_ge(copied_x, c)
                        pe.wait_ge(copied_d, c)
                    transpose4(pe, env, ta, xd[:, s, :, :])
                    transpose4(pe, env, tb, df[:, s, :, :]).then_inc(turned, 1)

                def mix(c, j, s):
                    pe.wait_ge(copied_x, c + 1)
                    pe.wait_ge(copied_d, c + 1)
                    if not (first(j) and s == 0):
                        pe.wait_ge(scanned, c)
                    pe.matmul(pm[:, :], env.wi, xt[:, s, :], start=True, stop=False)
                    pe.matmul(pm[:, :], env.wj, dt_[:, s, :], start=False, stop=True).then_inc(mixed, 1)

                def back(c, j, s):
                    pe.wait_ge(maxed, c + 1)
                    if not (first(j) and s < 2):
                        pe.wait_ge(added, c - 1)
                    for g in range(G):
                        last = pe.transpose(tr[s % 2][:, g * F:(g + 1) * F], am[:, s, g * P:(g + 1) * P], env.ident[:, :])
                    last.then_inc(returned, 1)
                pipeline(Steps(pe, own), CH, NS, (0, turn), (1, back), (0, mix))


def parts_of(c):
    return TP if isinstance(c, int) and c == DC - 1 else P


def node_rows(ap, c):
    if isinstance(c, int) and c == DC - 1:
        return ap[c * W:N, :].rearrange("(p g) f -> p (g f)", g=G)
    return ap[bass.ds(c * W, W), :].rearrange("(p g) f -> p (g f)", g=G)


def columns(ap, c, wide=W, base=0):
    return ap[:, bass.ds(c * W + base, wide)]


def dense_front(nc, env, A, D):
    with ExitStack() as ctx:
        m = Mem(nc, ctx, "df")
        x, xb, free = m.sb("x", NS, G, F), m.sb("xb", NS, G, F), m.sb("free", DC * G)
        xt, hid, x3 = m.sb("xt", NS, W), m.sb("hid", NS, W), m.sb("x3", NS, G, F)
        x3t, h = m.sb("x3t", NS, W), m.sb("h", NS, W)
        va, stats, mv, sd = m.sb("va", 2, G, F), m.sb("stats", 2, G, 6), m.sb("mv", 2, G, 2), m.sb("sd", 2, G)
        vv, stats2 = m.sb("vv", NS, G, F), m.sb("stats2", 2, G, 6)
        mv2, sd2, off2 = m.sb("mv2", NS, G, 2), m.sb("sd2", NS, G), m.sb("off2", NS, G)
        tx, ph, po, tx3, pa = (m.ps(n) for n in ("tx", "ph", "po", "tx3", "pa"))
        (filled, stored, h_stored, masked, with_bias, turned, copied, hidden, relued, projected, added, measured,
         rooted, measured2, rooted2, scaled, normed, turned3, copied3, mapped, biased, own,
         sampled, inverted, mixed, sampled2, inverted2, zeroed, cols_in, keyed, keys_out, keys_in, bounded,
         bounds_out, rest_in, rest_got, rest_out) = m.sems(
            "filled* stored* h_stored* masked with_bias turned copied hidden relued projected added measured rooted "
            "measured2 rooted2 scaled normed turned3 copied3 mapped biased own sampled inverted mixed sampled2 "
            "inverted2 zeroed cols_in keyed keys_out keys_in* bounded* bounds_out* rest_in rest_got rest_out")
        cf, ci = m.sb("cf", T, 4), m.sb("ci", T, 2, dt=i32)
        key, bounds = m.sb("key", NS, 2, dt=i32), m.sb("bounds", NS, 2, 4, dt=i32)
        more = T - DC
        key_r, bounds_r = m.sb("key_r", more, 2, dt=i32), m.sb("bounds_r", more, 2, 4, dt=i32)
        kv = D["keys_i"].rearrange("p (t k) -> p t k", k=2)
        bv = D["edge_bounds"].rearrange("p (t k b) -> p t k b", k=2, b=4)
        freev = D["free"].rearrange("(c p g) -> p c g", c=DC, g=G)
        with nc.Block() as block:
            @block.sync
            def _(sp):
                def load(c, j, s):
                    n = parts_of(c)
                    if not first(j):
                        sp.wait_ge(turned, c + 1 - NS)
                        sp.wait_ge(with_bias, c + 1 - NS)
                        sp.sem_inc(own, 1)
                    sp.dma_start(x[0:n, s, :, :].rearrange("p g f -> p (g f)"), node_rows(A["x"], c))\
                        .then_inc(filled[s], 16)

                def store(c, j, s):
                    n = parts_of(c)
                    sp.wait_ge(normed, c + 1)
                    sp.sem_inc(own, 1)
                    sp.dma_start(node_rows(D["x3n"], c), x3[0:n, s, :, :].rearrange("p g f -> p (g f)"))\
                        .then_inc(stored[s], 16)

                def store_h(c, j, s):
                    n = parts_of(c)
                    sp.wait_ge(biased, c + 1)
                    sp.sem_inc(own, 1)
                    sp.dma_start(columns(D["za"], c, n * G), h[:, s, 0:n * G]).then_inc(h_stored[s], 16)

                def load_keys(t, j, s):
                    if not first(j):
                        sp.wait_ge(bounded[s], 32 * j)
                    sp.sem_inc(own, 1)
                    sp.dma_start(key[:, s, :], kv[:, t, :]).then_inc(keys_in[s], 16)

                def store_bounds(t, j, s):
                    sp.wait_ge(bounded[s], 32 * (j + 1))
                    sp.sem_inc(own, 1)
                    sp.dma_start(bv[:, t, :, :].rearrange("p k b -> p (k b)"),
                                 bounds[:, s, :, :].rearrange("p k b -> p (k b)")).then_inc(bounds_out[s], 16)
                sp.dma_start(cf[:, :, :].rearrange("p t k -> p (t k)"), D["cols_s"]).then_inc(cols_in, 16)
                sp.dma_start(free[:, :].rearrange("p (c g) -> p c g", g=G), freev).then_inc(masked, 16)
                sp.wait_ge(keyed, 1)
                sp.dma_start(D["keys_i"], ci[:, :, :].rearrange("p t k -> p (t k)")).then_inc(keys_out, 16)
                sp.wait_ge(keys_out, 16)
                pipeline(Steps(sp, own), DC, NS, (0, load), (0, load_keys), (3, store_bounds), (7, store), (9, store_h))
                for s in range(NS):
                    sp.wait_ge(bounds_out[s], 16 * uses(s, DC))
                    sp.wait_ge(stored[s], 16 * uses(s, DC))
                    sp.wait_ge(h_stored[s], 16 * uses(s, DC))

            @block.gpsimd
            def _(pool):
                def offset(c, j, s):
                    n = parts_of(c)
                    pool.wait_ge(filled[s], 16 * (j + 1))
                    if not first(j):
                        pool.wait_ge(added, c + 1 - NS)
                    pool.tensor_tensor(xb[0:n, s, :, :], x[0:n, s, :, :], spread(env.bc["L0_gnn_b2"][0:n, :]),
                                       ALU.add).then_inc(with_bias, 1)

                def gather(t, j, s):
                    pool.wait_ge(keys_in[s], 16 * (j + 1))
                    if not first(j):
                        pool.wait_ge(bounds_out[s], 16 * j)
                    pool.sem_inc(own, 1)
                    for k in range(2):
                        pool.indirect_dma_start(
                            out=bounds[:, s, k, :], out_offset=None, in_=D["bounds"][:, :],
                            in_offset=bass.IndirectOffsetOnAxis(ap=key[:, s, k:k + 1], axis=0))\
                            .then_inc(bounded[s], 16)
                pipeline(Steps(pool, own), DC, NS, (0, offset), (0, gather))
                pool.dma_start(key_r[:, :, :], kv[:, DC:T, :]).then_inc(rest_in, 16)
                pool.wait_ge(rest_in, 16)
                pool.sem_inc(own, 1)
                for t in range(more):
                    for k in range(2):
                        pool.indirect_dma_start(
                            out=bounds_r[:, t, k, :], out_offset=None, in_=D["bounds"][:, :],
                            in_offset=bass.IndirectOffsetOnAxis(ap=key_r[:, t, k:k + 1], axis=0))\
                            .then_inc(rest_got, 16)
                pool.wait_ge(rest_got, 32 * more)
                pool.dma_start(bv[:, DC:T, :, :].rearrange("p t k b -> p (t k b)"),
                               bounds_r[:, :, :, :].rearrange("p t k b -> p (t k b)")).then_inc(rest_out, 16)
                pool.wait_ge(rest_out, 16)

            @block.vector
            def _(v):
                def add(c, j, s):
                    n, b = parts_of(c), s % 2
                    v.wait_ge(projected, c + 1)
                    v.wait_ge(with_bias, c + 1)
                    v.tensor_tensor(va[0:n, b, :, :], po[0:n, :].rearrange("p (g f) -> p g f", g=G),
                                    xb[0:n, s, :, :], ALU.add).then_inc(added, 1)

                def sample(c, j, s):
                    n, b = parts_of(c), s % 2
                    v.wait_ge(added, c + 1)
                    for g in range(G):
                        last = v.bn_stats(stats[0:n, b, g, :], va[0:n, b, g, :])
                    last.then_inc(sampled, 1)

                def measure(c, j, s):
                    n, b = parts_of(c), s % 2
                    v.wait_ge(sampled, c + 1)
                    v.sem_inc(own, 1)
                    for g in range(G):
                        last = v.bn_aggr(mv[0:n, b, g, :], stats[0:n, b, g, :])
                    last.then_inc(measured, 1)

                def invert(c, j, s):
                    n, b = parts_of(c), s % 2
                    v.wait_ge(rooted, c + 1)
                    v.reciprocal(sd[0:n, b, :], sd[0:n, b, :]).then_inc(inverted, 1)

                def mix(c, j, s):
                    n, b = parts_of(c), s % 2
                    v.wait_ge(inverted, c + 1)
                    for g in range(G):
                        last = v.scalar_tensor_tensor(
                            out=vv[0:n, s, g, :], in0=va[0:n, b, g, :], scalar=sd[0:n, b, g:g + 1],
                            in1=env.h0[0:n, :], op0=ALU.mult, op1=ALU.add)
                    last.then_inc(mixed, 1)

                def sample2(c, j, s):
                    n, b = parts_of(c), s % 2
                    v.wait_ge(mixed, c + 1)
                    for g in range(G):
                        last = v.bn_stats(stats2[0:n, b, g, :], vv[0:n, s, g, :])
                    last.then_inc(sampled2, 1)

                def measure2(c, j, s):
                    n, b = parts_of(c), s % 2
                    v.wait_ge(sampled2, c + 1)
                    v.sem_inc(own, 1)
                    for g in range(G):
                        last = v.bn_aggr(mv2[0:n, s, g, :], stats2[0:n, b, g, :])
                    last.then_inc(measured2, 1)

                def invert2(c, j, s):
                    n = parts_of(c)
                    v.wait_ge(rooted2, c + 1)
                    v.reciprocal(sd2[0:n, s, :], sd2[0:n, s, :]).then_inc(inverted2, 1)

                def mask(c, j, s):
                    n = parts_of(c)
                    v.wait_ge(inverted2, c + 1)
                    v.tensor_tensor(sd2[0:n, s, :], sd2[0:n, s, :], free[0:n, bass.ds(c * G, G)], ALU.mult)\
                        .then_inc(zeroed, 1)

                def offset(c, j, s):
                    n = parts_of(c)
                    v.wait_ge(zeroed, c + 1)
                    v.scalar_tensor_tensor(out=off2[0:n, s, :], in0=mv2[0:n, s, :, 0], scalar=-1.0,
                                           in1=sd2[0:n, s, :], op0=ALU.mult, op1=ALU.mult).then_inc(scaled, 1)
                v.wait_ge(cols_in, 16)
                v.tensor_copy(ci[:, :, :], cf[:, :, 0:2]).then_inc(keyed, 1)
                v.wait_ge(masked, 16)
                pipeline(Steps(v, own), DC, NS, (3, invert), (4, invert2), (2, add), (3, mix), (4, mask), (2, sample),
                         (3, sample2), (4, offset), (2, measure), (3, measure2))

            @block.scalar
            def _(act):
                def copy(c, j, s):
                    n = parts_of(c) * G
                    act.wait_ge(turned, c + 1)
                    act.activation(xt[:, s, 0:n], tx[:, 0:n], ACT.Copy).then_inc(copied, 1)

                def relu(c, j, s):
                    n = parts_of(c) * G
                    act.wait_ge(hidden, c + 1)
                    act.activation(hid[:, s, 0:n], ph[:, 0:n], ACT.Relu, bias=env.col["L0_gnn_b1"]).then_inc(relued, 1)

                def root(c, j, s):
                    n = parts_of(c)
                    act.wait_ge(measured, c + 1)
                    act.activation(sd[0:n, s % 2, :], mv[0:n, s % 2, :, 1], ACT.Sqrt, scale=0.25,
                                   bias=env.eps[0:n, 0:1]).then_inc(rooted, 1)

                def root2(c, j, s):
                    n = parts_of(c)
                    act.wait_ge(measured2, c + 1)
                    act.activation(sd2[0:n, s, :], mv2[0:n, s, :, 1], ACT.Sqrt, scale=1.0 + LN_EPS,
                                   bias=env.eps[0:n, 1:2]).then_inc(rooted2, 1)

                def norm(c, j, s):
                    n = parts_of(c)
                    act.wait_ge(scaled, c + 1)
                    if not first(j):
                        act.wait_ge(stored[s], 16 * j)
                    for g in range(G):
                        last = act.activation(x3[0:n, s, g, :], vv[0:n, s, g, :], ACT.Identity,
                                              scale=sd2[0:n, s, g:g + 1], bias=off2[0:n, s, g:g + 1])
                    last.then_inc(normed, 1)

                def copy3(c, j, s):
                    n = parts_of(c) * G
                    act.wait_ge(turned3, c + 1)
                    if not first(j):
                        act.wait_ge(mapped, c + 1 - NS)
                    act.activation(x3t[:, s, 0:n], tx3[:, 0:n], ACT.Copy).then_inc(copied3, 1)

                def bias(c, j, s):
                    n = parts_of(c) * G
                    act.wait_ge(mapped, c + 1)
                    if not first(j):
                        act.wait_ge(h_stored[s], 16 * j)
                    act.activation(h[:, s, 0:n], pa[:, 0:n], ACT.Identity, bias=env.col["L3_gnn_b_atom"])\
                        .then_inc(biased, 1)
                pipeline(Steps(act, own), DC, NS, (4, root2), (3, root), (5, norm), (7, bias), (6, copy3), (1, relu),
                         (0, copy))

            @block.tensor
            def _(pe):
                def turn(c, j, s):
                    n = parts_of(c)
                    pe.wait_ge(filled[s], 16 * (j + 1))
                    if not (first(j) and s == 0):
                        pe.wait_ge(copied, c)
                    transpose4(pe, env, tx, x[0:n, s, :, :], n).then_inc(turned, 1)

                def hide(c, j, s):
                    n = parts_of(c) * G
                    pe.wait_ge(copied, c + 1)
                    if not (first(j) and s == 0):
                        pe.wait_ge(relued, c)
                    pe.matmul(ph[:, 0:n], env.w["L0_gnn_W1"], xt[:, s, 0:n], start=True, stop=True).then_inc(hidden, 1)

                def project(c, j, s):
                    n = parts_of(c)
                    pe.wait_ge(relued, c + 1)
                    if not (first(j) and s == 0):
                        pe.wait_ge(added, c)
                    to_rows4(pe, po, hid[:, s, :], env.w["L0_gnn_W2"], n).then_inc(projected, 1)

                def turn3(c, j, s):
                    n = parts_of(c)
                    pe.wait_ge(normed, c + 1)
                    if not (first(j) and s == 0):
                        pe.wait_ge(copied3, c)
                    transpose4(pe, env, tx3, x3[0:n, s, :, :], n).then_inc(turned3, 1)

                def atom(c, j, s):
                    n = parts_of(c) * G
                    pe.wait_ge(copied3, c + 1)
                    if not (first(j) and s == 0):
                        pe.wait_ge(biased, c)
                    pe.matmul(pa[:, 0:n], env.w["L3_gnn_W_atom"], x3t[:, s, 0:n], start=True, stop=True)\
                        .then_inc(mapped, 1)
                pipeline(Steps(pe, own), DC, NS, (7, atom), (6, turn3), (2, project), (1, hide), (0, turn))


def slot_states(nc, env, D):
    n3 = 3 * CH
    with ExitStack() as ctx:
        m = Mem(nc, ctx, "ss")
        x, xt, o, ot = m.sb("x", NS, G, F), m.sb("xt", NS, W), m.sb("o", NS, G, F), m.sb("ot", NS, W)
        tx, pr, pt = (m.ps(n) for n in ("tx", "pr", "pt"))
        filled, stored, turned, copied, mapped, rows_out, cols_out, own = m.sems(
            "filled* stored* turned copied mapped rows_out cols_out own")
        bcol = {0: env.col["L3_gnn_b_atom"], 2: env.col["L3_gnn_b_bond"]}
        wts = {0: env.w["L3_gnn_W_atom"], 1: env.w["L3_gnn_W_atom"], 2: env.w["L3_gnn_W_bond"]}

        def run(kind):
            source = D["x3"] if kind == 0 else D["edges"][:, 0:F]
            target = D["hd"] if kind == 0 else D["ea"]
            with nc.Block() as block:
                @block.sync
                def _(sp):
                    def load(c, j, s):
                        if not first(j):
                            sp.wait_ge(turned, base + c + 1 - NS)
                            sp.sem_inc(own, 1)
                        sp.dma_start(x[:, s, :, :], rows4(source, c)).then_inc(filled[s], 16)

                    def store(c, j, s):
                        sp.wait_ge(cols_out, base + c + 1)
                        sp.sem_inc(own, 1)
                        sp.dma_start(columns(target, c), ot[:, s, :]).then_inc(stored[s], 16)
                    pipeline(Steps(sp, own), count, NS, (0, load), (NS, store))
                    for s in range(NS):
                        sp.wait_ge(stored[s], 16 * (uses_before[s] + uses(s, count)))

                @block.scalar
                def _(act):
                    def copy(c, j, s):
                        act.wait_ge(turned, base + c + 1)
                        act.activation(xt[:, s, :], tx[:, :], ACT.Copy).then_inc(copied, 1)
                    pipeline(Steps(act, own), count, NS, (0, copy))

                @block.vector
                def _(v):
                    def bias(c, j, s):
                        v.wait_ge(mapped, base + c + 1)
                        if not first(j):
                            v.wait_ge(stored[s], 16 * (uses_before[s] + j))
                        v.tensor_scalar(ot[:, s, :], pt[:, :], bcol[kind], None, ALU.add).then_inc(cols_out, 1)
                    pipeline(Steps(v, own), count, NS, (1, bias))

                @block.tensor
                def _(pe):
                    def turn(c, j, s):
                        pe.wait_ge(filled[s], 16 * (uses_before[s] + j + 1))
                        if not (first(j) and s == 0):
                            pe.wait_ge(copied, base + c)
                        transpose4(pe, env, tx, x[:, s, :, :]).then_inc(turned, 1)

                    def apply(c, j, s):
                        pe.wait_ge(copied, base + c + 1)
                        if not (first(j) and s == 0):
                            pe.wait_ge(cols_out, base + c)
                        pe.matmul(pt[:, :], wts[kind], xt[:, s, :], start=True, stop=True).then_inc(mapped, 1)
                    pipeline(Steps(pe, own), count, NS, (0, turn), (1, apply))
        base, uses_before = 0, [0] * NS
        count = 2 * CH
        run(0)
        base += count
        uses_before = [uses(s, count) for s in range(NS)]
        count = CH
        run(2)


def rows_of_states(nc, env, D, tag, src, norm):
    with ExitStack() as ctx:
        m = Mem(nc, ctx, tag)
        z, h, r = m.sb("z", NS, W), m.sb("h", NS, W), m.sb("r", NS, G, F)
        tr = [m.ps("tr0"), m.ps("tr1")]
        filled, stored, made, turned, copied, own = m.sems("filled* stored* made turned copied own")
        count = 2 * CH
        hh = z if norm is None else h
        with nc.Block() as block:
            @block.sync
            def _(sp):
                def load(c, j, s):
                    if not first(j):
                        sp.wait_ge(copied, c + 1 - NS)
                        sp.sem_inc(own, 1)
                    sp.dma_start(z[:, s, :], src(c)).then_inc(filled[s], 16)

                def store(c, j, s):
                    sp.wait_ge(copied, c + 1)
                    sp.sem_inc(own, 1)
                    sp.dma_start(rows4(D["hr"], c), r[:, s, :, :]).then_inc(stored[s], 16)
                    if norm is not None:
                        sp.dma_start(columns(D["hd"], c), hh[:, s, :]).then_inc(stored[s], 16)
                pipeline(Steps(sp, own), count, NS, (0, load), (NS, store))
                for s in range(NS):
                    sp.wait_ge(stored[s], (16 if norm is None else 32) * uses(s, count))

            if norm is not None:
                @block.scalar
                def _(act):
                    def make(c, j, s):
                        act.wait_ge(filled[s], 16 * (j + 1))
                        if not first(j):
                            act.wait_ge(stored[s], 32 * j)
                        act.activation(h[:, s, :], z[:, s, :], ACT.Relu, scale=norm[0], bias=norm[1]).then_inc(made, 1)
                    pipeline(Steps(act, own), count, NS, (0, make))

            @block.tensor
            def _(pe):
                def turn(c, j, s):
                    if norm is None:
                        pe.wait_ge(filled[s], 16 * (j + 1))
                    else:
                        pe.wait_ge(made, c + 1)
                    if not (first(j) and s < 2):
                        pe.wait_ge(copied, c - 1)
                    for g in range(G):
                        last = pe.transpose(tr[s % 2][:, g * F:(g + 1) * F], hh[:, s, g * P:(g + 1) * P],
                                            env.ident[:, :])
                    last.then_inc(turned, 1)
                pipeline(Steps(pe, own), count, NS, (0, turn))

            @block.vector
            def _(v):
                def copy(c, j, s):
                    v.wait_ge(turned, c + 1)
                    if not first(j):
                        v.wait_ge(stored[s], (16 if norm is None else 32) * j)
                    v.tensor_copy(r[:, s, :, :], tr[s % 2][:, :].rearrange("p (g f) -> p g f", g=G))\
                        .then_inc(copied, 1)
                pipeline(Steps(v, own), count, NS, (0, copy))


def aggregate_states(nc, env, D, i, z):
    with ExitStack() as ctx:
        m = Mem(nc, ctx, f"ag{i}")
        ix, keep = m.sb("ix", NS, G * NIX, dt=i32), m.sb("keep", NS, W)
        hs, hd, ea = m.sb("hs", NS, G, F), m.sb("hd", NS, W), m.sb("ea", NS, W)
        ms, agg, zd, zs = m.sb("ms", NS, W), m.sb("agg", NS, W), m.sb("zd", NS, W), m.sb("zs", NS, W)
        ts = [m.ps("ts0"), m.ps("ts1")]
        filled, got, stored, turned, scaled, summed, relued, done, own_v, own = m.sems(
            "filled* got* stored* turned scaled summed relued done own_v own")
        iv, fv, kv = views(D)
        with nc.Block() as block:
            @block.sync
            def _(sp):
                def load(c, j, s):
                    if not first(j):
                        sp.wait_ge(done, c + 1 - NS)
                        sp.sem_inc(own, 1)
                    sp.dma_start(ix[:, s, :], iv[:, c, :]).then_inc(filled[s], 16)
                    sp.dma_start(keep[:, s, :], kv[bass.ds(c, 1), :].broadcast_to([P, W])).then_inc(filled[s], 16)
                    sp.dma_start(hd[:, s, :], columns(D["hd"], c)).then_inc(filled[s], 16)
                    sp.dma_start(ea[:, s, :], columns(D["ea"], c)).then_inc(filled[s], 16)

                def store(c, j, s):
                    sp.wait_ge(done, c + 1)
                    sp.sem_inc(own, 1)
                    sp.dma_start(columns(z, c, W, SLOT0), zd[:, s, :]).then_inc(stored[s], 16)
                    sp.dma_start(columns(z, c, W, SLOT0 + EP), zs[:, s, :]).then_inc(stored[s], 16)
                pipeline(Steps(sp, own), CH, NS, (0, load), (NS, store))
                for s in range(NS):
                    sp.wait_ge(stored[s], 32 * uses(s))

            @block.gpsimd
            def _(pool):
                def gather(c, j, s):
                    pool.wait_ge(filled[s], 64 * (j + 1))
                    pool.sem_inc(own, 1)
                    gather4(pool, hs[:, s, :, :], D["hr"], ix[:, s, :], IX_SRC_D, got[s])
                pipeline(Steps(pool, own), CH, NS, (0, gather))

            @block.tensor
            def _(pe):
                def turn(c, j, s):
                    pe.wait_ge(got[s], 64 * (j + 1))
                    if not (first(j) and s < 2):
                        pe.wait_ge(scaled, c - 1)
                    transpose4(pe, env, ts[s % 2], hs[:, s, :, :]).then_inc(turned, 1)
                pipeline(Steps(pe, own), CH, NS, (0, turn))

            @block.scalar
            def _(act):
                def relu(c, j, s):
                    act.wait_ge(summed, c + 1)
                    act.activation(ms[:, s, :], ms[:, s, :], ACT.Relu).then_inc(relued, 1)
                pipeline(Steps(act, own), CH, NS, (0, relu))

            @block.vector
            def _(v):
                st = Steps(v, own_v)

                def add(c, j, s):
                    v.wait_ge(turned, c + 1)
                    if not first(j):
                        v.wait_ge(stored[s], 32 * j)
                    v.tensor_tensor(ms[:, s, :], ts[s % 2][:, :], ea[:, s, :], ALU.add).then_inc(own_v, one(st))
                    v.wait_ge(own_v, steps(st))
                    v.sem_inc(summed, 1)
                    v.tensor_scalar(zs[:, s, :], ts[s % 2][:, :], env.onep[:, i:i + 1], None, ALU.mult).then_inc(own_v, one(st))
                    v.wait_ge(own_v, steps(st))
                    v.sem_inc(scaled, 1)

                def scan(c, j, s):
                    v.wait_ge(relued, c + 1)
                    start = 0.0 if first(j) and s == 0 else agg[:, (s - 1) % NS, W - 1:W]
                    v.tensor_tensor_scan(out=agg[:, s, :], data0=keep[:, s, :], data1=ms[:, s, :],
                                                initial=start, op0=ALU.mult, op1=ALU.add).then_inc(own_v, one(st))
                    v.wait_ge(own_v, steps(st))
                    v.scalar_tensor_tensor(out=zd[:, s, :], in0=hd[:, s, :], scalar=env.onep[:, i:i + 1],
                                                  in1=agg[:, s, :], op0=ALU.mult, op1=ALU.add).then_inc(own_v, one(st))
                    v.wait_ge(own_v, steps(st))
                    v.sem_inc(done, 1)
                pipeline(st, CH, NS, (0, add), (1, scan))


def norm_constants(nc, env, tag, halves, bias, gain, offset, nodes, slots, out):
    with ExitStack() as ctx:
        m = Mem(nc, ctx, tag)
        mv, t, sm = m.sb("mv", halves, 2), m.sb("t", 4, halves), m.sb("sm", halves, 2)
        measured, rooted, own = m.sems("measured rooted own")
        with nc.Block() as block:
            @block.vector
            def _(v):
                st = Steps(v, own)

                def do(ins):
                    ins.then_inc(own, one(st))
                    v.wait_ge(own, steps(st))
                for k in range(halves):
                    v.bn_aggr(mv[:, k, :], nodes[:, k, :, :]).then_inc(own, one(st))
                    v.reduce_sum(sm[:, k, 0:1], slots[:, k, :, 0], axis=mybir.AxisListType.X).then_inc(own, one(st))
                    v.reduce_sum(sm[:, k, 1:2], slots[:, k, :, 1], axis=mybir.AxisListType.X).then_inc(own, one(st))
                v.wait_ge(own, steps(st))
                do(v.tensor_scalar(sm[:, :, :], sm[:, :, :], 1.0 / N, None, ALU.mult))
                do(v.tensor_tensor(t[:, 0, :], mv[:, :, 0], mv[:, :, 0], ALU.mult))
                do(v.tensor_tensor(t[:, 0, :], t[:, 0, :], mv[:, :, 1], ALU.add))
                do(v.tensor_tensor(t[:, 0, :], t[:, 0, :], sm[:, :, 1], ALU.add))
                do(v.tensor_tensor(t[:, 1, :], mv[:, :, 0], sm[:, :, 0], ALU.add))
                do(v.tensor_tensor(t[:, 2, :], t[:, 1, :], t[:, 1, :], ALU.mult))
                do(v.tensor_tensor(t[:, 0, :], t[:, 0, :], t[:, 2, :], ALU.subtract))
                do(v.tensor_scalar(t[:, 0, :], t[:, 0, :], BN_EPS, None, ALU.add))
                v.wait_ge(own, steps(st))
                v.sem_inc(measured, 1)
                v.wait_ge(rooted, 1)
                do(v.reciprocal(t[:, 2, :], t[:, 3, :]))
                do(v.tensor_tensor(out[:, 0, 0:halves], t[:, 2, :], gain, ALU.mult))
                do(v.tensor_tensor(t[:, 1, :], t[:, 1, :], bias, ALU.add))
                do(v.tensor_tensor(t[:, 1, :], bias, t[:, 1, :], ALU.subtract))
                do(v.tensor_tensor(t[:, 1, :], t[:, 1, :], out[:, 0, 0:halves], ALU.mult))
                do(v.tensor_tensor(out[:, 1, 0:halves], t[:, 1, :], offset, ALU.add))

            @block.scalar
            def _(act):
                act.wait_ge(measured, 1)
                act.activation(t[:, 3, :], t[:, 0, :], ACT.Sqrt).then_inc(rooted, 1)


def column_pass(nc, env, D, i, which, slots, source, target, prev, norm1, stats):
    tag = f"p{which}{'s' if slots else 'n'}{i}"
    count = 2 * CH if slots else DC
    base = SLOT0 if slots else 0
    w1 = env.w1 if slots else env.w1e
    halves = 2 if which == "a" else 1
    with ExitStack() as ctx:
        m = Mem(nc, ctx, tag)
        z, wt = m.sb("z", NS, W), m.sb("wt", NS, W)
        h = m.sb("h", NS, W) if prev is not None else z
        y, z2, scr = m.sb("y", NS, 2, W), m.sb("z2", NS, W), m.sb("scr", 4, W)
        p1 = [[m.ps(f"p1{a}{b}") for b in range(2)] for a in range(2)]
        p2 = [m.ps(f"p2{a}") for a in range(2)]
        filled, stored, made, multiplied, relued, projected, done, own_v, own_a, own = m.sems(
            "filled* stored* made multiplied relued projected done own_v own_a own")

        def wide(c):
            return W if slots else parts_of(c) * G
        loads = 32 if slots else 16
        with nc.Block() as block:
            @block.sync
            def _(sp):
                def load(c, j, s):
                    if not first(j):
                        sp.wait_ge(done, c + 1 - NS)
                        sp.sem_inc(own, 1)
                    sp.dma_start(z[:, s, 0:wide(c)], columns(source, c, wide(c), base)).then_inc(filled[s], 16)
                    if slots:
                        sp.dma_start(wt[:, s, :], D["weights"].rearrange("(c w) -> c w", w=W)[bass.ds(c, 1), :]
                                     .broadcast_to([P, W])).then_inc(filled[s], 16)

                def store(c, j, s):
                    sp.wait_ge(done, c + 1)
                    sp.sem_inc(own, 1)
                    sp.dma_start(columns(target, c, wide(c), base), z2[:, s, 0:wide(c)]).then_inc(stored[s], 16)
                if which == "a":
                    pipeline(Steps(sp, own), count, NS, (0, load))
                else:
                    pipeline(Steps(sp, own), count, NS, (0, load), (NS, store))
                    for s in range(NS):
                        sp.wait_ge(stored[s], 16 * uses(s, count))

            @block.scalar
            def _(act):
                st = Steps(act, own_a)

                def make(c, j, s):
                    act.wait_ge(filled[s], loads * (j + 1))
                    if not first(j):
                        act.wait_ge(multiplied, c + 1 - NS)
                    act.activation(h[:, s, 0:wide(c)], z[:, s, 0:wide(c)], ACT.Relu, scale=prev[0], bias=prev[1])\
                        .then_inc(made, 1)

                def relu(c, j, s):
                    n = wide(c)
                    act.wait_ge(multiplied, c + 1)
                    if not first(j):
                        act.wait_ge(projected, c + 1 - NS)
                    for k in range(2):
                        act.activation(y[:, s, k, 0:n], p1[s % 2][k][:, 0:n], ACT.Relu,
                                              scale=norm1[:, 0, k:k + 1], bias=norm1[:, 1, k:k + 1]).then_inc(own_a, one(st))
                    act.wait_ge(own_a, steps(st))
                    act.sem_inc(relued, 1)
                stages = []
                if prev is not None:
                    stages.append((0, make))
                if which == "b":
                    stages.append((1, relu))
                if stages:
                    pipeline(st, count, NS, *stages)

            @block.tensor
            def _(pe):
                def multiply(c, j, s):
                    n = wide(c)
                    if prev is None:
                        pe.wait_ge(filled[s], loads * (j + 1))
                    else:
                        pe.wait_ge(made, c + 1)
                    if not (first(j) and s < 2):
                        pe.wait_ge(done if which == "a" else relued, c - 1)
                    for k in range(2):
                        last = pe.matmul(p1[s % 2][k][:, 0:n], w1[:, i, k * F:(k + 1) * F], h[:, s, 0:n],
                                         start=True, stop=True)
                    last.then_inc(multiplied, 1)

                def project(c, j, s):
                    n = wide(c)
                    pe.wait_ge(relued, c + 1)
                    if not (first(j) and s < 2):
                        pe.wait_ge(done, c - 1)
                    for k in range(2):
                        last = pe.matmul(p2[s % 2][:, 0:n], env.w2[:, i, k, :], y[:, s, k, 0:n],
                                         start=k == 0, stop=k == 1)
                    last.then_inc(projected, 1)
                if which == "a":
                    pipeline(Steps(pe, own), count, NS, (0, multiply))
                else:
                    pipeline(Steps(pe, own), count, NS, (0, multiply), (1, project))

            @block.vector
            def _(v):
                st = Steps(v, own_v)

                def measure(c, j, s):
                    n = wide(c)
                    v.wait_ge(multiplied if which == "a" else projected, c + 1)
                    if which == "b" and not first(j):
                        v.wait_ge(stored[s], 16 * j)
                    ps = [p1[s % 2][k] if which == "a" else p2[s % 2] for k in range(halves)]
                    if slots:
                        v.wait_ge(filled[s], loads * (j + 1))
                        for k in range(halves):
                            v.scalar_tensor_tensor(out=scr[:, k, :], in0=ps[k][:, :], scalar=1.0, in1=wt[:, s, :],
                                                   op0=ALU.mult, op1=ALU.mult,
                                                   accum_out=stats[:, k, c, 0:1]).then_inc(own_v, one(st))
                        for k in range(halves):
                            v.wait_ge(own_v, steps(st) - halves + 1)
                            v.scalar_tensor_tensor(out=scr[:, 2 + k, :], in0=ps[k][:, :], scalar=1.0,
                                                   in1=scr[:, k, :], op0=ALU.mult, op1=ALU.mult,
                                                   accum_out=stats[:, k, c, 1:2]).then_inc(own_v, one(st))
                    else:
                        for k in range(halves):
                            v.bn_stats(stats[:, k, c, :], ps[k][:, 0:n]).then_inc(own_v, one(st))
                    if which == "b":
                        v.tensor_copy(z2[:, s, 0:n], p2[s % 2][:, 0:n]).then_inc(own_v, one(st))
                    v.wait_ge(own_v, steps(st))
                    v.sem_inc(done, 1)
                pipeline(st, count, NS, (0 if which == "a" else 1, measure))


def results(nc, env, D, out, slots, source, norm):
    tag = "rs" if slots else "rn"
    count = 2 * CH if slots else DC
    base = SLOT0 if slots else 0
    with ExitStack() as ctx:
        m = Mem(nc, ctx, tag)
        z, h, x3, ix = m.sb("z", NS, W), m.sb("h", NS, W), m.sb("x3", NS, G, F), m.sb("ix", NS, G * NIX, dt=i32)
        vv, stats, mv, sd, xo = m.sb("vv", NS, G, F), m.sb("stats", 2, G, 6), m.sb("mv", NS, G, 2), m.sb("sd", NS, G), m.sb("xo", NS, G, F)
        off = m.sb("off", NS, G)
        po = [m.ps("po0"), m.ps("po1")]
        (filled, rows_in, stored, made, with_bias, projected, added, sampled, measured, rooted, inverted, scaled,
         normed, own) = m.sems("filled* rows_in* stored* made with_bias projected added sampled measured rooted "
                               "inverted scaled normed own")
        iv, fv, kv = views(D)
        loads = 32

        def wide(c):
            return W if slots else parts_of(c) * G
        with nc.Block() as block:
            @block.sync
            def _(sp):
                def load(c, j, s):
                    n = wide(c)
                    if not first(j):
                        sp.wait_ge(added, c + 1 - NS)
                        sp.sem_inc(own, 1)
                    sp.dma_start(z[:, s, 0:n], columns(source, c, n, base)).then_inc(filled[s], 16)
                    if slots:
                        sp.dma_start(x3[:, s, :, :], rows4(D["x3"], c)).then_inc(filled[s], 16)
                    else:
                        p_ = parts_of(c)
                        sp.dma_start(x3[0:p_, s, :, :].rearrange("p g f -> p (g f)"), node_rows(D["x3n"], c))\
                            .then_inc(filled[s], 16)

                def load_rows(c, j, s):
                    if not first(j):
                        sp.wait_ge(stored[s], 64 * j)
                        sp.sem_inc(own, 1)
                    sp.dma_start(ix[:, s, :], D["index2"].rearrange("p (c k) -> p c k", c=2 * CH)[:, c, :])\
                        .then_inc(rows_in[s], 16)

                def store(c, j, s):
                    p_ = parts_of(c)
                    sp.wait_ge(normed, c + 1)
                    sp.sem_inc(own, 1)
                    sp.dma_start(node_rows(out, c), xo[0:p_, s, :, :].rearrange("p g f -> p (g f)"))\
                        .then_inc(stored[s], 16)
                if slots:
                    pipeline(Steps(sp, own), count, NS, (0, load), (2, load_rows))
                else:
                    pipeline(Steps(sp, own), count, NS, (0, load), (6, store))
                    for s in range(NS):
                        sp.wait_ge(stored[s], 16 * uses(s, count))

            if slots:
                @block.gpsimd
                def _(pool):
                    def scatter(c, j, s):
                        pool.wait_ge(normed, c + 1)
                        pool.wait_ge(rows_in[s], 16 * (j + 1))
                        pool.sem_inc(own, 1)
                        for g in range(G):
                            pool.indirect_dma_start(
                                out=out, out_offset=bass.IndirectOffsetOnAxis(ap=ix[:, s, g * NIX:g * NIX + 1], axis=0),
                                in_=xo[:, s, g, :], in_offset=None, bounds_check=N - 1, oob_is_err=False)\
                                .then_inc(stored[s], 16)
                    pipeline(Steps(pool, own), count, NS, (0, scatter))
                    for s in range(NS):
                        pool.wait_ge(stored[s], 64 * uses(s, count))

            else:
                @block.gpsimd
                def _(pool):
                    def offset(c, j, s):
                        n = parts_of(c)
                        pool.wait_ge(filled[s], loads * (j + 1))
                        pool.tensor_tensor(x3[0:n, s, :, :], x3[0:n, s, :, :], spread(env.bc["L3_gnn_b_out"][0:n, :]),
                                           ALU.add).then_inc(with_bias, 1)
                    pipeline(Steps(pool, own), count, NS, (0, offset))

            @block.scalar
            def _(act):
                def make(c, j, s):
                    n = wide(c)
                    act.wait_ge(filled[s], loads * (j + 1))
                    if not first(j):
                        act.wait_ge(projected, c + 1 - NS)
                    act.activation(h[:, s, 0:n], z[:, s, 0:n], ACT.Relu, scale=norm[0], bias=norm[1]).then_inc(made, 1)

                def root(c, j, s):
                    n = P if slots else parts_of(c)
                    act.wait_ge(measured, c + 1)
                    act.activation(sd[0:n, s, :], mv[0:n, s, :, 1], ACT.Sqrt, bias=env.eps[0:n, 2:3])\
                        .then_inc(rooted, 1)

                def apply(c, j, s):
                    n = P if slots else parts_of(c)
                    act.wait_ge(scaled, c + 1)
                    if not first(j):
                        act.wait_ge(stored[s], (64 if slots else 16) * j)
                    for g in range(G):
                        last = act.activation(xo[0:n, s, g, :], vv[0:n, s, g, :], ACT.Identity,
                                              scale=sd[0:n, s, g:g + 1], bias=off[0:n, s, g:g + 1])
                    last.then_inc(normed, 1)
                pipeline(Steps(act, own), count, NS, (2, root), (0, make), (3, apply))

            @block.tensor
            def _(pe):
                def project(c, j, s):
                    n = P if slots else parts_of(c)
                    pe.wait_ge(made, c + 1)
                    if not (first(j) and s < 2):
                        pe.wait_ge(added, c - 1)
                    to_rows4(pe, po[s % 2], h[:, s, :], env.w["L3_gnn_W_out"], n).then_inc(projected, 1)
                pipeline(Steps(pe, own), count, NS, (0, project))

            @block.vector
            def _(v):
                def parts(c):
                    return P if slots else parts_of(c)

                def add(c, j, s):
                    n = parts(c)
                    v.wait_ge(projected, c + 1)
                    if not slots:
                        v.wait_ge(with_bias, c + 1)
                    v.tensor_tensor(vv[0:n, s, :, :], po[s % 2][0:n, :].rearrange("p (g f) -> p g f", g=G),
                                    x3[0:n, s, :, :], ALU.add).then_inc(added, 1)

                def add_bias(c, j, s):
                    v.wait_ge(added, c + 1)
                    v.tensor_tensor(vv[:, s, :, :], vv[:, s, :, :], spread(env.bc["L3_gnn_b_out"]), ALU.add)\
                        .then_inc(with_bias, 1)

                def sample(c, j, s):
                    n = parts(c)
                    v.wait_ge(added, c + 1)
                    v.wait_ge(with_bias, c + 1)
                    for g in range(G):
                        last = v.bn_stats(stats[0:n, s % 2, g, :], vv[0:n, s, g, :])
                    last.then_inc(sampled, 1)

                def measure(c, j, s):
                    n = parts(c)
                    v.wait_ge(sampled, c + 1)
                    v.sem_inc(own, 1)
                    for g in range(G):
                        last = v.bn_aggr(mv[0:n, s, g, :], stats[0:n, s % 2, g, :])
                    last.then_inc(measured, 1)

                def invert(c, j, s):
                    n = parts(c)
                    v.wait_ge(rooted, c + 1)
                    v.reciprocal(sd[0:n, s, :], sd[0:n, s, :]).then_inc(inverted, 1)

                def offset(c, j, s):
                    n = parts(c)
                    v.wait_ge(inverted, c + 1)
                    v.scalar_tensor_tensor(out=off[0:n, s, :], in0=mv[0:n, s, :, 0], scalar=-1.0, in1=sd[0:n, s, :],
                                           op0=ALU.mult, op1=ALU.mult).then_inc(scaled, 1)
                if slots:
                    pipeline(Steps(v, own), count, NS, (2, invert), (1, add), (2, offset), (1, add_bias), (1, sample),
                             (1, measure))
                else:
                    pipeline(Steps(v, own), count, NS, (2, invert), (1, add), (2, offset), (1, sample), (1, measure))


def program(nc, A, out, D):
    env = Env()
    with ExitStack() as ctx:
        env.ctx = ctx
        constants(nc, env, A)
        with nc.sbuf_tensor("tabs", [P, 6, W], fp32) as tabs:
            def load_edges(sp, keys, extra, ec, loaded):
                for dst, src in ((keys[:, 0, :], A["dst"]), (keys[:, 1, :], A["src"]),
                                 (extra[:, 2, :], A["edge_weight"])):
                    sp.dma_start(dst[0:FULL, :], src[0:FULL * P].rearrange("(t p) -> t p", p=P))\
                        .then_inc(loaded, 16)
                    sp.dma_start(dst[FULL:FULL + 1, 0:REST],
                                 src[FULL * P:E].rearrange("(t p) -> t p", t=1)).then_inc(loaded, 16)
                return 6

            def load_permuted(sp, keys, extra, ec, loaded):
                sp.dma_start(ec[:, :, :], D["edges"].rearrange("(t p) f -> t p f", p=P)[:, :, F:ROW])\
                    .then_inc(loaded, 16)
                return 1
            rows = (D["row_key"], D["row_high"])
            env.key_loads = 6
            key_meta(nc, env, "d", load_edges, rows, D["meta"], D["cols"])
            rank_edges(nc, env, "d", rows, D["meta"], D["rank_d"], tabs[:, 0, :], tabs[:, 1, :], tabs[:, 2, :])
            scatter_edges(nc, env, A, D)
            env.key_loads = 1
            key_meta(nc, env, "s", load_permuted, rows, D["meta"], D["cols_s"], permuted=True)
            rank_edges(nc, env, "s", rows, D["meta"], D["rank_s"], tabs[:, 3, :], tabs[:, 4, :], tabs[:, 5, :])
            node_tables(nc, env, D, tabs)
        dense_front(nc, env, A, D)
        slot_indices(nc, env, D)
        edge_layer0(nc, env, A, D)
        edge_layer1(nc, env, D)
        keep_rows(nc, env, D)
        source_layer1(nc, env, D)
        edge_layer2(nc, env, D)
        slot_states(nc, env, D)
        rows_of_states(nc, env, D, "r0", lambda c: columns(D["hd"], c), None)

        def stat(name, *shape):
            return ctx.enter_context(nc.sbuf_tensor(name, [P, *shape], fp32))
        node_stats, slot_sums = stat("node_stats", 2, DC, 6), stat("slot_sums", 2, 2 * CH, 2)
        norm1, norm2 = stat("norm1", 2, 2), stat("norm2", 2, 1)
        source, prev = D["za"], None
        for i in range(LAYERS):
            aggregate_states(nc, env, D, i, source)
            target = D["zb"] if source is D["za"] else D["za"]
            column_pass(nc, env, D, i, "a", False, source, None, prev, None, node_stats)
            column_pass(nc, env, D, i, "a", True, source, None, None, None, slot_sums)
            b2i = slice(2 * i, 2 * i + 2)
            norm_constants(nc, env, f"c1{i}", 2, env.col["L3_gnn_b1"][:, b2i], env.col["L3_gnn_g1"][:, b2i],
                           env.col["L3_gnn_be1"][:, b2i], node_stats, slot_sums, norm1)
            column_pass(nc, env, D, i, "b", False, source, target, prev, norm1, node_stats)
            column_pass(nc, env, D, i, "b", True, source, target, None, norm1, slot_sums)
            norm_constants(nc, env, f"c2{i}", 1, env.col["L3_gnn_b2"][:, i:i + 1], env.col["L3_gnn_gn"][:, i:i + 1],
                           env.col["L3_gnn_bet"][:, i:i + 1], node_stats, slot_sums, norm2)
            source, prev = target, (norm2[:, 0, :], norm2[:, 1, :])
            if i < LAYERS - 1:
                rows_of_states(nc, env, D, f"r{i + 1}", lambda c: columns(source, c, W, SLOT0), prev)
        results(nc, env, D, out, False, source, prev)
        results(nc, env, D, out, True, source, prev)


_INS = ["x", "src", "dst", "edge_attr_128", "edge_weight", "L0_gnn_W1", "L0_gnn_b1", "L0_gnn_W2", "L0_gnn_b2",
        "L1_gnn_Wn", "L1_gnn_We1", "L1_gnn_be1", "L1_gnn_We2", "L1_gnn_be2", "L1_gnn_W2", "L1_gnn_b2", "L1_gnn_W3",
        "L1_gnn_b3", "L2_gnn_W", "L2_gnn_b", "L3_gnn_W_atom", "L3_gnn_b_atom", "L3_gnn_W_bond", "L3_gnn_b_bond",
        "L3_gnn_eps", "L3_gnn_W1", "L3_gnn_b1", "L3_gnn_g1", "L3_gnn_be1", "L3_gnn_W2", "L3_gnn_b2", "L3_gnn_gn",
        "L3_gnn_bet", "L3_gnn_W_out", "L3_gnn_b_out"]
_SCRATCH = {
    "row_key": ((EP,), fp32), "row_high": ((EP,), fp32), "meta": ((P, T * 4), fp32), "cols": ((P, T * 4), fp32),
    "rank_d": ((P, T), i32), "rank_s": ((P, T), i32), "cols_s": ((P, T * 4), fp32), "edges": ((EP, ROW), fp32),
    "bounds": ((HI * W, 4), i32), "free": ((HI * W,), fp32), "keys_i": ((P, 2 * T), i32),
    "edge_bounds": ((P, T * 2 * 4), i32), "keep_d": ((EP,), fp32), "weights": ((2 * EP,), fp32),
    "x3n": ((N, F), fp32), "za": ((F, ZW), fp32), "zb": ((F, ZW), fp32), "hd": ((F, 2 * EP), fp32),
    "ea": ((F, EP), fp32), "hr": ((2 * EP, F), fp32), "index2": ((P, 2 * T * NIX), i32),
    "x1": ((2 * EP, F), fp32), "x2": ((2 * EP, F), fp32), "x3": ((2 * EP, F), fp32),
    "message": ((EP, MROW), fp32), "keep_s": ((EP,), fp32),
    "index": ((P, T * NIX), i32), "factor": ((P, T * NFL), fp32),
}


def kernel(**inputs):
    import numpy as _np
    import concourse.bacc as _bacc
    from concourse import mybir as _mybir
    from concourse.bass_utils import run_bass_kernel_spmd as _run

    nc = _bacc.Bacc("TRN2", target_bir_lowering=False, num_devices=1)
    arrays, args = {}, {}
    for name in _INS:
        a = _np.ascontiguousarray(inputs[name])
        arrays[f"in_{name}"] = a
        args[name] = nc.dram_tensor(f"in_{name}", a.shape, _mybir.dt.from_np(a.dtype), kind="ExternalInput").ap()
    out = nc.dram_tensor("out", (N, F), fp32, kind="ExternalOutput").ap()
    scratch = {n: nc.dram_tensor(f"scratch_{n}", s, dt, kind=SCRATCH_KIND).ap() for n, (s, dt) in _SCRATCH.items()}
    program(nc, args, out, scratch)
    r = _run(nc, [arrays], core_ids=[0])
    return r.results[0]["out"]


SCRATCH_KIND = "Internal"
```

```python
import concourse.bass as bass
from concourse import mybir
from contextlib import ExitStack, contextmanager

fp32 = mybir.dt.float32
bf16 = mybir.dt.bfloat16
i32 = mybir.dt.int32
ALU = mybir.AluOpType
ACT = mybir.ActivationFunctionType

P = 128
F = 128
G = 4
W = G * P
N = 50000
E = 12500
PAIRS = -(-E // (2 * W))
CH = 2 * PAIRS
T = CH * G
EP = CH * W
FULL = E // P
REST = E - FULL * P
NS = 4
HI = -(-N // W)
DC = HI
TP = (N - (DC - 1) * W) // G
SLOT0 = DC * W
ZW = SLOT0 + 2 * EP
FAR = 1 << 20
LOG2 = 0.6931471824645996
LN_EPS = 1e-05
BN_EPS = 1e-05
LAYERS = 3
NEG = -3.0e38


@contextmanager
def phase(nc, tag, names):
    sems, every = [], []
    for n in names.split():
        n, star, number = n.partition("*")
        got = [nc.alloc_semaphore(f"{tag}_{n}{k}") for k in range(int(number or NS) if star else 1)]
        every += got
        sems.append(got if star else got[0])
    yield sems
    nc.clear_and_free_semaphores(every)
    nc.all_engine_barrier()


class Steps:

    def __init__(self, eng, sem):
        self.eng, self.sem, self.base, self.n = eng, sem, 0, 0

    def loop(self, count, body):
        first = self.base + self.n
        body(0)
        per = self.base + self.n - first
        with self.eng.Fori(1, count) as j:
            self.base, self.n = first + j * per, 0
            body(j)
        self.base, self.n = first + count * per, 0


def one(st):
    st.n += 1
    return 1


def steps(st):
    return st.base + st.n


def pipeline(st, chunks, slots, *stages):
    most = max(lag for lag, _ in stages)

    def group(k):
        for h in range(slots):
            for lag, fn in stages:
                turn, slot = k + (h - lag) // slots, (h - lag) % slots
                chunk = slots * turn + slot
                if isinstance(k, int) and not 0 <= chunk < chunks:
                    continue
                fn(chunk, turn, slot)
    even, last = -(-most // slots), (chunks - 1) // slots
    for k in range(even):
        group(k)
    begun = st.base + st.n
    group(even)
    per = st.base + st.n - begun
    with st.eng.Fori(even + 1, last) as k:
        st.base, st.n = begun + (k - even) * per, 0
        group(k)
    st.base, st.n = begun + (last - even) * per, 0
    for k in range(last, (chunks - 1 + most) // slots + 1):
        group(k)


def weave(st, chunks, stages, others):
    span = 2 * NS
    most = max(lag for lag, _ in stages + others)

    def group(k):
        for h in range(span):
            for lag, fn in stages:
                at = h - lag
                chunk, turn = span * k + at, 2 * k + at // NS
                if not isinstance(k, int) or 0 <= chunk < chunks:
                    fn(chunk, turn, at % NS)
            for lag, fn in others:
                at = h - lag
                if at % NS == 0:
                    chunk, turn = 2 * k + at // NS, k + at // span
                    if not isinstance(k, int) or 0 <= chunk < CH:
                        fn(chunk, turn, at // NS % 2)
    even, last = -(-most // span), min((chunks - 1) // span, PAIRS - 1)
    for k in range(even + 1):
        group(k)
    with st.eng.Fori(even + 1, last) as k:
        group(k)
    for k in range(last, (max(chunks - 1, (CH - 1) * NS) + most) // span + 1):
        group(k)


def first(j):
    return isinstance(j, int) and j == 0


class Env:
    pass


def constants(nc, env, A):
    ctx = env.ctx

    def sb(name, shape, dt=fp32):
        return ctx.enter_context(nc.sbuf_tensor(name, shape, dt))

    mats = ["L0_gnn_W1", "L0_gnn_W2", "L1_gnn_Wn", "L1_gnn_We1", "L1_gnn_We2", "L1_gnn_W2", "L1_gnn_W3",
            "L3_gnn_W_atom", "L3_gnn_W_bond", "L3_gnn_W_out"]
    wts = sb("wts", [P, len(mats), F])
    env.w = {m: wts[:, k, :] for k, m in enumerate(mats)}
    w1 = sb("l3_w1", [P, LAYERS, 2 * F])
    w1e = sb("l3_w1e", [P, LAYERS, 2 * F])
    w2 = sb("l3_w2", [P, LAYERS, 2, F])
    env.w1, env.w1e, env.w2 = w1, w1e, w2
    l2w = sb("l2_w", [P, 2, F])
    l2t = sb("l2_t", [P, 2, F])
    env.wi, env.wj = l2t[:, 0, :], l2t[:, 1, :]
    vecs = [("L0_gnn_b1", 1), ("L1_gnn_be1", 1), ("L1_gnn_b2", 1), ("L2_gnn_b", 1), ("L3_gnn_b_atom", 1),
            ("L3_gnn_b_bond", 1), ("L3_gnn_b1", 6), ("L3_gnn_g1", 6), ("L3_gnn_be1", 6), ("L3_gnn_b2", 3),
            ("L3_gnn_gn", 3), ("L3_gnn_bet", 3)]
    rows = sum(n for _, n in vecs)
    vrow = sb("vrow", [rows, F])
    vcol = sb("vcol", [P, rows])
    env.col, at = {}, 0
    for name, n in vecs:
        env.col[name] = vcol[:, at:at + n]
        at += n
    bcs = ["L0_gnn_b2", "L1_gnn_be2", "L1_gnn_b3", "L3_gnn_b_out"]
    bc = sb("bias_rows", [P, len(bcs) + 1, F])
    env.bc = {b: bc[:, k, :] for k, b in enumerate(bcs)}
    env.h0 = bc[:, len(bcs), :]
    epsb = sb("epsb", [P, LAYERS])
    env.onep = sb("onep", [P, LAYERS])
    env.ident = sb("ident", [P, P])
    env.earlier = sb("earlier", [P, P])
    env.below = sb("below", [P, P])
    env.iota = sb("iota_free", [P, W])
    env.iotap = sb("iota_part", [P, 1])
    env.ones = sb("ones", [P, W])
    env.eps = sb("eps", [P, 3])
    sp2 = sb("sp2", [P, 4])
    spb = sb("spb", [P, F])
    with phase(nc, "const", "loaded made transposed turned h_in h_mm own_v own_p own_a soft") as (
            loaded, made, transposed, turned, h_in, h_mm, own_v, own_p, own_a, soft):
        with nc.psum_tensor("tp", [P, 512], fp32) as tp, nc.Block() as block:
            loads = []
            for m in mats:
                loads.append((env.w[m], A[m]))
            loads.append((w1[:, :, :], A["L3_gnn_W1"].rearrange("l k n -> k l n")))
            for i in range(LAYERS):
                loads.append((w2[:, i, :, :], A["L3_gnn_W2"][i].rearrange("(h k) n -> k h n", h=2)))
            loads.append((l2w[:, :, :], A["L2_gnn_W"].rearrange("f (h k) -> f h k", h=2)))
            at = 0
            for name, n in vecs:
                src = A[name]
                if n == 1:
                    src = src.rearrange("(a f) -> a f", a=1)
                elif n == 6:
                    src = src.rearrange("l (h f) -> (l h) f", h=2)
                loads.append((vrow[at:at + n, :], src))
                at += n
            for b in bcs:
                loads.append((env.bc[b], A[b].rearrange("(a f) -> a f", a=1).broadcast_to([P, F])))
            loads.append((epsb[:, :], A["L3_gnn_eps"].rearrange("(a f) -> a f", a=1).broadcast_to([P, LAYERS])))

            @block.sync
            def _(sp):
                for dst, src in loads:
                    sp.dma_start(dst, src).then_inc(loaded, 16)

            @block.gpsimd
            def _(pool):
                st = Steps(pool, own_p)
                pool.memset(env.ident[:, :], 0.0).then_inc(own_p, one(st))
                pool.memset(env.earlier[:, :], 1.0).then_inc(own_p, one(st))
                pool.memset(env.below[:, :], 1.0).then_inc(own_p, one(st))
                pool.memset(env.ones[:, :], 1.0).then_inc(own_p, one(st))
                pool.wait_ge(own_p, steps(st))
                pool.affine_select(out=env.ident[:, :], in_=env.ident[:, :], compare_op=ALU.not_equal,
                                          fill=1.0, base=0, pattern=[[-1, P]], channel_multiplier=1).then_inc(own_p, one(st))
                pool.affine_select(out=env.earlier[:, :], in_=env.earlier[:, :], compare_op=ALU.is_gt,
                                          fill=0.0, base=0, pattern=[[-1, P]], channel_multiplier=1).then_inc(own_p, one(st))
                pool.affine_select(out=env.below[:, :], in_=env.below[:, :], compare_op=ALU.is_gt,
                                          fill=0.0, base=0, pattern=[[1, P]], channel_multiplier=-1).then_inc(own_p, one(st))
                pool.iota(env.iota[:, :], pattern=[[1, W]], base=0, channel_multiplier=0,
                                 allow_small_or_imprecise_dtypes=True).then_inc(own_p, one(st))
                pool.iota(env.iotap[:, :], pattern=[[0, 1]], base=0, channel_multiplier=1,
                                 allow_small_or_imprecise_dtypes=True).then_inc(own_p, one(st))
                pool.wait_ge(own_p, steps(st))
                pool.sem_inc(made, 1)

            @block.tensor
            def _(pe):
                pe.wait_ge(loaded, 16 * len(loads))
                pe.wait_ge(made, 1)
                pe.transpose(tp[:, 0:rows], vrow[:, :], env.ident[0:rows, 0:rows])
                pe.transpose(tp[:, 128:256], l2w[:, 0, :], env.ident[:, :])
                pe.transpose(tp[:, 256:384], l2w[:, 1, :], env.ident[:, :]).then_inc(transposed, 1)
                pe.wait_ge(h_in, 1)
                pe.matmul(tp[:, 384:512], spb[:, :], env.w["L1_gnn_W3"], start=True, stop=True).then_inc(h_mm, 1)

            @block.scalar
            def _(act):
                st = Steps(act, own_a)
                act.wait_ge(turned, 1)
                act.activation(sp2[:, 0:1], env.col["L1_gnn_b2"], ACT.Abs).then_inc(own_a, one(st))
                act.wait_ge(own_a, steps(st))
                act.activation(sp2[:, 0:1], sp2[:, 0:1], ACT.Exp, scale=-1.0).then_inc(own_a, one(st))
                act.wait_ge(own_a, steps(st))
                act.activation(sp2[:, 1:2], sp2[:, 0:1], ACT.Ln, bias=1.0).then_inc(soft, 1)

            @block.vector
            def _(v):
                st = Steps(v, own_v)
                v.memset(env.eps[:, 0:1], 0.25 * LN_EPS).then_inc(own_v, one(st))
                v.memset(env.eps[:, 2:3], LN_EPS).then_inc(own_v, one(st))
                v.memset(env.eps[:, 1:2], LN_EPS * LN_EPS).then_inc(own_v, one(st))
                v.wait_ge(transposed, 1)
                v.tensor_copy(vcol[:, :], tp[:, 0:rows]).then_inc(own_v, one(st))
                v.tensor_copy(l2t[:, :, :], tp[:, 128:384].rearrange("p (h k) -> p h k", h=2)).then_inc(own_v, one(st))
                v.tensor_scalar(env.onep[:, :], epsb[:, :], 1.0, None, ALU.add).then_inc(own_v, one(st))
                v.wait_ge(own_v, steps(st))
                for i in range(LAYERS):
                    v.tensor_scalar(w1e[:, i, :], w1[:, i, :], env.onep[:, i:i + 1], None, ALU.mult).then_inc(own_v, one(st))
                v.wait_ge(own_v, steps(st))
                v.sem_inc(turned, 1)
                v.tensor_scalar(sp2[:, 2:3], env.col["L1_gnn_b2"], 0.0, -LOG2, ALU.max, ALU.add).then_inc(own_v, one(st))
                v.wait_ge(soft, 1)
                v.wait_ge(own_v, steps(st))
                v.tensor_tensor(sp2[:, 3:4], sp2[:, 1:2], sp2[:, 2:3], ALU.add).then_inc(own_v, one(st))
                v.wait_ge(own_v, steps(st))
                v.tensor_scalar(spb[:, :], env.ones[:, 0:F], sp2[:, 3:4], None, ALU.mult).then_inc(h_in, 1)
                v.wait_ge(h_mm, 1)
                v.tensor_tensor(env.h0, tp[:, 384:512], env.bc["L1_gnn_b3"], ALU.add)



def key_meta(nc, env, tag, load, rows, meta, cols, permuted=False):
    with ExitStack() as ctx:
        def sb(name, shape, dt=fp32):
            return ctx.enter_context(nc.sbuf_tensor(f"{tag}_{name}", shape, dt))
        extra_i = sb("extra_i", [T, 2, P], i32)
        extra = sb("extra", [T, 4, P])
        ec = sb("ec", [T, P, 4])
        part = sb("part", [T, 2, P], i32)
        kf = sb("kf", [T, 3, P])
        mt = sb("mt", [P, T, 4])
        ct = sb("ct", [P, T, 4])
        ps = [ctx.enter_context(nc.psum_tensor(f"{tag}_mp{k}", [P, 512], fp32)) for k in range(2)]
        loaded, cleared, split, turned, copied, stored, own = ctx.enter_context(
            phase(nc, tag + "_meta", "loaded cleared split turned copied stored own"))
        with nc.Block() as block:
            @block.sync
            def _(sp):
                sp.wait_ge(cleared, 1)
                n = load(sp, extra_i, extra, ec, loaded)
                sp.wait_ge(copied, 1)
                sp.dma_start(rows[0].rearrange("(t p) -> t p", p=P), kf[:, 0, :]).then_inc(stored, 16)
                sp.dma_start(rows[1].rearrange("(t p) -> t p", p=P), kf[:, 1, :]).then_inc(stored, 16)
                sp.dma_start(meta, mt[:, :, :].rearrange("p t k -> p (t k)")).then_inc(stored, 16)
                k = 3
                if cols is not None:
                    sp.dma_start(cols, ct[:, :, :].rearrange("p t k -> p (t k)")).then_inc(stored, 16)
                    k += 1
                sp.wait_ge(stored, 16 * k)
                env.key_loads = n

            @block.vector
            def _(v):
                st = Steps(v, own)
                v.memset(extra_i[:, :, :], N).then_inc(own, one(st))
                v.memset(mt[:, :, :], 0.0).then_inc(own, one(st))
                v.memset(ec[:, :, :], 0.0).then_inc(own, one(st))
                v.memset(ct[:, :, :], 0.0).then_inc(own, one(st))
                v.wait_ge(own, steps(st))
                v.memset(extra[:, :, :], 0.0).then_inc(cleared, 1)
                v.wait_ge(loaded, 16 * env.key_loads)
                if permuted:
                    v.tensor_copy(extra_i[:, 0, :], ec[:, :, 1]).then_inc(own, one(st))
                    v.tensor_copy(extra[:, 2, :], ec[:, :, 2]).then_inc(own, one(st))
                    v.tensor_copy(extra_i[:, 1, :], ec[:, :, 0]).then_inc(own, one(st))
                    v.wait_ge(own, steps(st))
                v.tensor_copy(extra[:, 0:2, :], extra_i[:, :, :]).then_inc(own, one(st))
                v.tensor_scalar(part[:, 0, :], extra_i[:, 0, :], 9, None, ALU.logical_shift_right).then_inc(own, one(st))
                v.tensor_scalar(part[:, 1, :], extra_i[:, 0, :], W - 1, None, ALU.bitwise_and).then_inc(own, one(st))
                v.wait_ge(own, steps(st))
                v.tensor_copy(kf[:, 0, :], extra[:, 0, :]).then_inc(own, one(st))
                v.tensor_copy(kf[:, 1:3, :], part[:, :, :]).then_inc(own, one(st))
                v.wait_ge(own, steps(st))
                v.sem_inc(split, 1)
                v.wait_ge(turned, 1)
                for k in range(3):
                    v.tensor_copy(mt[:, :, k], ps[0][:, k * P:k * P + T]).then_inc(own, one(st))
                    v.tensor_copy(ct[:, :, k], ps[1][:, k * P:k * P + T]).then_inc(own, one(st))
                v.wait_ge(own, steps(st))
                v.sem_inc(copied, 1)

            @block.tensor
            def _(pe):
                pe.wait_ge(split, 1)
                for k in range(3):
                    pe.transpose(ps[0][:, k * P:k * P + T], kf[:, k, :], env.ident[0:T, 0:T])
                for k in range(3):
                    last = pe.transpose(ps[1][:, k * P:k * P + T], extra[:, k, :], env.ident[0:T, 0:T])
                last.then_inc(turned, 1)


def rank_edges(nc, env, tag, rows, meta, ranks, vtab, btab, count):
    with ExitStack() as ctx:
        def sb(name, shape, dt=fp32):
            return ctx.enter_context(nc.sbuf_tensor(f"{tag}_r_{name}", shape, dt))

        def pb(name):
            return ctx.enter_context(nc.psum_tensor(f"{tag}_r_{name}", [P, W], fp32))
        mt = sb("mt", [P, 2, G * 4])
        rk = sb("rk", [P, 2, W])
        rh = sb("rh", [P, 2, W])
        ohi = sb("ohi", [P, G, P], bf16)
        olo = sb("olo", [P, G, W], bf16)
        oht = sb("oht", [P, G, P])
        tab = sb("tab", [P, 2, W])
        run = sb("run", [P, W])
        off = sb("off", [P, 1])
        scr = sb("scr", [P, W])
        tie = sb("tie", [P, G, P])
        acc = sb("acc", [P, 2, G, 2])
        res = sb("res", [P, 2, G], i32)
        hist, offp, run_ps = pb("hist"), pb("offp"), pb("run_ps")
        look = [pb(f"look{k}") for k in range(2)]
        sems = ctx.enter_context(phase(
            nc, tag + "_rank", "meta0 meta1 onehot counted total offs tabs own m0 m1 hot hot_used copied looked inc rank0 rank1 st0 st1"))
        (meta0, meta1, onehot, counted, total, offs, tabs, own, m0, m1, hot, hot_used, copied, looked,
         inc, rank0, rank1, st0, st1) = sems
        meta_in, meta2_in, ranked, stored = [meta0, meta1], [m0, m1], [rank0, rank1], [st0, st1]
        mv = meta.rearrange("p (c k) -> p c k", c=CH)
        rvk = rows[0].rearrange("(c w) -> c w", w=W)
        rvh = rows[1].rearrange("(c w) -> c w", w=W)
        rkv = ranks.rearrange("p (c k) -> p c k", c=CH)

        with nc.Block() as block:
            @block.sync
            def _(sp):
                def histo(j):
                    for s in range(2):
                        if not first(j):
                            sp.wait_ge(onehot, (2 * j + s - 1) * G)
                        sp.dma_start(mt[:, s, :], mv[:, 2 * j + s, :]).then_inc(meta_in[s], 16)

                def ranking(j):
                    for s in range(2):
                        if first(j):
                            sp.wait_ge(onehot, CH * G)
                        else:
                            sp.wait_ge(ranked[s], j)
                        c = 2 * j + s
                        sp.dma_start(mt[:, s, :], mv[:, c, :]).then_inc(meta2_in[s], 16)
                        sp.dma_start(rk[:, s, :], rvk[bass.ds(c, 1), :].broadcast_to([P, W])).then_inc(meta2_in[s], 16)
                        sp.dma_start(rh[:, s, :], rvh[bass.ds(c, 1), :].broadcast_to([P, W])).then_inc(meta2_in[s], 16)
                Steps(sp, own).loop(PAIRS, histo)
                Steps(sp, own).loop(PAIRS, ranking)

            def onehots(v, s, g, b):
                v.tensor_scalar(ohi[:, b, :], env.iota[:, 0:P], mt[:, s, g * 4 + 1:g * 4 + 2], None, ALU.is_equal)
                return v.tensor_scalar(olo[:, b, :], env.iota[:, :], mt[:, s, g * 4 + 2:g * 4 + 3], None,
                                       ALU.is_equal)

            @block.vector
            def _(v):
                st = Steps(v, own)

                def histo(j):
                    for s in range(2):
                        v.wait_ge(meta_in[s], 16 * (j + 1))
                        for g in range(G):
                            t = (2 * j + s) * G + g
                            if not (first(j) and s == 0):
                                v.wait_ge(counted, t - 3)
                            onehots(v, s, g, g).then_inc(onehot, 1)
                st.loop(PAIRS, histo)
                v.wait_ge(counted, T)
                v.tensor_copy(count, hist[:, :]).then_inc(own, one(st))
                v.wait_ge(own, steps(st))
                v.tensor_tensor_scan(out=run[:, :], data0=env.ones[:, :], data1=count, initial=0.0,
                                            op0=ALU.mult, op1=ALU.add).then_inc(own, one(st))
                v.wait_ge(own, steps(st))
                v.tensor_copy(off[:, :], run[:, W - 1:W]).then_inc(own, one(st))
                v.wait_ge(own, steps(st))
                v.sem_inc(total, 1)
                v.wait_ge(offs, 1)
                v.tensor_copy(off[:, :], offp[:, 0:1]).then_inc(own, one(st))
                v.wait_ge(own, steps(st))
                v.tensor_scalar(run[:, :], run[:, :], off[:, :], None, ALU.add).then_inc(own, one(st))
                v.wait_ge(own, steps(st))
                v.tensor_tensor(btab, run[:, :], count, ALU.subtract).then_inc(own, one(st))
                v.tensor_scalar(scr[:, :], count, 0.0, None, ALU.is_gt).then_inc(own, one(st))
                v.tensor_scalar(vtab, run[:, :], -1.0 - FAR, None, ALU.add).then_inc(own, one(st))
                v.wait_ge(own, steps(st))
                v.tensor_tensor(vtab, vtab, scr[:, :], ALU.mult).then_inc(own, one(st))
                v.wait_ge(own, steps(st))
                v.tensor_scalar(vtab, vtab, float(FAR), None, ALU.add).then_inc(own, one(st))
                v.wait_ge(own, steps(st))
                v.wait_ge(own, steps(st))
                v.sem_inc(tabs, 1)

                before = steps(st)

                def prepare(j, s, g):
                    t = (2 * j + s) * G + g
                    if g == 0:
                        v.wait_ge(meta2_in[s], 48 * (j + 1))
                        if not first(j):
                            v.wait_ge(ranked[s], j)
                    if not (first(j) and s == 0):
                        v.wait_ge(inc, t - 2)
                        v.wait_ge(hot_used, t - 3)
                    onehots(v, s, g, g)
                    v.tensor_scalar(oht[:, g, :], rh[:, s, g * P:(g + 1) * P], env.iotap[:, :], None,
                                    ALU.is_equal).then_inc(hot, 1)
                    v.wait_ge(own, before + t)
                    v.scalar_tensor_tensor(
                        out=tie[:, g, :], in0=rk[:, s, g * P:(g + 1) * P], scalar=mt[:, s, g * 4:g * 4 + 1],
                        in1=env.earlier[:, :], op0=ALU.is_equal, op1=ALU.mult,
                        accum_out=acc[:, s, g, 0:1]).then_inc(own, 1)

                def look_up(j, s, g):
                    t = (2 * j + s) * G + g
                    b = g % 2
                    v.wait_ge(looked, t + 1)
                    v.wait_ge(own, before + t + 1)
                    if not (first(j) and s == 0 and g == 0):
                        v.wait_ge(hot_used, t)
                    v.scalar_tensor_tensor(
                        out=scr[:, :], in0=look[b][:, :], scalar=1.0, in1=olo[:, g, :],
                        op0=ALU.mult, op1=ALU.mult, accum_out=acc[:, s, g, 1:2]).then_inc(hot_used, 1)

                def ranking(j, more=True):
                    for s in range(2):
                        for g in range(G):
                            if g < G - 1:
                                prepare(j, s, g + 1)
                            elif s == 0:
                                prepare(j, 1, 0)
                            elif more:
                                prepare(j + 1, 0, 0)
                            look_up(j, s, g)
                        v.wait_ge(hot_used, (2 * j + s + 1) * G)
                        if not first(j):
                            v.wait_ge(stored[s], 16 * j)
                        v.tensor_tensor(res[:, s, :], acc[:, s, :, 0], acc[:, s, :, 1], ALU.add)\
                            .then_inc(ranked[s], 1)
                prepare(0, 0, 0)
                st.loop(PAIRS - 1, ranking)
                ranking(PAIRS - 1, more=False)

            @block.tensor
            def _(pe):
                st = Steps(pe, own)

                def count_tile(b, t, start):
                    pe.wait_ge(onehot, t + 1)
                    pe.matmul(hist[:, :], ohi[:, b, :], olo[:, b, :], start=start, stop=False,
                              skip_group_check=True).then_inc(counted, 1)

                def histo(j):
                    for k in range(2 * G):
                        count_tile(k % G, 2 * G * j + k, first(j) and k == 0)
                st.loop(PAIRS, histo)
                pe.wait_ge(total, 1)
                pe.matmul(offp[:, 0:1], env.below[:, :], off[:, :], start=True, stop=True).then_inc(offs, 1)
                pe.wait_ge(tabs, 1)
                pe.matmul(run_ps[:, :], env.ident[:, :], btab, start=True, stop=False,
                          skip_group_check=True).then_inc(inc, 1)

                def ranking(j):
                    for k in range(2 * G):
                        b = k % 2
                        t = 2 * G * j + k
                        pe.wait_ge(hot, t + 1)
                        pe.wait_ge(copied, t + 1)
                        pe.matmul(run_ps[:, :], ohi[:, k % G, :], olo[:, k % G, :], start=False, stop=False,
                                  skip_group_check=True).then_inc(inc, 1)
                        if not (first(j) and k < 2):
                            pe.wait_ge(hot_used, t - 1)
                        pe.matmul(look[b][:, :], oht[:, k % G, :], tab[:, b, :], start=True, stop=True)\
                            .then_inc(looked, 1)
                st.loop(PAIRS, ranking)

            @block.scalar
            def _(act):
                def ranking(j):
                    for k in range(2 * G):
                        t = 2 * G * j + k
                        act.wait_ge(inc, t + 1)
                        act.activation(tab[:, k % 2, :], run_ps[:, :], ACT.Copy).then_inc(copied, 1)
                Steps(act, own).loop(PAIRS, ranking)

            @block.gpsimd
            def _(pool):
                def store(j):
                    for s in range(2):
                        pool.wait_ge(ranked[s], j + 1)
                        pool.dma_start(rkv[:, 2 * j + s, :], res[:, s, :]).then_inc(stored[s], 16)
                Steps(pool, own).loop(PAIRS, store)
                for s in range(2):
                    pool.wait_ge(stored[s], 16 * PAIRS)


ROW = F + 4
NIX = 8
(IX_SRC, IX_DST, IX_SRC_D, IX_DST_D, IX_SRC_S, IX_DST_S, IX_OUT_D, IX_OUT_S) = range(NIX)
NFL = 4
FL_W, FL_KEEP_S, FL_REAL = range(3)
MROW = 2 * F + 4


def scatter_edges(nc, env, A, D):
    with ExitStack() as ctx:
        row = ctx.enter_context(nc.sbuf_tensor("sc_row", [P, 2, G, ROW], fp32))
        idx = ctx.enter_context(nc.sbuf_tensor("sc_idx", [P, 2, G], i32))
        in0, in1, out0, out1, own = ctx.enter_context(phase(nc, "sc", "in0 in1 out0 out1 own"))
        filled, left = [in0, in1], [out0, out1]
        ev = A["edge_attr_128"]
        cv = D["cols"].rearrange("p (c g k) -> p c g k", c=CH, g=G)
        rv = D["rank_d"].rearrange("p (c g) -> p c g", c=CH)
        whole = PAIRS - 1
        with nc.Block() as block:
            @block.sync
            def _(sp):
                def load(j, last):
                    for s in range(2):
                        c = 2 * j + s
                        if not first(j):
                            sp.wait_ge(left[s], 16 * G * j)
                        sp.dma_start(idx[:, s, :], rv[:, c, :]).then_inc(filled[s], 16)
                        sp.dma_start(row[:, s, :, F:ROW], cv[:, c, :, :]).then_inc(filled[s], 16)
                        if not last:
                            sp.dma_start(row[:, s, :, 0:F],
                                         ev[bass.ds(c * W, W), :].rearrange("(g p) f -> p g f", p=P))\
                                .then_inc(filled[s], 16)
                        elif s == 0:
                            whole_tiles = (E - c * W) // P
                            for g in range(whole_tiles):
                                sp.dma_start(row[:, s, g, 0:F], ev[c * W + g * P:c * W + (g + 1) * P, :])\
                                    .then_inc(filled[s], 16)
                            sp.dma_start(row[0:REST, s, whole_tiles, 0:F], ev[FULL * P:E, :])\
                                .then_inc(filled[s], 16)
                Steps(sp, own).loop(whole, lambda j: load(j, False))
                load(whole, True)

            @block.gpsimd
            def _(pool):
                def scatter(j, extra):
                    for s in range(2):
                        pool.wait_ge(filled[s], 48 * (j + 1) if extra is None else 48 * j + 32 + extra[s])
                        pool.sem_inc(own, 1)
                        for g in range(G):
                            pool.indirect_dma_start(
                                out=D["edges"][:, :], out_offset=bass.IndirectOffsetOnAxis(ap=idx[:, s, g:g + 1], axis=0),
                                in_=row[:, s, g, :], in_offset=None).then_inc(left[s], 16)
                Steps(pool, own).loop(whole, lambda j: scatter(j, None))
                scatter(whole, (16 * ((E - 2 * whole * W) // P + 1), 0))
                for s in range(2):
                    pool.wait_ge(left[s], 16 * G * PAIRS)


def node_tables(nc, env, D, tabs):
    vd, bd, cd, vs, bs, cs = (tabs[:, k, :] for k in range(6))
    with ExitStack() as ctx:
        vv = ctx.enter_context(nc.sbuf_tensor("nt_vv", [P, W, 4], i32))
        free = ctx.enter_context(nc.sbuf_tensor("nt_free", [P, 2, W], fp32))
        made, stored, own = ctx.enter_context(phase(nc, "nt", "made stored own"))
        with nc.Block() as block:
            @block.vector
            def _(v):
                st = Steps(v, own)
                for k, t in enumerate((vd, vs, bd, bs)):
                    v.tensor_copy(vv[:, :, k], t).then_inc(own, one(st))
                v.tensor_scalar(free[:, 0, :], cd, 0.0, None, ALU.is_equal).then_inc(own, one(st))
                v.tensor_scalar(free[:, 1, :], cs, 0.0, None, ALU.is_equal).then_inc(own, one(st))
                v.wait_ge(own, steps(st))
                v.tensor_tensor(free[:, 0, :], free[:, 0, :], free[:, 1, :], ALU.mult).then_inc(own, one(st))
                v.wait_ge(own, steps(st))
                v.sem_inc(made, 1)

            @block.sync
            def _(sp):
                sp.wait_ge(made, 1)
                sp.dma_start(D["bounds"].rearrange("(h l) k -> h (l k)", l=W),
                             vv[0:HI, :, :].rearrange("h l k -> h (l k)")).then_inc(stored, 16)
                sp.dma_start(D["free"].rearrange("(h l) -> h l", l=W), free[0:HI, 0, :]).then_inc(stored, 16)
                sp.wait_ge(stored, 32)


def slot_indices(nc, env, D):
    with ExitStack() as ctx:
        def sb(name, shape, dt=fp32):
            return ctx.enter_context(nc.sbuf_tensor(f"si_{name}", shape, dt))
        cf, rki, bi = sb("cf", [P, T, 4]), sb("rki", [P, T], i32), sb("bi", [P, T, 2, 4], i32)
        b = sb("b", [P, 2, 4, T])
        rank = sb("rank", [P, T])
        slot, far = sb("slot", [P, T]), sb("far", [P, T])
        real, td, ts, tmp, tmp2, ond, ons = (sb(n, [P, T]) for n in ("real", "td", "ts", "tmp", "tmp2", "ond", "ons"))
        ixf, ixi, ixo = sb("ixf", [P, T]), sb("ixi", [P, T, NIX], i32), sb("ixo", [P, 2, T, NIX], i32)
        fl, rowf, mcol, corner = sb("fl", [P, T, NFL]), sb("rowf", [T, 3, P]), sb("mcol", [P, 2]), sb("corner", [P, 1])
        tp = ctx.enter_context(nc.psum_tensor("si_tp", [P, 512], fp32))
        loaded, iota_done, summed, m_done, made, turned, copied, stored, own, own_p = ctx.enter_context(
            phase(nc, "si", "loaded iota_done summed m_done made turned copied stored own own_p"))
        with nc.Block() as block:
            @block.sync
            def _(sp):
                sp.dma_start(cf[:, :, :].rearrange("p t k -> p (t k)"), D["cols_s"]).then_inc(loaded, 16)
                sp.dma_start(rki[:, :], D["rank_s"]).then_inc(loaded, 16)
                sp.dma_start(bi[:, :, :, :].rearrange("p t k b -> p (t k b)"), D["edge_bounds"])\
                    .then_inc(loaded, 16)
                sp.wait_ge(copied, 1)
                sp.dma_start(D["keep_d"].rearrange("(t p) -> t p", p=P), rowf[:, 0, :]).then_inc(stored, 16)
                sp.dma_start(D["weights"][0:EP].rearrange("(t p) -> t p", p=P), rowf[:, 1, :]).then_inc(stored, 16)
                sp.dma_start(D["weights"][EP:2 * EP].rearrange("(t p) -> t p", p=P), rowf[:, 2, :])\
                    .then_inc(stored, 16)
                sp.dma_start(D["index"], ixi[:, :, :].rearrange("p t k -> p (t k)")).then_inc(stored, 16)
                sp.dma_start(D["factor"], fl[:, :, :].rearrange("p t k -> p (t k)")).then_inc(stored, 16)
                for k in range(2):
                    sp.dma_start(D["index2"][:, k * T * NIX:(k + 1) * T * NIX],
                                 ixo[:, k, :, :].rearrange("p t k -> p (t k)")).then_inc(stored, 16)
                sp.wait_ge(stored, 112)

            @block.gpsimd
            def _(pool):
                st = Steps(pool, own_p)
                pool.iota(slot[:, :], pattern=[[P, T]], base=0, channel_multiplier=1,
                                 allow_small_or_imprecise_dtypes=True).then_inc(own_p, one(st))
                pool.memset(corner[:, :], 0.0).then_inc(own_p, one(st))
                pool.wait_ge(own_p, steps(st))
                pool.affine_select(out=corner[:, :], in_=corner[:, :], compare_op=ALU.not_equal, fill=1.0,
                                          base=1 - P, pattern=[[0, 1]], channel_multiplier=1).then_inc(own_p, one(st))
                pool.wait_ge(own_p, steps(st))
                pool.sem_inc(iota_done, 1)

            @block.vector
            def _(v):
                st = Steps(v, own)

                def do(ins):
                    ins.then_inc(own, one(st))
                    v.wait_ge(own, steps(st))
                v.wait_ge(loaded, 48)
                v.wait_ge(iota_done, 1)
                for k in range(2):
                    for q in range(4):
                        v.tensor_copy(b[:, k, q, :], bi[:, :, k, q]).then_inc(own, one(st))
                v.memset(far[:, :], float(FAR)).then_inc(own, one(st))
                v.memset(fl[:, :, :], 0.0).then_inc(own, one(st))
                do(v.tensor_copy(rank[:, :], rki[:, :]))
                src, dst = cf[:, :, 0], cf[:, :, 1]
                s_vd, s_vs, s_bd, s_bs = (b[:, 0, q, :] for q in range(4))
                d_vd, d_vs, d_bd, d_bs = (b[:, 1, q, :] for q in range(4))
                do(v.tensor_scalar(real[:, :], slot[:, :], float(E), None, ALU.is_lt))
                do(v.tensor_scalar(td[:, :], s_vd, float(FAR), None, ALU.is_lt))
                do(v.tensor_tensor(td[:, :], td[:, :], real[:, :], ALU.mult))
                do(v.tensor_scalar(ts[:, :], d_vs, float(FAR), None, ALU.is_lt))

                def put(k, value):
                    do(v.tensor_copy(ixi[:, :, k], value))

                def pick(k, cond, value, other, shift):
                    do(v.tensor_scalar(tmp[:, :], other, float(shift), None, ALU.add))
                    do(v.tensor_tensor(tmp2[:, :], value, cond, ALU.mult))
                    do(v.tensor_scalar(ixf[:, :], cond, -1.0, 1.0, ALU.mult, ALU.add))
                    do(v.tensor_tensor(tmp[:, :], tmp[:, :], ixf[:, :], ALU.mult))
                    do(v.tensor_tensor(tmp[:, :], tmp[:, :], tmp2[:, :], ALU.add))
                    put(k, tmp[:, :])
                do(v.tensor_scalar(tmp[:, :], src, float(N - 1), None, ALU.min))
                put(IX_SRC, tmp[:, :])
                do(v.tensor_scalar(tmp[:, :], dst, float(N - 1), None, ALU.min))
                put(IX_DST, tmp[:, :])
                pick(IX_SRC_D, td[:, :], s_vd, slot[:, :], EP)
                put(IX_DST_D, d_vd)
                put(IX_SRC_S, s_vs)
                pick(IX_DST_S, ts[:, :], d_vs, slot[:, :], EP)
                do(v.tensor_tensor(ond[:, :], slot[:, :], d_vd, ALU.is_equal))
                do(v.tensor_tensor(ond[:, :], ond[:, :], real[:, :], ALU.mult))
                pick(IX_OUT_D, ond[:, :], dst, far[:, :], 0)
                do(v.tensor_tensor(fl[:, :, FL_KEEP_S], rank[:, :], s_bs, ALU.not_equal))
                do(v.tensor_tensor(ons[:, :], rank[:, :], s_bs, ALU.is_equal))
                do(v.tensor_tensor(ons[:, :], ons[:, :], real[:, :], ALU.mult))
                do(v.tensor_tensor(tmp[:, :], ons[:, :], td[:, :], ALU.mult))
                do(v.tensor_tensor(ons[:, :], ons[:, :], tmp[:, :], ALU.subtract))
                pick(IX_OUT_S, ons[:, :], src, far[:, :], 0)
                do(v.tensor_copy(fl[:, :, FL_W], cf[:, :, 2]))
                do(v.tensor_copy(fl[:, :, FL_REAL], real[:, :]))
                do(v.tensor_copy(ixo[:, 0, :, :], ixi[:, :, :]))
                do(v.tensor_copy(ixo[:, 1, :, :], ixi[:, :, :]))
                do(v.tensor_copy(ixo[:, 0, :, 0], ixi[:, :, IX_OUT_D]))
                do(v.tensor_copy(ixo[:, 1, :, 0], ixi[:, :, IX_OUT_S]))
                do(v.reduce_sum(mcol[:, 0:1], ond[:, :], axis=mybir.AxisListType.X))
                do(v.reduce_sum(mcol[:, 1:2], ons[:, :], axis=mybir.AxisListType.X))
                do(v.tensor_tensor(mcol[:, 0:1], mcol[:, 0:1], mcol[:, 1:2], ALU.add))
                v.wait_ge(own, steps(st))
                v.sem_inc(summed, 1)
                v.wait_ge(m_done, 1)
                do(v.tensor_scalar(mcol[:, 1:2], tp[:, 0:1], corner[:, :], -1.0, ALU.mult, ALU.mult))
                do(v.tensor_tensor(ons[:, T - 1:T], ons[:, T - 1:T], mcol[:, 1:2], ALU.add))
                do(v.tensor_tensor(tmp[:, :], slot[:, :], d_bd, ALU.not_equal))
                v.wait_ge(own, steps(st))
                v.sem_inc(made, 1)
                v.wait_ge(turned, 1)
                do(v.tensor_copy(rowf[:, :, :], tp[0:T, 128:512].rearrange("t (k p) -> t k p", k=3)))
                v.wait_ge(own, steps(st))
                v.sem_inc(copied, 1)

            @block.tensor
            def _(pe):
                pe.wait_ge(summed, 1)
                pe.matmul(tp[:, 0:1], env.ones[:, 0:P], mcol[:, 0:1], start=True, stop=True).then_inc(m_done, 1)
                pe.wait_ge(made, 1)
                pe.transpose(tp[0:T, 128:256], tmp[:, :], env.ident[:, :])
                pe.transpose(tp[0:T, 256:384], ond[:, :], env.ident[:, :])
                pe.transpose(tp[0:T, 384:512], ons[:, :], env.ident[:, :]).then_inc(turned, 1)


def rows4(ap, c):
    return ap[bass.ds(c * W, W), :].rearrange("(g p) f -> p g f", p=P)


def spread(row, n=G):
    return row.rearrange("p (a f) -> p a f", a=1).broadcast_to([row.shape[0], n, F])


def moments(v, st, x, stats, mv):
    n = x.shape[1]
    for g in range(n):
        v.bn_stats(stats[:, g, :], x[:, g, :]).then_inc(st.sem, one(st))
    v.wait_ge(st.sem, steps(st))
    v.sem_inc(st.sem, one(st))
    for g in range(n):
        v.bn_aggr(mv[:, g, :], stats[:, g, :]).then_inc(st.sem, one(st))


def norm_apply(v, st, x, mv, sd, out, mask=None):
    v.reciprocal(sd, sd).then_inc(st.sem, one(st))
    v.wait_ge(st.sem, steps(st))
    if mask is not None:
        v.tensor_tensor(sd, sd, mask, ALU.mult).then_inc(st.sem, one(st))
        v.wait_ge(st.sem, steps(st))
    for g in range(x.shape[1]):
        v.tensor_scalar(out[:, g, :], x[:, g, :], mv[:, g, 0:1], sd[:, g:g + 1], ALU.subtract, ALU.mult).then_inc(st.sem, one(st))


def norm_scale(v, st, mv, sd, off, mask=None):
    v.reciprocal(sd, sd).then_inc(st.sem, one(st))
    v.wait_ge(st.sem, steps(st))
    if mask is not None:
        v.tensor_tensor(sd, sd, mask, ALU.mult).then_inc(st.sem, one(st))
        v.wait_ge(st.sem, steps(st))
    v.scalar_tensor_tensor(out=off, in0=mv[:, :, 0], scalar=-1.0, in1=sd, op0=ALU.mult, op1=ALU.mult)\
        .then_inc(st.sem, one(st))


def norm_rows(act, x, sd, off, out):
    for g in range(x.shape[1]):
        last = act.activation(out[:, g, :], x[:, g, :], ACT.Identity, scale=sd[:, g:g + 1], bias=off[:, g:g + 1])
    return last


def views(D):
    return (D["index"].rearrange("p (c k) -> p c k", c=CH), D["factor"].rearrange("p (c k) -> p c k", c=CH),
            D["keep_d"].rearrange("(c w) -> c w", w=W))


def gather4(pool, out, table, ix, k, sem):
    for g in range(G):
        pool.indirect_dma_start(out=out[:, g, :], out_offset=None, in_=table,
                                in_offset=bass.IndirectOffsetOnAxis(ap=ix[:, g * NIX + k:g * NIX + k + 1], axis=0))\
            .then_inc(sem, 16)


def transpose4(pe, env, out, rows, parts=P):
    for g in range(G):
        last = pe.transpose(out[:, g * parts:(g + 1) * parts], rows[:, g, :], env.ident[0:parts, 0:parts])
    return last


def to_rows4(pe, out, cols, w, parts=P):
    for g in range(G):
        last = pe.matmul(out[0:parts, g * F:(g + 1) * F], cols[:, g * parts:(g + 1) * parts], w,
                         start=True, stop=True)
    return last


def uses(s, n=CH):
    return (n - s + NS - 1) // NS


class Mem:

    def __init__(self, nc, ctx, tag):
        self.nc, self.ctx, self.tag = nc, ctx, tag

    def sb(self, name, *shape, dt=fp32):
        return self.ctx.enter_context(self.nc.sbuf_tensor(f"{self.tag}_{name}", [P, *shape], dt))

    def ps(self, name):
        return self.ctx.enter_context(self.nc.psum_tensor(f"{self.tag}_{name}", [P, W], fp32))

    def sems(self, names):
        return self.ctx.enter_context(phase(self.nc, self.tag, names))


def edge_layer0(nc, env, A, D):
    with ExitStack() as ctx:
        m = Mem(nc, ctx, "e0")
        ix, fl, keep = m.sb("ix", NS, G * NIX, dt=i32), m.sb("fl", NS, G * NFL), m.sb("keep", NS, W)
        xs, xd, ms = m.sb("xs", NS, G, F), m.sb("xd", NS, G, F), m.sb("ms", NS, G, F)
        agg, zs, zd = m.sb("agg", NS, W), m.sb("zs", NS, W), m.sb("zd", NS, W)
        hs, hd = m.sb("hs", NS, W), m.sb("hd", NS, W)
        vv, stats = m.sb("vv", NS, 2 * G, F), m.sb("stats", 2 * G, 6)
        mv, sd, off = m.sb("mv", NS, 2 * G, 2), m.sb("sd", NS, 2 * G), m.sb("off", NS, 2 * G)
        xo = m.sb("xo", NS, 2, G, F)
        tm, ts, td, ps_s, ps_d, o_s, o_d = (m.ps(n) for n in ("tm", "ts", "td", "ps_s", "ps_d", "o_s", "o_d"))
        (filled, got, stored, weighted, turned, summed, copied, hidden, relued, projected, added, measured, rooted,
         normed, own_v, own_a, own, scaled) = m.sems("filled* got* stored* weighted turned summed copied hidden relued projected "
                                             "added measured rooted normed own_v own_a own scaled")
        iv, fv, kv = views(D)
        with nc.Block() as block:
            @block.sync
            def _(sp):
                def load(c, j, s):
                    if not first(j):
                        sp.wait_ge(summed, c + 1 - NS)
                        sp.sem_inc(own, 1)
                        sp.wait_ge(got[s], 128 * j)
                    sp.sem_inc(own, 1)
                    sp.dma_start(ix[:, s, :], iv[:, c, :]).then_inc(filled[s], 16)
                    sp.dma_start(fl[:, s, :], fv[:, c, :]).then_inc(filled[s], 16)
                    sp.dma_start(keep[:, s, :], kv[bass.ds(c, 1), :].broadcast_to([P, W])).then_inc(filled[s], 16)

                def store(c, j, s):
                    sp.wait_ge(normed, c + 1)
                    sp.sem_inc(own, 1)
                    sp.dma_start(rows4(D["x1"], c), xo[:, s, 1, :, :]).then_inc(stored[s], 16)
                    sp.dma_start(rows4(D["x1"], c + CH), xo[:, s, 0, :, :]).then_inc(stored[s], 16)
                pipeline(Steps(sp, own), CH, NS, (6, store), (0, load))
                for s in range(NS):
                    sp.wait_ge(stored[s], 32 * uses(s))

            @block.gpsimd
            def _(pool):
                def gather(c, j, s):
                    if not first(j):
                        pool.wait_ge(added, c + 1 - NS)
                    pool.wait_ge(filled[s], 48 * (j + 1))
                    pool.sem_inc(own, 1)
                    gather4(pool, xs[:, s, :, :], A["x"], ix[:, s, :], IX_SRC, got[s])
                    gather4(pool, xd[:, s, :, :], A["x"], ix[:, s, :], IX_DST, got[s])
                pipeline(Steps(pool, own), CH, NS, (0, gather))

            @block.vector
            def _(v):
                st = Steps(v, own_v)

                def weigh(c, j, s):
                    v.wait_ge(got[s], 128 * (j + 1))
                    if not first(j):
                        v.wait_ge(turned, c + 1 - NS)
                    for g in range(G):
                        k = g * NFL + FL_W
                        v.tensor_scalar(ms[:, s, g, :], xs[:, s, g, :], fl[:, s, k:k + 1], None, ALU.mult).then_inc(own_v, one(st))
                    v.wait_ge(own_v, steps(st))
                    v.sem_inc(weighted, 1)

                def scan(c, j, s):
                    v.wait_ge(turned, c + 1)
                    start = 0.0 if first(j) and s == 0 else agg[:, (s - 1) % NS, W - 1:W]
                    v.tensor_tensor_scan(out=agg[:, s, :], data0=keep[:, s, :], data1=tm[:, :], initial=start,
                                                op0=ALU.mult, op1=ALU.add).then_inc(own_v, one(st))
                    v.wait_ge(own_v, steps(st))
                    v.tensor_tensor(zd[:, s, :], td[:, :], agg[:, s, :], ALU.add).then_inc(own_v, one(st))
                    v.wait_ge(own_v, steps(st))
                    v.sem_inc(summed, 1)

                def measure(c, j, s):
                    v.wait_ge(projected, c + 1)
                    v.tensor_tensor(vv[:, s, 0:G, :], o_s[:, :].rearrange("p (g f) -> p g f", g=G),
                                           xs[:, s, :, :], ALU.add).then_inc(own_v, one(st))
                    v.tensor_tensor(vv[:, s, G:2 * G, :], o_d[:, :].rearrange("p (g f) -> p g f", g=G),
                                           xd[:, s, :, :], ALU.add).then_inc(own_v, one(st))
                    v.wait_ge(own_v, steps(st))
                    v.sem_inc(added, 1)
                    v.tensor_tensor(vv[:, s, :, :], vv[:, s, :, :], spread(env.bc["L0_gnn_b2"], 2 * G), ALU.add).then_inc(own_v, one(st))
                    v.wait_ge(own_v, steps(st))
                    moments(v, st, vv[:, s], stats, mv[:, s])
                    v.wait_ge(own_v, steps(st))
                    v.sem_inc(measured, 1)

                def scale(c, j, s):
                    v.wait_ge(rooted, c + 1)
                    norm_scale(v, st, mv[:, s], sd[:, s, :], off[:, s, :])
                    v.wait_ge(own_v, steps(st))
                    v.sem_inc(scaled, 1)
                pipeline(st, CH, NS, (1, scan), (3, scale), (0, weigh), (2, measure))

            @block.scalar
            def _(act):
                st = Steps(act, own_a)

                def copy(c, j, s):
                    act.wait_ge(turned, c + 1)
                    act.activation(zs[:, s, :], ts[:, :], ACT.Copy).then_inc(copied, 1)

                def relu(c, j, s):
                    act.wait_ge(hidden, c + 1)
                    if not first(j):
                        act.wait_ge(projected, c + 1 - NS)
                    act.activation(hs[:, s, :], ps_s[:, :], ACT.Relu, bias=env.col["L0_gnn_b1"]).then_inc(own_a, one(st))
                    act.activation(hd[:, s, :], ps_d[:, :], ACT.Relu, bias=env.col["L0_gnn_b1"]).then_inc(own_a, one(st))
                    act.wait_ge(own_a, steps(st))
                    act.sem_inc(relued, 1)

                def root(c, j, s):
                    act.wait_ge(measured, c + 1)
                    act.activation(sd[:, s, :], mv[:, s, :, 1], ACT.Sqrt, bias=env.eps[:, 2:3]).then_inc(rooted, 1)

                def apply(c, j, s):
                    act.wait_ge(scaled, c + 1)
                    if not first(j):
                        act.wait_ge(stored[s], 32 * j)
                    norm_rows(act, vv[:, s], sd[:, s, :], off[:, s, :],
                              xo[:, s, :, :, :].rearrange("p k g f -> p (k g) f")).then_inc(normed, 1)
                pipeline(st, CH, NS, (3, root), (1, relu), (4, apply), (0, copy))

            @block.tensor
            def _(pe):
                def turn(c, j, s):
                    pe.wait_ge(weighted, c + 1)
                    if not (first(j) and s == 0):
                        pe.wait_ge(summed, c)
                        pe.wait_ge(copied, c)
                    transpose4(pe, env, tm, ms[:, s, :, :])
                    transpose4(pe, env, ts, xs[:, s, :, :])
                    transpose4(pe, env, td, xd[:, s, :, :]).then_inc(turned, 1)

                def hide(c, j, s):
                    pe.wait_ge(summed, c + 1)
                    pe.wait_ge(copied, c + 1)
                    if not (first(j) and s == 0):
                        pe.wait_ge(relued, c)
                    pe.matmul(ps_s[:, :], env.w["L0_gnn_W1"], zs[:, s, :], start=True, stop=True)
                    pe.matmul(ps_d[:, :], env.w["L0_gnn_W1"], zd[:, s, :], start=True, stop=True)\
                        .then_inc(hidden, 1)

                def project(c, j, s):
                    pe.wait_ge(relued, c + 1)
                    if not (first(j) and s == 0):
                        pe.wait_ge(added, c)
                    to_rows4(pe, o_s, hs[:, s, :], env.w["L0_gnn_W2"])
                    to_rows4(pe, o_d, hd[:, s, :], env.w["L0_gnn_W2"]).then_inc(projected, 1)
                pipeline(Steps(pe, own), CH, NS, (2, project), (1, hide), (0, turn))


def soft_plus_scalar(act, st, src, bias, t, r):
    act.activation(r, src, ACT.Relu, bias=bias).then_inc(st.sem, one(st))
    act.activation(t, src, ACT.Abs, bias=bias).then_inc(st.sem, one(st))
    act.wait_ge(st.sem, steps(st))
    act.activation(t, t, ACT.Exp, scale=-1.0).then_inc(st.sem, one(st))
    act.wait_ge(st.sem, steps(st))
    act.activation(t, t, ACT.Ln, bias=1.0).then_inc(st.sem, one(st))


def edge_layer1(nc, env, D):
    with ExitStack() as ctx:
        m = Mem(nc, ctx, "e1")
        ix, fl, rk = m.sb("ix", NS, G * NIX, dt=i32), m.sb("fl", NS, G * NFL), m.sb("rk", NS, G, dt=i32)
        ea, xd, mr = m.sb("ea", NS, G, F), m.sb("xd", NS, G, F), m.sb("mr", NS, G, MROW)
        xt, et, sp_t, sp_r, fs = m.sb("xt", NS, W), m.sb("et", NS, W), m.sb("sp_t", W), m.sb("sp_r", W), m.sb("fs", NS, W)
        fr = m.sb("fr", G, F)
        vv, stats, mv, sd, xo = m.sb("vv", G, F), m.sb("stats", G, 6), m.sb("mv", G, 2), m.sb("sd", G), m.sb("xo", NS, G, F)
        td, te, pe1, pf, px = (m.ps(n) for n in ("td", "te", "pe1", "pf", "px"))
        (filled, ranks_in, got, stored, sent, turned, copied_x, copied_e, hidden, softened, filtered, projected, multiplied,
         measured, rooted, normed, own_v, own_a, own) = m.sems(
            "filled* ranks_in* got* stored* sent* turned copied_x copied_e hidden softened filtered projected multiplied "
            "measured rooted normed own_v own_a own")
        iv, fv, kv = views(D)
        rv = D["rank_s"].rearrange("p (c g) -> p c g", c=CH)
        with nc.Block() as block:
            @block.sync
            def _(sp):
                def load(c, j, s):
                    if not first(j):
                        sp.wait_ge(measured, c + 1 - NS)
                    sp.sem_inc(own, 1)
                    sp.dma_start(ix[:, s, :], iv[:, c, :]).then_inc(filled[s], 16)
                    sp.dma_start(fl[:, s, :], fv[:, c, :]).then_inc(filled[s], 16)
                    sp.dma_start(ea[:, s, :, :], rows4(D["edges"], c)[:, :, 0:F]).then_inc(filled[s], 16)

                def load_ranks(c, j, s):
                    if not first(j):
                        sp.wait_ge(sent[s], 16 * G * j)
                    sp.sem_inc(own, 1)
                    sp.dma_start(rk[:, s, :], rv[:, c, :]).then_inc(ranks_in[s], 16)

                def store(c, j, s):
                    sp.wait_ge(normed, c + 1)
                    sp.sem_inc(own, 1)
                    sp.dma_start(rows4(D["x2"], c + CH), xo[:, s, :, :]).then_inc(stored[s], 16)
                pipeline(Steps(sp, own), CH, NS, (6, store), (0, load), (1, load_ranks))
                for s in range(NS):
                    sp.wait_ge(stored[s], 16 * uses(s))

            @block.gpsimd
            def _(pool):
                def gather(c, j, s):
                    pool.wait_ge(filled[s], 48 * (j + 1))
                    pool.sem_inc(own, 1)
                    gather4(pool, xd[:, s, :, :], D["x1"], ix[:, s, :], IX_DST_D, got[s])

                def gather_src(c, j, s):
                    if not first(j):
                        pool.wait_ge(sent[s], 16 * G * j)
                    pool.sem_inc(own, 1)
                    gather4(pool, mr[:, s, :, F:2 * F], D["x1"], ix[:, s, :], IX_SRC_D, got[s])

                def send(c, j, s):
                    pool.wait_ge(multiplied, c + 1)
                    pool.wait_ge(got[s], 128 * (j + 1))
                    pool.wait_ge(ranks_in[s], 16 * (j + 1))
                    pool.sem_inc(own, 1)
                    for g in range(G):
                        pool.indirect_dma_start(
                            out=D["message"], out_offset=bass.IndirectOffsetOnAxis(ap=rk[:, s, g:g + 1], axis=0),
                            in_=mr[:, s, g, :], in_offset=None).then_inc(sent[s], 16)
                pipeline(Steps(pool, own), CH, NS, (0, gather), (3, send), (0, gather_src))
                for s in range(NS):
                    pool.wait_ge(sent[s], 16 * G * uses(s))

            @block.vector
            def _(v):
                st = Steps(v, own_v)

                def copy(c, j, s):
                    v.wait_ge(turned, c + 1)
                    v.tensor_copy(et[:, s, :], te[:, :]).then_inc(copied_e, 1)

                def filt(c, j, s):
                    v.wait_ge(softened, c + 1)
                    if not first(j):
                        v.wait_ge(projected, c + 1 - NS)
                    v.scalar_tensor_tensor(out=fs[:, s, :], in0=sp_r[:, :], scalar=-LOG2, in1=sp_t[:, :],
                                                  op0=ALU.add, op1=ALU.add).then_inc(own_v, one(st))
                    v.wait_ge(own_v, steps(st))
                    v.sem_inc(filtered, 1)

                def product(c, j, s):
                    v.wait_ge(projected, c + 1)
                    v.wait_ge(got[s], 128 * (j + 1))
                    v.tensor_tensor(fr[:, :, :], pf[:, :].rearrange("p (g f) -> p g f", g=G),
                                           spread(env.bc["L1_gnn_be2"]), ALU.add).then_inc(own_v, one(st))
                    v.wait_ge(own_v, steps(st))
                    if first(j):
                        v.memset(mr[:, s, :, 2 * F:MROW], 0.0).then_inc(own_v, one(st))
                        v.wait_ge(own_v, steps(st))
                    else:
                        v.memset(vv[:, 0, 0:1], 0.0).then_inc(own_v, one(st))
                    v.tensor_tensor(mr[:, s, :, 0:F], fr[:, :, :], px[:, :].rearrange("p (g f) -> p g f", g=G),
                                           ALU.mult).then_inc(own_v, one(st))
                    v.tensor_copy(mr[:, s, :, 2 * F], fl[:, s, :].rearrange("p (g k) -> p g k", k=NFL)
                                         [:, :, FL_KEEP_S]).then_inc(own_v, one(st))
                    v.wait_ge(own_v, steps(st))
                    v.sem_inc(multiplied, 1)
                    v.scalar_tensor_tensor(out=vv[:, :, :], in0=xd[:, s, :, :], scalar=2.0,
                                                  in1=spread(env.h0), op0=ALU.mult, op1=ALU.add).then_inc(own_v, one(st))
                    v.wait_ge(own_v, steps(st))
                    moments(v, st, vv, stats, mv)
                    v.wait_ge(own_v, steps(st))
                    v.sem_inc(measured, 1)

                def finish(c, j, s):
                    v.wait_ge(rooted, c + 1)
                    if not first(j):
                        v.wait_ge(stored[s], 16 * j)
                    norm_apply(v, st, vv, mv, sd[:, :], xo[:, s, :, :])
                    v.wait_ge(own_v, steps(st))
                    v.sem_inc(normed, 1)
                pipeline(st, CH, NS, (3, finish), (2, product), (1, filt), (0, copy))

            @block.scalar
            def _(act):
                st = Steps(act, own_a)

                def copy(c, j, s):
                    act.wait_ge(turned, c + 1)
                    act.activation(xt[:, s, :], td[:, :], ACT.Copy).then_inc(copied_x, 1)

                def soft(c, j, s):
                    act.wait_ge(hidden, c + 1)
                    if not (first(j) and s == 0):
                        act.wait_ge(filtered, c)
                    soft_plus_scalar(act, st, pe1[:, :], env.col["L1_gnn_be1"], sp_t[:, :], sp_r[:, :])
                    act.wait_ge(own_a, steps(st))
                    act.sem_inc(softened, 1)

                def root(c, j, s):
                    act.wait_ge(measured, c + 1)
                    act.activation(sd[:, :], mv[:, :, 1], ACT.Sqrt, bias=env.eps[:, 2:3]).then_inc(rooted, 1)
                pipeline(st, CH, NS, (3, root), (1, soft), (0, copy))

            @block.tensor
            def _(pe):
                def turn(c, j, s):
                    pe.wait_ge(got[s], 128 * (j + 1))
                    pe.wait_ge(filled[s], 48 * (j + 1))
                    if not (first(j) and s == 0):
                        pe.wait_ge(copied_x, c)
                        pe.wait_ge(copied_e, c)
                    transpose4(pe, env, td, xd[:, s, :, :])
                    transpose4(pe, env, te, ea[:, s, :, :]).then_inc(turned, 1)

                def hide(c, j, s):
                    pe.wait_ge(copied_e, c + 1)
                    if not (first(j) and s == 0):
                        pe.wait_ge(softened, c)
                    pe.matmul(pe1[:, :], env.w["L1_gnn_We1"], et[:, s, :], start=True, stop=True).then_inc(hidden, 1)

                def project(c, j, s):
                    pe.wait_ge(filtered, c + 1)
                    pe.wait_ge(copied_x, c + 1)
                    if not (first(j) and s == 0):
                        pe.wait_ge(multiplied, c)
                    to_rows4(pe, px, xt[:, s, :], env.w["L1_gnn_Wn"])
                    to_rows4(pe, pf, fs[:, s, :], env.w["L1_gnn_We2"]).then_inc(projected, 1)
                pipeline(Steps(pe, own), CH, NS, (2, project), (1, hide), (0, turn))


def keep_rows(nc, env, D):
    with ExitStack() as ctx:
        m = Mem(nc, ctx, "kr")
        buf, row = m.sb("buf", P, 4), m.sb("row", P)
        loaded, copied, stored = m.sems("loaded copied stored")
        with nc.Block() as block:
            @block.sync
            def _(sp):
                sp.dma_start(buf[0:T, :, :], D["message"].rearrange("(t p) f -> t p f", p=P)[:, :, 2 * F:MROW])\
                    .then_inc(loaded, 16)
                sp.wait_ge(copied, 1)
                sp.dma_start(D["keep_s"].rearrange("(t p) -> t p", p=P), row[0:T, :]).then_inc(stored, 16)
                sp.wait_ge(stored, 16)

            @block.vector
            def _(v):
                v.wait_ge(loaded, 16)
                v.tensor_copy(row[0:T, :], buf[0:T, :, 0]).then_inc(copied, 1)


def source_layer1(nc, env, D):
    with ExitStack() as ctx:
        m = Mem(nc, ctx, "s1")
        mr, keep = m.sb("mr", NS, G, MROW), m.sb("keep", NS, W)
        agg, sp_t, sp_r, fs = m.sb("agg", NS, W), m.sb("sp_t", 2, W), m.sb("sp_r", 2, W), m.sb("fs", NS, W)
        vv, stats, mv, sd, xo = m.sb("vv", G, F), m.sb("stats", G, 6), m.sb("mv", G, 2), m.sb("sd", G), m.sb("xo", NS, G, F)
        tm, po, ph = m.ps("tm"), m.ps("po"), [m.ps("ph0"), m.ps("ph1")]
        (filled, stored, turned, summed, hidden, softened, filtered, projected, added,
         measured, rooted, normed, own_v, own_a, own) = m.sems(
            "filled* stored* turned summed hidden softened filtered projected added measured rooted normed own_v own_a own")
        kv = D["keep_s"].rearrange("(c w) -> c w", w=W)
        with nc.Block() as block:
            @block.sync
            def _(sp):
                def load(c, j, s):
                    if not first(j):
                        sp.wait_ge(added, c + 1 - NS)
                    sp.sem_inc(own, 1)
                    sp.dma_start(mr[:, s, :, :], rows4(D["message"], c)).then_inc(filled[s], 16)
                    sp.dma_start(keep[:, s, :], kv[bass.ds(c, 1), :].broadcast_to([P, W])).then_inc(filled[s], 16)

                def store(c, j, s):
                    sp.wait_ge(normed, c + 1)
                    sp.sem_inc(own, 1)
                    sp.dma_start(rows4(D["x2"], c), xo[:, s, :, :]).then_inc(stored[s], 16)
                pipeline(Steps(sp, own), CH, NS, (6, store), (0, load))
                for s in range(NS):
                    sp.wait_ge(stored[s], 16 * uses(s))

            @block.vector
            def _(v):
                st = Steps(v, own_v)

                def scan(c, j, s):
                    v.wait_ge(turned, c + 1)
                    start = 0.0 if first(j) and s == 0 else agg[:, (s - 1) % NS, W - 1:W]
                    if not first(j):
                        v.wait_ge(hidden, c + 1 - NS)
                    v.tensor_tensor_scan(out=agg[:, s, :], data0=keep[:, s, :], data1=tm[:, :], initial=start,
                                                op0=ALU.mult, op1=ALU.add).then_inc(own_v, one(st))
                    v.wait_ge(own_v, steps(st))
                    v.sem_inc(summed, 1)

                def filt(c, j, s):
                    v.wait_ge(softened, c + 1)
                    if not first(j):
                        v.wait_ge(projected, c + 1 - NS)
                    v.scalar_tensor_tensor(out=fs[:, s, :], in0=sp_r[:, s % 2, :], scalar=-LOG2, in1=sp_t[:, s % 2, :],
                                                  op0=ALU.add, op1=ALU.add).then_inc(own_v, one(st))
                    v.wait_ge(own_v, steps(st))
                    v.sem_inc(filtered, 1)

                def measure(c, j, s):
                    v.wait_ge(projected, c + 1)
                    v.scalar_tensor_tensor(out=vv[:, :, :], in0=mr[:, s, :, F:2 * F], scalar=2.0,
                                                  in1=po[:, :].rearrange("p (g f) -> p g f", g=G),
                                                  op0=ALU.mult, op1=ALU.add).then_inc(own_v, one(st))
                    v.wait_ge(own_v, steps(st))
                    v.sem_inc(added, 1)
                    v.tensor_tensor(vv[:, :, :], vv[:, :, :], spread(env.bc["L1_gnn_b3"]), ALU.add).then_inc(own_v, one(st))
                    v.wait_ge(own_v, steps(st))
                    moments(v, st, vv, stats, mv)
                    v.wait_ge(own_v, steps(st))
                    v.sem_inc(measured, 1)

                def finish(c, j, s):
                    v.wait_ge(rooted, c + 1)
                    if not first(j):
                        v.wait_ge(stored[s], 16 * j)
                    norm_apply(v, st, vv, mv, sd[:, :], xo[:, s, :, :])
                    v.wait_ge(own_v, steps(st))
                    v.sem_inc(normed, 1)
                pipeline(st, CH, NS, (2, filt), (0, scan), (3, finish), (2, measure))

            @block.scalar
            def _(act):
                st = Steps(act, own_a)

                def soft(c, j, s):
                    act.wait_ge(hidden, c + 1)
                    if not (first(j) and s < 2):
                        act.wait_ge(filtered, c - 1)
                    soft_plus_scalar(act, st, ph[s % 2][:, :], env.col["L1_gnn_b2"], sp_t[:, s % 2, :],
                                     sp_r[:, s % 2, :])
                    act.wait_ge(own_a, steps(st))
                    act.sem_inc(softened, 1)

                def root(c, j, s):
                    act.wait_ge(measured, c + 1)
                    act.activation(sd[:, :], mv[:, :, 1], ACT.Sqrt, bias=env.eps[:, 2:3]).then_inc(rooted, 1)
                pipeline(st, CH, NS, (3, root), (1, soft))

            @block.tensor
            def _(pe):
                def turn(c, j, s):
                    pe.wait_ge(filled[s], 32 * (j + 1))
                    if not (first(j) and s == 0):
                        pe.wait_ge(summed, c)
                    transpose4(pe, env, tm, mr[:, s, :, 0:F]).then_inc(turned, 1)

                def hide(c, j, s):
                    pe.wait_ge(summed, c + 1)
                    if not (first(j) and s < 2):
                        pe.wait_ge(softened, c - 1)
                    pe.matmul(ph[s % 2][:, :], env.w["L1_gnn_W2"], agg[:, s, :], start=True, stop=True).then_inc(hidden, 1)

                def project(c, j, s):
                    pe.wait_ge(filtered, c + 1)
                    if not (first(j) and s == 0):
                        pe.wait_ge(added, c)
                    to_rows4(pe, po, fs[:, s, :], env.w["L1_gnn_W3"]).then_inc(projected, 1)
                pipeline(Steps(pe, own), CH, NS, (0, turn), (2, project), (0, hide))


def edge_layer2(nc, env, D):
    with ExitStack() as ctx:
        m = Mem(nc, ctx, "e2")
        ix, fl, keep = m.sb("ix", NS, G * NIX, dt=i32), m.sb("fl", NS, G * NFL), m.sb("keep", NS, W)
        xs, xd, df = m.sb("xs", NS, G, F), m.sb("xd", NS, G, F), m.sb("df", NS, G, F)
        xt, dt_, pen, agg = m.sb("xt", NS, W), m.sb("dt", NS, W), m.sb("pen", NS, W), m.sb("agg", NS, W)
        ab, fin, am = m.sb("ab", 2, W), m.sb("fin", 2, W), m.sb("am", NS, W)
        vv, stats, mv, sd = m.sb("vv", NS, 2 * G, F), m.sb("stats", 2 * G, 6), m.sb("mv", NS, 2 * G, 2), m.sb("sd", NS, 2 * G)
        off = m.sb("off", NS, 2 * G)
        mask, xo = m.sb("mask", NS, 2 * G), m.sb("xo", NS, 2, G, F)
        ta, tb, pm, tr = m.ps("ta"), m.ps("tb"), m.ps("pm"), [m.ps("tr0"), m.ps("tr1")]
        (filled, got, stored, differed, turned, copied_x, copied_d, mixed, scanned, maxed, returned, added,
         measured, rooted, normed, own_v, own_a, own, scaled, biased, subtracted) = m.sems(
            "filled* got* stored* differed turned copied_x copied_d mixed scanned maxed returned added measured rooted "
            "normed own_v own_a own scaled biased subtracted")
        iv, fv, kv = views(D)
        with nc.Block() as block:
            @block.sync
            def _(sp):
                def load(c, j, s):
                    if not first(j):
                        sp.wait_ge(differed, c + 1 - NS)
                        sp.sem_inc(own, 1)
                        sp.wait_ge(got[s], 128 * j)
                    sp.sem_inc(own, 1)
                    sp.dma_start(ix[:, s, :], iv[:, c, :]).then_inc(filled[s], 16)
                    sp.dma_start(fl[:, s, :], fv[:, c, :]).then_inc(filled[s], 16)
                    sp.dma_start(keep[:, s, :], kv[bass.ds(c, 1), :].broadcast_to([P, W])).then_inc(filled[s], 16)

                def store(c, j, s):
                    sp.wait_ge(normed, c + 1)
                    sp.sem_inc(own, 1)
                    sp.dma_start(rows4(D["x3"], c), xo[:, s, 0, :, :]).then_inc(stored[s], 16)
                    sp.dma_start(rows4(D["x3"], c + CH), xo[:, s, 1, :, :]).then_inc(stored[s], 16)
                pipeline(Steps(sp, own), CH, NS, (6, store), (0, load))
                for s in range(NS):
                    sp.wait_ge(stored[s], 32 * uses(s))

            @block.gpsimd
            def _(pool):
                def gather(c, j, s):
                    if not first(j):
                        pool.wait_ge(added, c + 1 - NS)
                        pool.wait_ge(copied_x, c + 1 - NS)
                    pool.wait_ge(filled[s], 48 * (j + 1))
                    pool.sem_inc(own, 1)
                    gather4(pool, xs[:, s, :, :], D["x2"], ix[:, s, :], IX_SRC_S, got[s])
                    gather4(pool, xd[:, s, :, :], D["x2"], ix[:, s, :], IX_DST_S, got[s])
                pipeline(Steps(pool, own), CH, NS, (0, gather))

            @block.vector
            def _(v):
                st = Steps(v, own_v)

                def differ(c, j, s):
                    v.wait_ge(got[s], 128 * (j + 1))
                    if not first(j):
                        v.wait_ge(scaled, c + 1 - NS)
                    v.memset(mask[:, s, 0:G], 1.0).then_inc(own_v, one(st))
                    v.tensor_copy(mask[:, s, G:2 * G], fl[:, s, :].rearrange("p (g k) -> p g k", k=NFL)
                                         [:, :, FL_REAL]).then_inc(own_v, one(st))
                    v.tensor_tensor(df[:, s, :, :], xs[:, s, :, :], xd[:, s, :, :], ALU.subtract).then_inc(own_v, one(st))
                    v.tensor_scalar(pen[:, s, :], keep[:, s, :], -1.0, -NEG, ALU.add, ALU.mult).then_inc(own_v, one(st))
                    v.wait_ge(own_v, steps(st))
                    v.sem_inc(differed, 1)

                def scan(c, j, s):
                    v.wait_ge(mixed, c + 1)
                    start = NEG if first(j) and s == 0 else agg[:, (s - 1) % NS, W - 1:W]
                    v.tensor_tensor_scan(out=agg[:, s, :], data0=pen[:, s, :], data1=pm[:, :], initial=start,
                                                op0=ALU.add, op1=ALU.max).then_inc(own_v, one(st))
                    v.wait_ge(own_v, steps(st))
                    v.sem_inc(scanned, 1)

                def subtract(c, j, s):
                    v.wait_ge(biased, c + 1)
                    v.tensor_tensor(fin[:, s % 2, :], ab[:, s % 2, :], ab[:, s % 2, :], ALU.subtract)\
                        .then_inc(own_v, one(st))
                    if not first(j):
                        v.wait_ge(returned, c + 1 - NS)
                    v.memset(am[:, s, :], 0.0).then_inc(own_v, one(st))
                    v.wait_ge(own_v, steps(st))
                    v.sem_inc(subtracted, 1)

                def select(c, j, s):
                    v.tensor_scalar(fin[:, s % 2, :], fin[:, s % 2, :], 0.0, None, ALU.is_equal).then_inc(own_v, one(st))
                    v.wait_ge(own_v, steps(st))
                    v.sem_inc(own_v, one(st))
                    v.copy_predicated(am[:, s, :], fin[:, s % 2, :].bitcast(i32), ab[:, s % 2, :]).then_inc(own_v, one(st))
                    v.wait_ge(own_v, steps(st))
                    v.sem_inc(maxed, 1)

                def measure(c, j, s):
                    v.wait_ge(returned, c + 1)
                    v.tensor_tensor(vv[:, s, 0:G, :], tr[s % 2][:, :].rearrange("p (g f) -> p g f", g=G),
                                           xd[:, s, :, :], ALU.add).then_inc(own_v, one(st))
                    v.wait_ge(own_v, steps(st))
                    v.sem_inc(added, 1)
                    v.wait_ge(copied_x, c + 1)
                    moments(v, st, vv[:, s], stats, mv[:, s])
                    v.wait_ge(own_v, steps(st))
                    v.sem_inc(measured, 1)

                def scale(c, j, s):
                    v.wait_ge(rooted, c + 1)
                    norm_scale(v, st, mv[:, s], sd[:, s, :], off[:, s, :], mask[:, s, :])
                    v.wait_ge(own_v, steps(st))
                    v.sem_inc(scaled, 1)
                pipeline(st, CH, NS, (2, subtract), (2, select), (0, differ), (3, scale), (1, scan), (2, measure))

            @block.scalar
            def _(act):
                st = Steps(act, own_a)

                def copy(c, j, s):
                    act.wait_ge(turned, c + 1)
                    act.activation(xt[:, s, :], ta[:, :], ACT.Copy)
                    if not first(j):
                        act.wait_ge(normed, c + 1 - NS)
                    act.activation(vv[:, s, G:2 * G, :], xs[:, s, :, :], ACT.Copy).then_inc(copied_x, 1)
                    act.activation(dt_[:, s, :], tb[:, :], ACT.Copy).then_inc(copied_d, 1)

                def bias(c, j, s):
                    act.wait_ge(scanned, c + 1)
                    if not (first(j) and s < 2):
                        act.wait_ge(maxed, c - 1)
                    act.activation(ab[:, s % 2, :], agg[:, s, :], ACT.Identity, bias=env.col["L2_gnn_b"])\
                        .then_inc(biased, 1)

                def apply(c, j, s):
                    act.wait_ge(scaled, c + 1)
                    if not first(j):
                        act.wait_ge(stored[s], 32 * j)
                    norm_rows(act, vv[:, s], sd[:, s, :], off[:, s, :],
                              xo[:, s, :, :, :].rearrange("p k g f -> p (k g) f")).then_inc(normed, 1)

                def root(c, j, s):
                    act.wait_ge(measured, c + 1)
                    act.activation(sd[:, s, :], mv[:, s, :, 1], ACT.Sqrt, bias=env.eps[:, 2:3]).then_inc(rooted, 1)
                pipeline(st, CH, NS, (3, root), (4, apply), (0, copy), (1, bias))

            @block.tensor
            def _(pe):
                def turn(c, j, s):
                    pe.wait_ge(differed, c + 1)
                    if not (first(j) and s == 0):
                        pe.wait_ge(copied_x, c)
                        pe.wait_ge(copied_d, c)
                    transpose4(pe, env, ta, xd[:, s, :, :])
                    transpose4(pe, env, tb, df[:, s, :, :]).then_inc(turned, 1)

                def mix(c, j, s):
                    pe.wait_ge(copied_x, c + 1)
                    pe.wait_ge(copied_d, c + 1)
                    if not (first(j) and s == 0):
                        pe.wait_ge(scanned, c)
                    pe.matmul(pm[:, :], env.wi, xt[:, s, :], start=True, stop=False)
                    pe.matmul(pm[:, :], env.wj, dt_[:, s, :], start=False, stop=True).then_inc(mixed, 1)

                def back(c, j, s):
                    pe.wait_ge(maxed, c + 1)
                    if not (first(j) and s < 2):
                        pe.wait_ge(added, c - 1)
                    for g in range(G):
                        last = pe.transpose(tr[s % 2][:, g * F:(g + 1) * F], am[:, s, g * P:(g + 1) * P], env.ident[:, :])
                    last.then_inc(returned, 1)
                pipeline(Steps(pe, own), CH, NS, (0, turn), (2, back), (0, mix))


def parts_of(c):
    return TP if isinstance(c, int) and c == DC - 1 else P


def node_rows(ap, c):
    if isinstance(c, int) and c == DC - 1:
        return ap[c * W:N, :].rearrange("(p g) f -> p (g f)", g=G)
    return ap[bass.ds(c * W, W), :].rearrange("(p g) f -> p (g f)", g=G)


def columns(ap, c, wide=W, base=0):
    return ap[:, bass.ds(c * W + base, wide)]


def dense_front(nc, env, A, D):
    with ExitStack() as ctx:
        m = Mem(nc, ctx, "df")
        x, xb, free = m.sb("x", NS, G, F), m.sb("xb", NS, G, F), m.sb("free", DC * G)
        xt, hid, x3 = m.sb("xt", NS, W), m.sb("hid", NS, W), m.sb("x3", NS, G, F)
        x3t, h = m.sb("x3t", NS, W), m.sb("h", NS, W)
        va, stats, mv, sd = m.sb("va", 2, G, F), m.sb("stats", 2, G, 6), m.sb("mv", 2, G, 2), m.sb("sd", 2, G)
        vv, stats2 = m.sb("vv", NS, G, F), m.sb("stats2", 2, G, 6)
        mv2, sd2, off2 = m.sb("mv2", NS, G, 2), m.sb("sd2", NS, G), m.sb("off2", NS, G)
        tx, ph, po, tx3, pa = (m.ps(n) for n in ("tx", "ph", "po", "tx3", "pa"))
        (filled, stored, h_stored, masked, with_bias, turned, copied, hidden, relued, projected, added, measured,
         rooted, measured2, rooted2, scaled, normed, turned3, copied3, mapped, biased, own,
         sampled, inverted, mixed, sampled2, inverted2, zeroed, cols_in, keyed, keys_out, keys_in, bounded,
         bounds_out, rest_in, rest_got, rest_out) = m.sems(
            "filled* stored* h_stored* masked with_bias turned copied hidden relued projected added measured rooted "
            "measured2 rooted2 scaled normed turned3 copied3 mapped biased own sampled inverted mixed sampled2 "
            "inverted2 zeroed cols_in keyed keys_out keys_in* bounded* bounds_out* rest_in rest_got rest_out")
        cf, ci = m.sb("cf", T, 4), m.sb("ci", T, 2, dt=i32)
        key, bounds = m.sb("key", NS, 2, dt=i32), m.sb("bounds", NS, 2, 4, dt=i32)
        more = T - DC
        key_r, bounds_r = m.sb("key_r", more, 2, dt=i32), m.sb("bounds_r", more, 2, 4, dt=i32)
        kv = D["keys_i"].rearrange("p (t k) -> p t k", k=2)
        bv = D["edge_bounds"].rearrange("p (t k b) -> p t k b", k=2, b=4)
        freev = D["free"].rearrange("(c p g) -> p c g", c=DC, g=G)
        with nc.Block() as block:
            @block.sync
            def _(sp):
                def load(c, j, s):
                    n = parts_of(c)
                    if not first(j):
                        sp.wait_ge(turned, c + 1 - NS)
                        sp.wait_ge(with_bias, c + 1 - NS)
                        sp.sem_inc(own, 1)
                    sp.dma_start(x[0:n, s, :, :].rearrange("p g f -> p (g f)"), node_rows(A["x"], c))\
                        .then_inc(filled[s], 16)

                def store(c, j, s):
                    n = parts_of(c)
                    sp.wait_ge(normed, c + 1)
                    sp.sem_inc(own, 1)
                    sp.dma_start(node_rows(D["x3n"], c), x3[0:n, s, :, :].rearrange("p g f -> p (g f)"))\
                        .then_inc(stored[s], 16)

                def store_h(c, j, s):
                    n = parts_of(c)
                    sp.wait_ge(biased, c + 1)
                    sp.sem_inc(own, 1)
                    sp.dma_start(columns(D["za"], c, n * G), h[:, s, 0:n * G]).then_inc(h_stored[s], 16)

                def load_keys(t, j, s):
                    if not first(j):
                        sp.wait_ge(bounded[s], 32 * j)
                    sp.sem_inc(own, 1)
                    sp.dma_start(key[:, s, :], kv[:, t, :]).then_inc(keys_in[s], 16)

                def store_bounds(t, j, s):
                    sp.wait_ge(bounded[s], 32 * (j + 1))
                    sp.sem_inc(own, 1)
                    sp.dma_start(bv[:, t, :, :].rearrange("p k b -> p (k b)"),
                                 bounds[:, s, :, :].rearrange("p k b -> p (k b)")).then_inc(bounds_out[s], 16)
                sp.dma_start(cf[:, :, :].rearrange("p t k -> p (t k)"), D["cols_s"]).then_inc(cols_in, 16)
                sp.dma_start(free[:, :].rearrange("p (c g) -> p c g", g=G), freev).then_inc(masked, 16)
                sp.wait_ge(keyed, 1)
                sp.dma_start(D["keys_i"], ci[:, :, :].rearrange("p t k -> p (t k)")).then_inc(keys_out, 16)
                sp.wait_ge(keys_out, 16)
                pipeline(Steps(sp, own), DC, NS, (0, load), (0, load_keys), (3, store_bounds), (7, store), (9, store_h))
                for s in range(NS):
                    sp.wait_ge(bounds_out[s], 16 * uses(s, DC))
                    sp.wait_ge(stored[s], 16 * uses(s, DC))
                    sp.wait_ge(h_stored[s], 16 * uses(s, DC))

            @block.gpsimd
            def _(pool):
                def offset(c, j, s):
                    n = parts_of(c)
                    pool.wait_ge(filled[s], 16 * (j + 1))
                    if not first(j):
                        pool.wait_ge(added, c + 1 - NS)
                    pool.tensor_tensor(xb[0:n, s, :, :], x[0:n, s, :, :], spread(env.bc["L0_gnn_b2"][0:n, :]),
                                       ALU.add).then_inc(with_bias, 1)

                def gather(t, j, s):
                    pool.wait_ge(keys_in[s], 16 * (j + 1))
                    if not first(j):
                        pool.wait_ge(bounds_out[s], 16 * j)
                    pool.sem_inc(own, 1)
                    for k in range(2):
                        pool.indirect_dma_start(
                            out=bounds[:, s, k, :], out_offset=None, in_=D["bounds"][:, :],
                            in_offset=bass.IndirectOffsetOnAxis(ap=key[:, s, k:k + 1], axis=0))\
                            .then_inc(bounded[s], 16)
                pipeline(Steps(pool, own), DC, NS, (0, offset), (0, gather))
                pool.dma_start(key_r[:, :, :], kv[:, DC:T, :]).then_inc(rest_in, 16)
                pool.wait_ge(rest_in, 16)
                pool.sem_inc(own, 1)
                for t in range(more):
                    for k in range(2):
                        pool.indirect_dma_start(
                            out=bounds_r[:, t, k, :], out_offset=None, in_=D["bounds"][:, :],
                            in_offset=bass.IndirectOffsetOnAxis(ap=key_r[:, t, k:k + 1], axis=0))\
                            .then_inc(rest_got, 16)
                pool.wait_ge(rest_got, 32 * more)
                pool.dma_start(bv[:, DC:T, :, :].rearrange("p t k b -> p (t k b)"),
                               bounds_r[:, :, :, :].rearrange("p t k b -> p (t k b)")).then_inc(rest_out, 16)
                pool.wait_ge(rest_out, 16)

            @block.vector
            def _(v):
                def add(c, j, s):
                    n, b = parts_of(c), s % 2
                    v.wait_ge(projected, c + 1)
                    v.wait_ge(with_bias, c + 1)
                    v.tensor_tensor(va[0:n, b, :, :], po[0:n, :].rearrange("p (g f) -> p g f", g=G),
                                    xb[0:n, s, :, :], ALU.add).then_inc(added, 1)

                def sample(c, j, s):
                    n, b = parts_of(c), s % 2
                    v.wait_ge(added, c + 1)
                    for g in range(G):
                        last = v.bn_stats(stats[0:n, b, g, :], va[0:n, b, g, :])
                    last.then_inc(sampled, 1)

                def measure(c, j, s):
                    n, b = parts_of(c), s % 2
                    v.wait_ge(sampled, c + 1)
                    v.sem_inc(own, 1)
                    for g in range(G):
                        last = v.bn_aggr(mv[0:n, b, g, :], stats[0:n, b, g, :])
                    last.then_inc(measured, 1)

                def invert(c, j, s):
                    n, b = parts_of(c), s % 2
                    v.wait_ge(rooted, c + 1)
                    v.reciprocal(sd[0:n, b, :], sd[0:n, b, :]).then_inc(inverted, 1)

                def mix(c, j, s):
                    n, b = parts_of(c), s % 2
                    v.wait_ge(inverted, c + 1)
                    for g in range(G):
                        last = v.scalar_tensor_tensor(
                            out=vv[0:n, s, g, :], in0=va[0:n, b, g, :], scalar=sd[0:n, b, g:g + 1],
                            in1=env.h0[0:n, :], op0=ALU.mult, op1=ALU.add)
                    last.then_inc(mixed, 1)

                def sample2(c, j, s):
                    n, b = parts_of(c), s % 2
                    v.wait_ge(mixed, c + 1)
                    for g in range(G):
                        last = v.bn_stats(stats2[0:n, b, g, :], vv[0:n, s, g, :])
                    last.then_inc(sampled2, 1)

                def measure2(c, j, s):
                    n, b = parts_of(c), s % 2
                    v.wait_ge(sampled2, c + 1)
                    v.sem_inc(own, 1)
                    for g in range(G):
                        last = v.bn_aggr(mv2[0:n, s, g, :], stats2[0:n, b, g, :])
                    last.then_inc(measured2, 1)

                def invert2(c, j, s):
                    n = parts_of(c)
                    v.wait_ge(rooted2, c + 1)
                    v.reciprocal(sd2[0:n, s, :], sd2[0:n, s, :]).then_inc(inverted2, 1)

                def mask(c, j, s):
                    n = parts_of(c)
                    v.wait_ge(inverted2, c + 1)
                    v.tensor_tensor(sd2[0:n, s, :], sd2[0:n, s, :], free[0:n, bass.ds(c * G, G)], ALU.mult)\
                        .then_inc(zeroed, 1)

                def offset(c, j, s):
                    n = parts_of(c)
                    v.wait_ge(zeroed, c + 1)
                    v.scalar_tensor_tensor(out=off2[0:n, s, :], in0=mv2[0:n, s, :, 0], scalar=-1.0,
                                           in1=sd2[0:n, s, :], op0=ALU.mult, op1=ALU.mult).then_inc(scaled, 1)
                v.wait_ge(cols_in, 16)
                v.tensor_copy(ci[:, :, :], cf[:, :, 0:2]).then_inc(keyed, 1)
                v.wait_ge(masked, 16)
                pipeline(Steps(v, own), DC, NS, (3, invert), (4, invert2), (2, add), (3, mix), (4, mask), (2, sample),
                         (3, sample2), (4, offset), (2, measure), (3, measure2))

            @block.scalar
            def _(act):
                def copy(c, j, s):
                    n = parts_of(c) * G
                    act.wait_ge(turned, c + 1)
                    act.activation(xt[:, s, 0:n], tx[:, 0:n], ACT.Copy).then_inc(copied, 1)

                def relu(c, j, s):
                    n = parts_of(c) * G
                    act.wait_ge(hidden, c + 1)
                    act.activation(hid[:, s, 0:n], ph[:, 0:n], ACT.Relu, bias=env.col["L0_gnn_b1"]).then_inc(relued, 1)

                def root(c, j, s):
                    n = parts_of(c)
                    act.wait_ge(measured, c + 1)
                    act.activation(sd[0:n, s % 2, :], mv[0:n, s % 2, :, 1], ACT.Sqrt, scale=0.25,
                                   bias=env.eps[0:n, 0:1]).then_inc(rooted, 1)

                def root2(c, j, s):
                    n = parts_of(c)
                    act.wait_ge(measured2, c + 1)
                    act.activation(sd2[0:n, s, :], mv2[0:n, s, :, 1], ACT.Sqrt, scale=1.0 + LN_EPS,
                                   bias=env.eps[0:n, 1:2]).then_inc(rooted2, 1)

                def norm(c, j, s):
                    n = parts_of(c)
                    act.wait_ge(scaled, c + 1)
                    if not first(j):
                        act.wait_ge(stored[s], 16 * j)
                    for g in range(G):
                        last = act.activation(x3[0:n, s, g, :], vv[0:n, s, g, :], ACT.Identity,
                                              scale=sd2[0:n, s, g:g + 1], bias=off2[0:n, s, g:g + 1])
                    last.then_inc(normed, 1)

                def copy3(c, j, s):
                    n = parts_of(c) * G
                    act.wait_ge(turned3, c + 1)
                    if not first(j):
                        act.wait_ge(mapped, c + 1 - NS)
                    act.activation(x3t[:, s, 0:n], tx3[:, 0:n], ACT.Copy).then_inc(copied3, 1)

                def bias(c, j, s):
                    n = parts_of(c) * G
                    act.wait_ge(mapped, c + 1)
                    if not first(j):
                        act.wait_ge(h_stored[s], 16 * j)
                    act.activation(h[:, s, 0:n], pa[:, 0:n], ACT.Identity, bias=env.col["L3_gnn_b_atom"])\
                        .then_inc(biased, 1)
                pipeline(Steps(act, own), DC, NS, (4, root2), (3, root), (5, norm), (7, bias), (6, copy3), (1, relu),
                         (0, copy))

            @block.tensor
            def _(pe):
                def turn(c, j, s):
                    n = parts_of(c)
                    pe.wait_ge(filled[s], 16 * (j + 1))
                    if not (first(j) and s == 0):
                        pe.wait_ge(copied, c)
                    transpose4(pe, env, tx, x[0:n, s, :, :], n).then_inc(turned, 1)

                def hide(c, j, s):
                    n = parts_of(c) * G
                    pe.wait_ge(copied, c + 1)
                    if not (first(j) and s == 0):
                        pe.wait_ge(relued, c)
                    pe.matmul(ph[:, 0:n], env.w["L0_gnn_W1"], xt[:, s, 0:n], start=True, stop=True).then_inc(hidden, 1)

                def project(c, j, s):
                    n = parts_of(c)
                    pe.wait_ge(relued, c + 1)
                    if not (first(j) and s == 0):
                        pe.wait_ge(added, c)
                    to_rows4(pe, po, hid[:, s, :], env.w["L0_gnn_W2"], n).then_inc(projected, 1)

                def turn3(c, j, s):
                    n = parts_of(c)
                    pe.wait_ge(normed, c + 1)
                    if not (first(j) and s == 0):
                        pe.wait_ge(copied3, c)
                    transpose4(pe, env, tx3, x3[0:n, s, :, :], n).then_inc(turned3, 1)

                def atom(c, j, s):
                    n = parts_of(c) * G
                    pe.wait_ge(copied3, c + 1)
                    if not (first(j) and s == 0):
                        pe.wait_ge(biased, c)
                    pe.matmul(pa[:, 0:n], env.w["L3_gnn_W_atom"], x3t[:, s, 0:n], start=True, stop=True)\
                        .then_inc(mapped, 1)
                pipeline(Steps(pe, own), DC, NS, (7, atom), (6, turn3), (2, project), (1, hide), (0, turn))


def slot_states(nc, env, D):
    with ExitStack() as ctx:
        m = Mem(nc, ctx, "ss")
        x, xt, o, ot = m.sb("x", NS, G, F), m.sb("xt", NS, W), m.sb("o", NS, G, F), m.sb("ot", NS, W)
        tx, pt, pr = m.ps("tx"), [m.ps("pt0"), m.ps("pt1")], [m.ps("pr0"), m.ps("pr1")]
        filled, stored, turned, copied, mapped, rows_out, cols_out, own = m.sems(
            "filled* stored* turned copied mapped rows_out cols_out own")

        def run(edges, base, uses_before, stored_before, count):
            source = D["edges"][:, 0:F] if edges else D["x3"]
            target = D["ea"] if edges else D["hd"]
            each = 16 if edges else 32
            with nc.Block() as block:
                @block.sync
                def _(sp):
                    def load(c, j, s):
                        if not first(j):
                            sp.wait_ge(turned, base + c + 1 - NS)
                            sp.sem_inc(own, 1)
                        sp.dma_start(x[:, s, :, :], rows4(source, c)).then_inc(filled[s], 16)

                    def store(c, j, s):
                        sp.wait_ge(cols_out, base + c + 1)
                        sp.sem_inc(own, 1)
                        sp.dma_start(columns(target, c), ot[:, s, :]).then_inc(stored[s], 16)
                        if not edges:
                            sp.wait_ge(rows_out, c + 1)
                            sp.sem_inc(own, 1)
                            sp.dma_start(rows4(D["hr"], c), o[:, s, :, :]).then_inc(stored[s], 16)
                    pipeline(Steps(sp, own), count, NS, (0, load), (NS, store))
                    for s in range(NS):
                        sp.wait_ge(stored[s], stored_before[s] + each * uses(s, count))

                @block.scalar
                def _(act):
                    def copy(c, j, s):
                        act.wait_ge(turned, base + c + 1)
                        act.activation(xt[:, s, :], tx[:, :], ACT.Copy).then_inc(copied, 1)

                    def rows(c, j, s):
                        act.wait_ge(mapped, c + 1)
                        if not first(j):
                            act.wait_ge(stored[s], each * j)
                        act.activation(o[:, s, :, :], pr[s % 2][:, :].rearrange("p (g f) -> p g f", g=G), ACT.Copy)\
                            .then_inc(rows_out, 1)
                    if edges:
                        pipeline(Steps(act, own), count, NS, (0, copy))
                    else:
                        pipeline(Steps(act, own), count, NS, (0, copy), (1, rows))

                @block.vector
                def _(v):
                    def cols(c, j, s):
                        v.wait_ge(mapped, base + c + 1)
                        if not first(j) or edges:
                            v.wait_ge(stored[s], stored_before[s] + each * j)
                        if edges:
                            v.tensor_scalar(ot[:, s, :], pt[s % 2][:, :], env.col["L3_gnn_b_bond"], None, ALU.add)\
                                .then_inc(cols_out, 1)
                        else:
                            v.tensor_copy(ot[:, s, :], pt[s % 2][:, :]).then_inc(cols_out, 1)
                    pipeline(Steps(v, own), count, NS, (1, cols))

                @block.tensor
                def _(pe):
                    def turn(c, j, s):
                        pe.wait_ge(filled[s], 16 * (uses_before[s] + j + 1))
                        if edges or not (first(j) and s == 0):
                            pe.wait_ge(copied, base + c)
                        transpose4(pe, env, tx, x[:, s, :, :]).then_inc(turned, 1)

                    def apply(c, j, s):
                        pe.wait_ge(copied, base + c + 1)
                        if edges or not (first(j) and s < 2):
                            pe.wait_ge(cols_out, base + c - 1)
                        last = pe.matmul(pt[s % 2][:, :], env.w["L3_gnn_W_bond" if edges else "L3_gnn_W_atom"],
                                         xt[:, s, :], start=True, stop=True)
                        if not edges:
                            if not (first(j) and s < 2):
                                pe.wait_ge(rows_out, c - 1)
                            last = to_rows4(pe, pr[s % 2], xt[:, s, :], env.w["L3_gnn_W_atom"])
                        last.then_inc(mapped, 1)
                    pipeline(Steps(pe, own), count, NS, (0, turn), (1, apply))
        none = [0] * NS
        run(False, 0, none, none, 2 * CH)
        before = [uses(s, 2 * CH) for s in range(NS)]
        run(True, 2 * CH, before, [32 * n for n in before], CH)


def gather_states(nc, env, D, i, z, states, prev, stats, slot_sums, z_sums):
    func, scale, shift = prev
    lead = 2 if i else 0
    with ExitStack() as ctx:
        m = Mem(nc, ctx, f"gs{i}")
        ix, keep = m.sb("ix", 2, G * NIX, dt=i32), m.sb("keep", 2, W)
        hs, hd, ea = m.sb("hs", 2, G, F), m.sb("hd", 2, W), m.sb("ea", 2, W)
        hn, hdn = m.sb("hn", 2, W), m.sb("hdn", 2, W)
        ms, agg, zd, zs = m.sb("ms", 2, W), m.sb("agg", 2, W), m.sb("zd", 2, W), m.sb("zs", 2, W)
        wt, junk, sq = m.sb("wt", 2, 2, W), m.sb("junk", 4, W), m.sb("sq", 2, W)
        px = [m.ps("px0"), m.ps("px1")]
        zn = m.sb("zn", NS, W)
        h = m.sb("h", NS, W) if i else zn
        ts = [m.ps("ts0"), m.ps("ts1")]
        p1 = [[m.ps(f"p1{a}{b}") for b in range(2)] for a in range(2)]
        (index_in, filled, got, stored, turned, stated, summed, scaled, relued, scanned, done, nodes_in, made, multiplied,
         measured, own, weights_in, slots_multiplied, squared, weighed, totalled) = m.sems("index_in*2 filled*2 got*2 stored*2 turned stated summed scaled relued scanned done nodes_in* "
                                 "made multiplied measured own weights_in*2 slots_multiplied squared weighed totalled")
        iv, fv, kv = views(D)
        wv = D["weights"].rearrange("(c w) -> c w", w=W)
        with nc.Block() as block:
            @block.sync
            def _(sp):
                def load_index(c, j, s):
                    if not first(j):
                        sp.wait_ge(got[s], 64 * j)
                        sp.sem_inc(own, 1)
                    sp.dma_start(ix[:, s, :], iv[:, c, :]).then_inc(index_in[s], 16)

                def load(c, j, s):
                    if not first(j):
                        sp.wait_ge(done, c - 1)
                        sp.sem_inc(own, 1)
                    sp.dma_start(keep[:, s, :], kv[bass.ds(c, 1), :].broadcast_to([P, W])).then_inc(filled[s], 16)
                    sp.dma_start(hd[:, s, :], states(c)).then_inc(filled[s], 16)
                    sp.dma_start(ea[:, s, :], columns(D["ea"], c)).then_inc(filled[s], 16)

                def store(c, j, s):
                    sp.wait_ge(done, c + 1)
                    sp.sem_inc(own, 1)
                    sp.dma_start(columns(z, c, W, SLOT0), zd[:, s, :]).then_inc(stored[s], 16)
                    sp.dma_start(columns(z, c, W, SLOT0 + EP), zs[:, s, :]).then_inc(stored[s], 16)

                def load_weights(c, j, s):
                    if not first(j):
                        sp.wait_ge(weighed, 2 * (c - 1))
                        sp.sem_inc(own, 1)
                    for half in range(2):
                        sp.dma_start(wt[:, s, half, :], wv[bass.ds(c + half * CH, 1), :].broadcast_to([P, W]))\
                            .then_inc(weights_in[s], 16)

                def load_nodes(c, j, s):
                    n = parts_of(c) * G
                    if not first(j):
                        sp.wait_ge(made if i else measured, c + 1 - NS)
                        sp.sem_inc(own, 1)
                    sp.dma_start(zn[:, s, 0:n], columns(z, c, n)).then_inc(nodes_in[s], 16)
                weave(Steps(sp, own), DC, [(0, load_nodes)], [(1, load_index), (6, load), (11, load_weights), (14, store)])
                for s in range(2):
                    sp.wait_ge(stored[s], 32 * PAIRS)

            @block.gpsimd
            def _(pool):
                def gather(c, j, s):
                    pool.wait_ge(index_in[s], 16 * (j + 1))
                    if not first(j):
                        pool.wait_ge(turned, c - 1)
                    pool.sem_inc(own, 1)
                    gather4(pool, hs[:, s, :, :], D["hr"], ix[:, s, :], IX_SRC_D, got[s])
                pipeline(Steps(pool, own), CH, 2, (0, gather))

            @block.tensor
            def _(pe):
                def turn(c, j, s):
                    pe.wait_ge(got[s], 64 * (j + 1))
                    if not first(j):
                        pe.wait_ge(stated, c - 1)
                    transpose4(pe, env, ts[s], hs[:, s, :, :]).then_inc(turned, 1)

                def multiply_slots(half):
                    def run(c, j, s):
                        pe.wait_ge(done, c + 1)
                        if half or not (first(j) and s == 0):
                            pe.wait_ge(squared, 2 * c + half)
                        for k in range(2):
                            last = pe.matmul(px[k][:, :], env.w1[:, i, k * F:(k + 1) * F], (zd, zs)[half][:, s, :],
                                             start=True, stop=True)
                        last.then_inc(slots_multiplied, 1)
                    return run

                def multiply(c, j, s):
                    n = parts_of(c) * G
                    if i:
                        pe.wait_ge(made, c + 1)
                    else:
                        pe.wait_ge(nodes_in[s], 16 * (j + 1))
                    if not (first(j) and s < 2):
                        pe.wait_ge(measured, c - 1)
                    for k in range(2):
                        last = pe.matmul(p1[s % 2][k][:, 0:n], env.w1e[:, i, k * F:(k + 1) * F], h[:, s, 0:n],
                                         start=True, stop=True)
                    last.then_inc(multiplied, 1)
                weave(Steps(pe, own), DC, [(lead, multiply)], [(4, turn), (10, multiply_slots(0)), (12, multiply_slots(1))])

            @block.scalar
            def _(act):
                def make(c, j, s):
                    n = parts_of(c) * G
                    act.wait_ge(nodes_in[s], 16 * (j + 1))
                    if not first(j):
                        act.wait_ge(multiplied, c + 1 - NS)
                    act.activation(h[:, s, 0:n], zn[:, s, 0:n], ACT.Relu, scale=scale, bias=shift).then_inc(made, 1)

                def state(c, j, s):
                    act.wait_ge(turned, c + 1)
                    act.wait_ge(filled[s], 48 * (j + 1))
                    if not first(j):
                        act.wait_ge(scaled, c - 1)
                    act.activation(hn[:, s, :], ts[s][:, :], func, scale=scale, bias=shift)
                    act.activation(hdn[:, s, :], hd[:, s, :], func, scale=scale, bias=shift).then_inc(stated, 1)

                def relu(c, j, s):
                    act.wait_ge(summed, c + 1)
                    act.activation(ms[:, s, :], ms[:, s, :], ACT.Relu).then_inc(relued, 1)

                def square(half):
                    def run(c, j, s):
                        act.wait_ge(slots_multiplied, 2 * c + 1 + half)
                        if half or not (first(j) and s == 0):
                            act.wait_ge(weighed, 2 * c + half)
                        for k in range(2):
                            last = act.activation(sq[:, k, :], px[k][:, :], ACT.Square)
                        last.then_inc(squared, 1)
                    return run
                weave(Steps(act, own), DC, [(0, make)] if i else [],
                      [(5, state), (7, relu), (11, square(0)), (13, square(1))])

            @block.vector
            def _(v):
                def measure(c, j, s):
                    n = parts_of(c) * G
                    v.wait_ge(multiplied, c + 1)
                    for k in range(2):
                        last = v.bn_stats(stats[:, k, c, :], p1[s % 2][k][:, 0:n])
                    last.then_inc(measured, 1)

                def add(c, j, s):
                    v.wait_ge(stated, c + 1)
                    if not first(j):
                        v.wait_ge(stored[s], 32 * j)
                        v.wait_ge(slots_multiplied, 2 * (c - 1))
                    v.tensor_tensor(ms[:, s, :], hn[:, s, :], ea[:, s, :], ALU.add).then_inc(summed, 1)
                    v.tensor_scalar(zs[:, s, :], hn[:, s, :], env.onep[:, i:i + 1], None, ALU.mult)\
                        .then_inc(scaled, 1)

                def scan(c, j, s):
                    v.wait_ge(relued, c + 1)
                    start = 0.0 if first(j) and s == 0 else agg[:, 1 - s, W - 1:W]
                    v.tensor_tensor_scan(out=agg[:, s, :], data0=keep[:, s, :], data1=ms[:, s, :], initial=start,
                                         op0=ALU.mult, op1=ALU.add).then_inc(scanned, 1)

                def join(c, j, s):
                    v.wait_ge(scanned, c + 1)
                    v.scalar_tensor_tensor(out=zd[:, s, :], in0=hdn[:, s, :], scalar=env.onep[:, i:i + 1],
                                           in1=agg[:, s, :], op0=ALU.mult, op1=ALU.add).then_inc(done, 1)

                def total(c, j, s):
                    v.wait_ge(done, c + 1)
                    v.wait_ge(weights_in[s], 32 * (j + 1))
                    if not (first(j) and s == 0):
                        v.wait_ge(totalled, c)
                    for half in range(2):
                        last = v.scalar_tensor_tensor(
                            out=junk[:, half, :], in0=(zd, zs)[half][:, s, :], scalar=1.0, in1=wt[:, s, half, :],
                            op0=ALU.mult, op1=ALU.mult, accum_out=z_sums[:, half, c, 0:1])
                    last.then_inc(totalled, 1)

                def weigh(half):
                    def run(c, j, s):
                        v.wait_ge(squared, 2 * c + 1 + half)
                        if half or not (first(j) and s == 0):
                            v.wait_ge(weighed, 2 * c + half)
                        for k in range(2):
                            last = v.scalar_tensor_tensor(
                                out=junk[:, 2 + k, :], in0=sq[:, k, :], scalar=1.0, in1=wt[:, s, half, :],
                                op0=ALU.mult, op1=ALU.mult, accum_out=slot_sums[:, k, c + half * CH, 1:2])
                        last.then_inc(weighed, 1)
                    return run
                weave(Steps(v, own), DC, [(lead, measure)],
                      [(6, add), (8, scan), (9, join), (10, total), (12, weigh(0)), (14, weigh(1))])


def norm_constants(nc, env, tag, halves, bias, gain, offset, nodes, slots, out, linear=None):
    with ExitStack() as ctx:
        m = Mem(nc, ctx, tag)
        mv, t, sm = m.sb("mv", halves, 2), m.sb("t", 4, halves), m.sb("sm", halves, 2)
        measured, rooted, own, totalled, multiplied = m.sems("measured rooted own totalled multiplied")
        zt, pz = m.sb("zt", 1), m.ps("pz")
        with nc.Block() as block:
            @block.vector
            def _(v):
                st = Steps(v, own)

                def do(ins):
                    ins.then_inc(own, one(st))
                    v.wait_ge(own, steps(st))
                for k in range(halves):
                    v.bn_aggr(mv[:, k, :], nodes[:, k, :, :]).then_inc(own, one(st))
                    if linear is None:
                        v.reduce_sum(sm[:, k, 0:1], slots[:, k, :, 0], axis=mybir.AxisListType.X)\
                            .then_inc(own, one(st))
                    v.reduce_sum(sm[:, k, 1:2], slots[:, k, :, 1], axis=mybir.AxisListType.X).then_inc(own, one(st))
                if linear is not None:
                    do(v.reduce_sum(zt[:, :], linear[0][:, :, :, 0].rearrange("p h c -> p (h c)"),
                                    axis=mybir.AxisListType.X))
                    v.sem_inc(totalled, 1)
                    v.wait_ge(multiplied, 1)
                    do(v.tensor_copy(sm[:, :, 0], pz[:, 0:halves]))
                v.wait_ge(own, steps(st))
                do(v.tensor_scalar(sm[:, :, :], sm[:, :, :], 1.0 / N, None, ALU.mult))
                do(v.tensor_tensor(t[:, 0, :], mv[:, :, 0], mv[:, :, 0], ALU.mult))
                do(v.tensor_tensor(t[:, 0, :], t[:, 0, :], mv[:, :, 1], ALU.add))
                do(v.tensor_tensor(t[:, 0, :], t[:, 0, :], sm[:, :, 1], ALU.add))
                do(v.tensor_tensor(t[:, 1, :], mv[:, :, 0], sm[:, :, 0], ALU.add))
                do(v.tensor_tensor(t[:, 2, :], t[:, 1, :], t[:, 1, :], ALU.mult))
                do(v.tensor_tensor(t[:, 0, :], t[:, 0, :], t[:, 2, :], ALU.subtract))
                do(v.tensor_scalar(t[:, 0, :], t[:, 0, :], BN_EPS, None, ALU.add))
                v.wait_ge(own, steps(st))
                v.sem_inc(measured, 1)
                v.wait_ge(rooted, 1)
                do(v.reciprocal(t[:, 2, :], t[:, 3, :]))
                do(v.tensor_tensor(out[:, 0, 0:halves], t[:, 2, :], gain, ALU.mult))
                do(v.tensor_tensor(t[:, 1, :], t[:, 1, :], bias, ALU.add))
                do(v.tensor_tensor(t[:, 1, :], bias, t[:, 1, :], ALU.subtract))
                do(v.tensor_tensor(t[:, 1, :], t[:, 1, :], out[:, 0, 0:halves], ALU.mult))
                do(v.tensor_tensor(out[:, 1, 0:halves], t[:, 1, :], offset, ALU.add))

            if linear is not None:
                @block.tensor
                def _(pe):
                    pe.wait_ge(totalled, 1)
                    for k in range(halves):
                        last = pe.matmul(pz[:, k:k + 1], linear[1][:, k * F:(k + 1) * F], zt[:, :],
                                         start=True, stop=True)
                    last.then_inc(multiplied, 1)

            @block.scalar
            def _(act):
                act.wait_ge(measured, 1)
                act.activation(t[:, 3, :], t[:, 0, :], ACT.Sqrt).then_inc(rooted, 1)


def column_pass(nc, env, D, i, which, slots, source, target, prev, norm1, stats,
                rows=False):
    tag = f"p{which}{'s' if slots else 'n'}{i}"
    count = 2 * CH if slots else DC
    base = SLOT0 if slots else 0
    w1 = env.w1 if slots else env.w1e
    halves = 2 if which == "a" else 1
    with ExitStack() as ctx:
        m = Mem(nc, ctx, tag)
        z, wt = m.sb("z", NS, W), m.sb("wt", NS, W)
        h = m.sb("h", NS, W) if prev is not None else z
        y, z2, scr = m.sb("y", NS, 2, W), m.sb("z2", NS, W), m.sb("scr", 4, W)
        p1 = [[m.ps(f"p1{a}{b}") for b in range(2)] for a in range(2)]
        p2 = [m.ps(f"p2{a}") for a in range(2)]
        if rows:
            r, pr = m.sb("r", NS, G, F), [m.ps("pr0"), m.ps("pr1")]
        (filled, stored, made, multiplied, relued, projected, done, own_v, own_a, own, turned, rows_out,
         written, rows_stored) = m.sems(
            "filled* stored* made multiplied relued projected done own_v own_a own turned rows_out written rows_stored*")

        def wide(c):
            return W if slots else parts_of(c) * G
        loads = 32 if slots else 16
        with nc.Block() as block:
            @block.sync
            def _(sp):
                def load(c, j, s):
                    if not first(j):
                        sp.wait_ge(done, c + 1 - NS)
                        sp.sem_inc(own, 1)
                    sp.dma_start(z[:, s, 0:wide(c)], columns(source, c, wide(c), base)).then_inc(filled[s], 16)
                    if slots:
                        sp.dma_start(wt[:, s, :], D["weights"].rearrange("(c w) -> c w", w=W)[bass.ds(c, 1), :]
                                     .broadcast_to([P, W])).then_inc(filled[s], 16)

                def store(c, j, s):
                    sp.wait_ge(done, c + 1)
                    sp.sem_inc(own, 1)
                    sp.dma_start(columns(target, c, wide(c), base), z2[:, s, 0:wide(c)]).then_inc(stored[s], 16)
                def store_rows(c, j, s):
                    sp.wait_ge(rows_out, c + 1)
                    sp.sem_inc(own, 1)
                    sp.dma_start(rows4(D["hr"], c), r[:, s, :, :]).then_inc(rows_stored[s], 16)
                if which == "a":
                    pipeline(Steps(sp, own), count, NS, (0, load))
                elif rows:
                    pipeline(Steps(sp, own), count, NS, (0, load), (NS, store), (6, store_rows))
                    for s in range(NS):
                        sp.wait_ge(stored[s], 16 * uses(s, count))
                        sp.wait_ge(rows_stored[s], 16 * uses(s, count))
                else:
                    pipeline(Steps(sp, own), count, NS, (0, load), (NS, store))
                    for s in range(NS):
                        sp.wait_ge(stored[s], 16 * uses(s, count))

            @block.scalar
            def _(act):
                st = Steps(act, own_a)

                def make(c, j, s):
                    act.wait_ge(filled[s], loads * (j + 1))
                    if not first(j):
                        act.wait_ge(multiplied, c + 1 - NS)
                    act.activation(h[:, s, 0:wide(c)], z[:, s, 0:wide(c)], ACT.Relu, scale=prev[0], bias=prev[1])\
                        .then_inc(made, 1)

                def relu(c, j, s):
                    n = wide(c)
                    act.wait_ge(multiplied, c + 1)
                    if not first(j):
                        act.wait_ge(projected, c + 1 - NS)
                    for k in range(2):
                        act.activation(y[:, s, k, 0:n], p1[s % 2][k][:, 0:n], ACT.Relu,
                                              scale=norm1[:, 0, k:k + 1], bias=norm1[:, 1, k:k + 1]).then_inc(own_a, one(st))
                    act.wait_ge(own_a, steps(st))
                    act.sem_inc(relued, 1)

                def copy_rows(c, j, s):
                    act.wait_ge(turned, c + 1)
                    if not first(j):
                        act.wait_ge(rows_stored[s], 16 * j)
                    act.activation(r[:, s, :, :], pr[s % 2][:, :].rearrange("p (g f) -> p g f", g=G), ACT.Copy)\
                        .then_inc(rows_out, 1)
                stages = []
                if prev is not None:
                    stages.append((0, make))
                if which == "b":
                    stages.append((1, relu))
                if rows:
                    stages.append((3, copy_rows))
                if stages:
                    pipeline(st, count, NS, *stages)

            @block.tensor
            def _(pe):
                def multiply(c, j, s):
                    n = wide(c)
                    if prev is None:
                        pe.wait_ge(filled[s], loads * (j + 1))
                    else:
                        pe.wait_ge(made, c + 1)
                    if not (first(j) and s < 2):
                        pe.wait_ge(done if which == "a" else relued, c - 1)
                    for k in range(2):
                        last = pe.matmul(p1[s % 2][k][:, 0:n], w1[:, i, k * F:(k + 1) * F], h[:, s, 0:n],
                                         start=True, stop=True)
                    last.then_inc(multiplied, 1)

                def project(c, j, s):
                    n = wide(c)
                    pe.wait_ge(relued, c + 1)
                    if not (first(j) and s < 2):
                        pe.wait_ge(done, c - 1)
                    for k in range(2):
                        last = pe.matmul(p2[s % 2][:, 0:n], env.w2[:, i, k, :], y[:, s, k, 0:n],
                                         start=k == 0, stop=k == 1)
                    last.then_inc(projected, 1)
                def turn(c, j, s):
                    pe.wait_ge(written, c + 1)
                    if not (first(j) and s < 2):
                        pe.wait_ge(rows_out, c - 1)
                    for g in range(G):
                        last = pe.transpose(pr[s % 2][:, g * F:(g + 1) * F], z2[:, s, g * P:(g + 1) * P],
                                            env.ident[:, :])
                    last.then_inc(turned, 1)
                if which == "a":
                    pipeline(Steps(pe, own), count, NS, (0, multiply))
                elif rows:
                    pipeline(Steps(pe, own), count, NS, (0, multiply), (1, project), (2, turn))
                else:
                    pipeline(Steps(pe, own), count, NS, (0, multiply), (1, project))

            @block.vector
            def _(v):
                st = Steps(v, own_v)

                def measure(c, j, s):
                    n = wide(c)
                    v.wait_ge(multiplied if which == "a" else projected, c + 1)
                    if which == "b" and not first(j):
                        v.wait_ge(stored[s], 16 * j)
                        if rows:
                            v.wait_ge(turned, c + 1 - NS)
                    if which == "b":
                        v.tensor_copy(z2[:, s, 0:n], p2[s % 2][:, 0:n]).then_inc(written, 1)
                    ps = [p1[s % 2][k] if which == "a" else p2[s % 2] for k in range(halves)]
                    if slots:
                        v.wait_ge(filled[s], loads * (j + 1))
                        for k in range(halves):
                            v.scalar_tensor_tensor(out=scr[:, k, :], in0=ps[k][:, :], scalar=1.0, in1=wt[:, s, :],
                                                   op0=ALU.mult, op1=ALU.mult,
                                                   accum_out=stats[:, k, c, 0:1]).then_inc(own_v, one(st))
                        for k in range(halves):
                            v.wait_ge(own_v, steps(st) - halves + 1)
                            v.scalar_tensor_tensor(out=scr[:, 2 + k, :], in0=ps[k][:, :], scalar=1.0,
                                                   in1=scr[:, k, :], op0=ALU.mult, op1=ALU.mult,
                                                   accum_out=stats[:, k, c, 1:2]).then_inc(own_v, one(st))
                    else:
                        for k in range(halves):
                            v.bn_stats(stats[:, k, c, :], ps[k][:, 0:n]).then_inc(own_v, one(st))
                    v.wait_ge(own_v, steps(st))
                    v.sem_inc(done, 1)
                pipeline(st, count, NS, (0 if which == "a" else 1, measure))


def results(nc, env, D, out, slots, source, norm):
    tag = "rs" if slots else "rn"
    count = 2 * CH if slots else DC
    base = SLOT0 if slots else 0
    with ExitStack() as ctx:
        m = Mem(nc, ctx, tag)
        z, h, x3, ix = m.sb("z", NS, W), m.sb("h", NS, W), m.sb("x3", NS, G, F), m.sb("ix", NS, G * NIX, dt=i32)
        vv, stats, mv, sd, xo = m.sb("vv", NS, G, F), m.sb("stats", 2, G, 6), m.sb("mv", NS, G, 2), m.sb("sd", NS, G), m.sb("xo", NS, G, F)
        off = m.sb("off", NS, G)
        po = [m.ps("po0"), m.ps("po1")]
        (filled, rows_in, stored, made, with_bias, projected, added, sampled, measured, rooted, inverted, scaled,
         normed, own) = m.sems("filled* rows_in* stored* made with_bias projected added sampled measured rooted "
                               "inverted scaled normed own")
        iv, fv, kv = views(D)
        loads = 32

        def wide(c):
            return W if slots else parts_of(c) * G
        with nc.Block() as block:
            @block.sync
            def _(sp):
                def load(c, j, s):
                    n = wide(c)
                    if not first(j):
                        sp.wait_ge(added, c + 1 - NS)
                        sp.sem_inc(own, 1)
                    sp.dma_start(z[:, s, 0:n], columns(source, c, n, base)).then_inc(filled[s], 16)
                    if slots:
                        sp.dma_start(x3[:, s, :, :], rows4(D["x3"], c)).then_inc(filled[s], 16)
                    else:
                        p_ = parts_of(c)
                        sp.dma_start(x3[0:p_, s, :, :].rearrange("p g f -> p (g f)"), node_rows(D["x3n"], c))\
                            .then_inc(filled[s], 16)

                def load_rows(c, j, s):
                    if not first(j):
                        sp.wait_ge(stored[s], 64 * j)
                        sp.sem_inc(own, 1)
                    sp.dma_start(ix[:, s, :], D["index2"].rearrange("p (c k) -> p c k", c=2 * CH)[:, c, :])\
                        .then_inc(rows_in[s], 16)

                def store(c, j, s):
                    p_ = parts_of(c)
                    sp.wait_ge(normed, c + 1)
                    sp.sem_inc(own, 1)
                    sp.dma_start(node_rows(out, c), xo[0:p_, s, :, :].rearrange("p g f -> p (g f)"))\
                        .then_inc(stored[s], 16)
                if slots:
                    pipeline(Steps(sp, own), count, NS, (0, load), (2, load_rows))
                else:
                    pipeline(Steps(sp, own), count, NS, (0, load), (6, store))
                    for s in range(NS):
                        sp.wait_ge(stored[s], 16 * uses(s, count))

            if slots:
                @block.gpsimd
                def _(pool):
                    def scatter(c, j, s):
                        pool.wait_ge(normed, c + 1)
                        pool.wait_ge(rows_in[s], 16 * (j + 1))
                        pool.sem_inc(own, 1)
                        for g in range(G):
                            pool.indirect_dma_start(
                                out=out, out_offset=bass.IndirectOffsetOnAxis(ap=ix[:, s, g * NIX:g * NIX + 1], axis=0),
                                in_=xo[:, s, g, :], in_offset=None, bounds_check=N - 1, oob_is_err=False)\
                                .then_inc(stored[s], 16)
                    pipeline(Steps(pool, own), count, NS, (0, scatter))
                    for s in range(NS):
                        pool.wait_ge(stored[s], 64 * uses(s, count))

            else:
                @block.gpsimd
                def _(pool):
                    def offset(c, j, s):
                        n = parts_of(c)
                        pool.wait_ge(filled[s], loads * (j + 1))
                        pool.tensor_tensor(x3[0:n, s, :, :], x3[0:n, s, :, :], spread(env.bc["L3_gnn_b_out"][0:n, :]),
                                           ALU.add).then_inc(with_bias, 1)
                    pipeline(Steps(pool, own), count, NS, (0, offset))

            @block.scalar
            def _(act):
                def make(c, j, s):
                    n = wide(c)
                    act.wait_ge(filled[s], loads * (j + 1))
                    if not first(j):
                        act.wait_ge(projected, c + 1 - NS)
                    act.activation(h[:, s, 0:n], z[:, s, 0:n], ACT.Relu, scale=norm[0], bias=norm[1]).then_inc(made, 1)

                def root(c, j, s):
                    n = P if slots else parts_of(c)
                    act.wait_ge(measured, c + 1)
                    act.activation(sd[0:n, s, :], mv[0:n, s, :, 1], ACT.Sqrt, bias=env.eps[0:n, 2:3])\
                        .then_inc(rooted, 1)

                def apply(c, j, s):
                    n = P if slots else parts_of(c)
                    act.wait_ge(scaled, c + 1)
                    if not first(j):
                        act.wait_ge(stored[s], (64 if slots else 16) * j)
                    for g in range(G):
                        last = act.activation(xo[0:n, s, g, :], vv[0:n, s, g, :], ACT.Identity,
                                              scale=sd[0:n, s, g:g + 1], bias=off[0:n, s, g:g + 1])
                    last.then_inc(normed, 1)
                pipeline(Steps(act, own), count, NS, (2, root), (0, make), (3, apply))

            @block.tensor
            def _(pe):
                def project(c, j, s):
                    n = P if slots else parts_of(c)
                    pe.wait_ge(made, c + 1)
                    if not (first(j) and s < 2):
                        pe.wait_ge(added, c - 1)
                    to_rows4(pe, po[s % 2], h[:, s, :], env.w["L3_gnn_W_out"], n).then_inc(projected, 1)
                pipeline(Steps(pe, own), count, NS, (0, project))

            @block.vector
            def _(v):
                def parts(c):
                    return P if slots else parts_of(c)

                def add(c, j, s):
                    n = parts(c)
                    v.wait_ge(projected, c + 1)
                    if not slots:
                        v.wait_ge(with_bias, c + 1)
                    v.tensor_tensor(vv[0:n, s, :, :], po[s % 2][0:n, :].rearrange("p (g f) -> p g f", g=G),
                                    x3[0:n, s, :, :], ALU.add).then_inc(added, 1)

                def add_bias(c, j, s):
                    v.wait_ge(added, c + 1)
                    v.tensor_tensor(vv[:, s, :, :], vv[:, s, :, :], spread(env.bc["L3_gnn_b_out"]), ALU.add)\
                        .then_inc(with_bias, 1)

                def sample(c, j, s):
                    n = parts(c)
                    v.wait_ge(added, c + 1)
                    v.wait_ge(with_bias, c + 1)
                    for g in range(G):
                        last = v.bn_stats(stats[0:n, s % 2, g, :], vv[0:n, s, g, :])
                    last.then_inc(sampled, 1)

                def measure(c, j, s):
                    n = parts(c)
                    v.wait_ge(sampled, c + 1)
                    v.sem_inc(own, 1)
                    for g in range(G):
                        last = v.bn_aggr(mv[0:n, s, g, :], stats[0:n, s % 2, g, :])
                    last.then_inc(measured, 1)

                def invert(c, j, s):
                    n = parts(c)
                    v.wait_ge(rooted, c + 1)
                    v.reciprocal(sd[0:n, s, :], sd[0:n, s, :]).then_inc(inverted, 1)

                def offset(c, j, s):
                    n = parts(c)
                    v.wait_ge(inverted, c + 1)
                    v.scalar_tensor_tensor(out=off[0:n, s, :], in0=mv[0:n, s, :, 0], scalar=-1.0, in1=sd[0:n, s, :],
                                           op0=ALU.mult, op1=ALU.mult).then_inc(scaled, 1)
                if slots:
                    pipeline(Steps(v, own), count, NS, (2, invert), (1, add), (2, offset), (1, add_bias), (1, sample),
                             (1, measure))
                else:
                    pipeline(Steps(v, own), count, NS, (2, invert), (1, add), (2, offset), (1, sample), (1, measure))


def program(nc, A, out, D):
    env = Env()
    with ExitStack() as ctx:
        env.ctx = ctx
        constants(nc, env, A)
        with nc.sbuf_tensor("tabs", [P, 6, W], fp32) as tabs:
            def load_edges(sp, keys, extra, ec, loaded):
                for dst, src in ((keys[:, 0, :], A["dst"]), (keys[:, 1, :], A["src"]),
                                 (extra[:, 2, :], A["edge_weight"])):
                    sp.dma_start(dst[0:FULL, :], src[0:FULL * P].rearrange("(t p) -> t p", p=P))\
                        .then_inc(loaded, 16)
                    sp.dma_start(dst[FULL:FULL + 1, 0:REST],
                                 src[FULL * P:E].rearrange("(t p) -> t p", t=1)).then_inc(loaded, 16)
                return 6

            def load_permuted(sp, keys, extra, ec, loaded):
                sp.dma_start(ec[:, :, :], D["edges"].rearrange("(t p) f -> t p f", p=P)[:, :, F:ROW])\
                    .then_inc(loaded, 16)
                return 1
            rows = (D["row_key"], D["row_high"])
            env.key_loads = 6
            key_meta(nc, env, "d", load_edges, rows, D["meta"], D["cols"])
            rank_edges(nc, env, "d", rows, D["meta"], D["rank_d"], tabs[:, 0, :], tabs[:, 1, :], tabs[:, 2, :])
            scatter_edges(nc, env, A, D)
            env.key_loads = 1
            key_meta(nc, env, "s", load_permuted, rows, D["meta"], D["cols_s"], permuted=True)
            rank_edges(nc, env, "s", rows, D["meta"], D["rank_s"], tabs[:, 3, :], tabs[:, 4, :], tabs[:, 5, :])
            node_tables(nc, env, D, tabs)
        dense_front(nc, env, A, D)
        slot_indices(nc, env, D)
        edge_layer0(nc, env, A, D)
        edge_layer1(nc, env, D)
        keep_rows(nc, env, D)
        source_layer1(nc, env, D)
        edge_layer2(nc, env, D)
        slot_states(nc, env, D)

        def stat(name, *shape):
            return ctx.enter_context(nc.sbuf_tensor(name, [P, *shape], fp32))
        node_stats, slot_sums = stat("node_stats", 2, DC, 6), stat("slot_sums", 2, 2 * CH, 2)
        z_sums = stat("z_sums", 2, CH, 1)
        norm1, norm2 = stat("norm1", 2, 2), stat("norm2", 2, 1)
        source, prev = D["za"], None
        for i in range(LAYERS):
            if i:
                gather_states(nc, env, D, i, source, lambda c: columns(source, c, W, SLOT0), (ACT.Relu, *prev),
                              node_stats, slot_sums, z_sums)
            else:
                gather_states(nc, env, D, i, source, lambda c: columns(D["hd"], c),
                              (ACT.Identity, 1.0, env.col["L3_gnn_b_atom"]), node_stats, slot_sums,
                              z_sums)
            target = D["zb"] if source is D["za"] else D["za"]
            b2i = slice(2 * i, 2 * i + 2)
            norm_constants(nc, env, f"c1{i}", 2, env.col["L3_gnn_b1"][:, b2i], env.col["L3_gnn_g1"][:, b2i],
                           env.col["L3_gnn_be1"][:, b2i], node_stats, slot_sums, norm1, (z_sums, env.w1[:, i, :]))
            column_pass(nc, env, D, i, "b", False, source, target, prev, norm1, node_stats)
            column_pass(nc, env, D, i, "b", True, source, target, None, norm1, slot_sums, rows=i < LAYERS - 1)
            norm_constants(nc, env, f"c2{i}", 1, env.col["L3_gnn_b2"][:, i:i + 1], env.col["L3_gnn_gn"][:, i:i + 1],
                           env.col["L3_gnn_bet"][:, i:i + 1], node_stats, slot_sums, norm2)
            source, prev = target, (norm2[:, 0, :], norm2[:, 1, :])
        results(nc, env, D, out, False, source, prev)
        results(nc, env, D, out, True, source, prev)


_INS = ["x", "src", "dst", "edge_attr_128", "edge_weight", "L0_gnn_W1", "L0_gnn_b1", "L0_gnn_W2", "L0_gnn_b2",
        "L1_gnn_Wn", "L1_gnn_We1", "L1_gnn_be1", "L1_gnn_We2", "L1_gnn_be2", "L1_gnn_W2", "L1_gnn_b2", "L1_gnn_W3",
        "L1_gnn_b3", "L2_gnn_W", "L2_gnn_b", "L3_gnn_W_atom", "L3_gnn_b_atom", "L3_gnn_W_bond", "L3_gnn_b_bond",
        "L3_gnn_eps", "L3_gnn_W1", "L3_gnn_b1", "L3_gnn_g1", "L3_gnn_be1", "L3_gnn_W2", "L3_gnn_b2", "L3_gnn_gn",
        "L3_gnn_bet", "L3_gnn_W_out", "L3_gnn_b_out"]
_SCRATCH = {
    "row_key": ((EP,), fp32), "row_high": ((EP,), fp32), "meta": ((P, T * 4), fp32), "cols": ((P, T * 4), fp32),
    "rank_d": ((P, T), i32), "rank_s": ((P, T), i32), "cols_s": ((P, T * 4), fp32), "edges": ((EP, ROW), fp32),
    "bounds": ((HI * W, 4), i32), "free": ((HI * W,), fp32), "keys_i": ((P, 2 * T), i32),
    "edge_bounds": ((P, T * 2 * 4), i32), "keep_d": ((EP,), fp32), "weights": ((2 * EP,), fp32),
    "x3n": ((N, F), fp32), "za": ((F, ZW), fp32), "zb": ((F, ZW), fp32), "hd": ((F, 2 * EP), fp32),
    "ea": ((F, EP), fp32), "hr": ((2 * EP, F), fp32), "index2": ((P, 2 * T * NIX), i32),
    "x1": ((2 * EP, F), fp32), "x2": ((2 * EP, F), fp32), "x3": ((2 * EP, F), fp32),
    "message": ((EP, MROW), fp32), "keep_s": ((EP,), fp32),
    "index": ((P, T * NIX), i32), "factor": ((P, T * NFL), fp32),
}


def kernel(**inputs):
    import numpy as _np
    import concourse.bacc as _bacc
    from concourse import mybir as _mybir
    from concourse.bass_utils import run_bass_kernel_spmd as _run

    nc = _bacc.Bacc("TRN2", target_bir_lowering=False, num_devices=1)
    arrays, args = {}, {}
    for name in _INS:
        a = _np.ascontiguousarray(inputs[name])
        arrays[f"in_{name}"] = a
        args[name] = nc.dram_tensor(f"in_{name}", a.shape, _mybir.dt.from_np(a.dtype), kind="ExternalInput").ap()
    out = nc.dram_tensor("out", (N, F), fp32, kind="ExternalOutput").ap()
    scratch = {n: nc.dram_tensor(f"scratch_{n}", s, dt, kind=SCRATCH_KIND).ap() for n, (s, dt) in _SCRATCH.items()}
    program(nc, args, out, scratch)
    r = _run(nc, [arrays], core_ids=[0])
    return r.results[0]["out"]


SCRATCH_KIND = "Internal"
```
